# Optimizing a Trainium2 kernel written in Bass

```python
import numpy as np
import jax
import jax.numpy as jnp

def _softmax(x, axis=-1):
    return jax.nn.softmax(x, axis=axis)

def _gelu(x):
    return jax.nn.gelu(x, approximate=True)

def _silu(x):
    return jax.nn.silu(x)

def _sigmoid(x):
    return jax.nn.sigmoid(x)

def _layernorm(x, axis=-1, eps=1e-05):
    m = jnp.mean(x, axis=axis, keepdims=True)
    v = jnp.var(x, axis=axis, keepdims=True)
    return (x - m) / jnp.sqrt(v + eps)

def _scatter_add(tgt, idx, src, axis=0):
    return tgt.at[idx].add(src)

def _segment_sum(src, seg, n):
    return jax.ops.segment_sum(src, seg, n)
kernel_name = 'mk_decoder_postln_d4_seqx_r8_338630'

def setup_inputs(seed: int=0):
    np.random.seed(seed)
    _w = jnp.asarray

    def _rec_inputs():
        import jax
        import jax.numpy as jnp
        _rk = jax.random.key(seed)
        x = -1.394e-06 + 0.9999 * jax.random.normal(jax.random.fold_in(_rk, 1), (64, 128, 128), jnp.float32)
        _lenS = 128 - jax.random.randint(jax.random.fold_in(_rk, 7), (64,), 0, max(1, 128 // 4) + 1, jnp.int32)
        _lenS2 = 77 - jax.random.randint(jax.random.fold_in(_rk, 8), (64,), 0, max(1, 77 // 4) + 1, jnp.int32)
        _ctx_1024P = jax.random.normal(jax.random.fold_in(_rk, 11), (64, 16, 128), jnp.float32)
        _ctx_1024c = jax.random.dirichlet(jax.random.fold_in(_rk, 511), 0.3 * jnp.ones((16,), jnp.float32), (64, 77))
        _ctx_1024t = jnp.einsum('bsk,bkd->bsd', _ctx_1024c, _ctx_1024P)
        _ctx_1024t = _ctx_1024t * jax.lax.rsqrt(jnp.mean(jnp.square(_ctx_1024t)) + 1e-12) * 0.953939
        ctx_1024 = -0.000292821 + 1.00034 * (_ctx_1024t + 0.3 * jax.random.normal(jax.random.fold_in(_rk, 611), (64, 77, 128), jnp.float32))
        _validS = jnp.arange(128)[None, :] < _lenS[:, None]
        _validS2 = jnp.arange(77)[None, :] < _lenS2[:, None]
        _causal = jnp.tril(jnp.ones((128, 128), dtype=bool))
        mask_BxS2_ik0 = jnp.where(jnp.broadcast_to(_validS2[:, :], (64, 77)), 0, 1).astype(jnp.int32)
        mask_1x1xSxS2_ik0 = jnp.where(jnp.broadcast_to(_validS2[0:1, None, None, :], (1, 1, 128, 77)), 0, 1).astype(jnp.int32)
        mask_1xSxS2_ff0 = jnp.where(jnp.ones((1, 128, 77), dtype=bool), 0.0, -1000000000.0).astype(jnp.float32)
        return (x, ctx_1024, mask_BxS2_ik0, mask_1x1xSxS2_ik0, mask_1xSxS2_ff0)
    x, ctx_1024, mask_BxS2_ik0, mask_1x1xSxS2_ik0, mask_1xSxS2_ff0 = _rec_inputs()

    def _L0_attn_setup():
        import jax, jax.numpy as jnp
        import numpy as np
        LAMBDA_0 = 1.0
        EPS = 1e-06
        key = jax.random.key(seed)
        ks = jax.random.split(key, 5)
        B, T, D, H = (4, 256, 128, 128)
        x = jax.random.normal(ks[0], (B, T, D), dtype=jnp.float32)
        Wq = jax.random.normal(ks[1], (H, D), dtype=jnp.float32) * D ** (-0.5)
        Wk = jax.random.normal(ks[2], (H, D), dtype=jnp.float32) * D ** (-0.5)
        Wv = jax.random.normal(ks[3], (H, D), dtype=jnp.float32) * D ** (-0.5)
        Wo = jax.random.normal(ks[4], (D, H), dtype=jnp.float32) * H ** (-0.5)
        bq = jnp.zeros((H,), jnp.float32)
        bk = jnp.zeros((H,), jnp.float32)
        bv = jnp.zeros((H,), jnp.float32)
        bo = jnp.zeros((D,), jnp.float32)
        return {'x': x, 'Wq': Wq, 'bq': bq, 'Wk': Wk, 'bk': bk, 'Wv': Wv, 'bv': bv, 'Wo': Wo, 'bo': bo}
    _L0_attn_all = _L0_attn_setup()
    _L0_attn_in = {k: v for k, v in _L0_attn_all.items() if k in ('Wq', 'bq', 'Wk', 'bk', 'Wv', 'bv', 'Wo', 'bo')}
    del _L0_attn_all

    def _L0_xattn_setup():
        import jax, jax.numpy as jnp
        import numpy as np
        D_MODEL = 128
        N_HEAD = 16
        HEAD_DIM = D_MODEL // N_HEAD
        key = jax.random.key(seed)
        ks = jax.random.split(key, 9)
        B, T = (2, 256)
        s = 0.02
        return {'k': jax.random.normal(ks[0], (B, T, D_MODEL), jnp.float32), 'q': jax.random.normal(ks[1], (B, T, D_MODEL), jnp.float32), 'v': jax.random.normal(ks[2], (B, T, D_MODEL), jnp.float32), 'Wk': jax.random.normal(ks[3], (D_MODEL, D_MODEL), jnp.float32) * s, 'bk': jnp.zeros((D_MODEL,), jnp.float32), 'Wq': jax.random.normal(ks[4], (D_MODEL, D_MODEL), jnp.float32) * s, 'bq': jnp.zeros((D_MODEL,), jnp.float32), 'Wc': jax.random.normal(ks[5], (D_MODEL, D_MODEL), jnp.float32) * s, 'bc': jnp.zeros((D_MODEL,), jnp.float32)}
    _L0_xattn_all = _L0_xattn_setup()
    _L0_xattn_in = {k: v for k, v in _L0_xattn_all.items() if k in ('Wk', 'bk', 'Wq', 'bq', 'Wc', 'bc')}
    del _L0_xattn_all

    def _L0_ffn_setup():
        import jax, jax.numpy as jnp
        import numpy as np
        NUM_EXPERTS = 8
        EXPERT_CAPACITY = 2.0
        key = jax.random.key(seed)
        k1, k2, k3, k4 = jax.random.split(key, 4)
        B, T, C, H, E = (4, 512, 128, 512, NUM_EXPERTS)
        x = jax.random.normal(k1, (B, T, C), jnp.float32)
        gate_w = jax.random.normal(k2, (C, E), jnp.float32) * 0.02
        w1 = jax.random.normal(k3, (E, C, H), jnp.float32) * 0.02
        w2 = jax.random.normal(k4, (E, H, C), jnp.float32) * 0.02
        return {'x': x, 'gate_w': gate_w, 'w1': w1, 'w2': w2}
    _L0_ffn_all = _L0_ffn_setup()
    _L0_ffn_in = {k: v for k, v in _L0_ffn_all.items() if k in ('gate_w', 'w1', 'w2')}
    del _L0_ffn_all

    def _L1_attn_setup():
        import jax, jax.numpy as jnp
        import numpy as np
        D_MODEL, N_HEADS, N_KV, HEAD_DIM, D_LAT = (128, 8, 2, 128, 32)
        N_REP = N_HEADS // N_KV
        B, T = (2, 256)
        key = jax.random.key(seed)
        ks = jax.random.split(key, 8)
        s = lambda fan_in: 1.0 / np.sqrt(fan_in)
        return {'x': jax.random.normal(ks[0], (B, T, D_MODEL), jnp.float32), 'wq': jax.random.normal(ks[1], (D_MODEL, N_HEADS * HEAD_DIM), jnp.float32) * s(D_MODEL), 'wk_down': jax.random.normal(ks[2], (D_MODEL, N_KV * D_LAT), jnp.float32) * s(D_MODEL), 'wv_down': jax.random.normal(ks[3], (D_MODEL, N_KV * D_LAT), jnp.float32) * s(D_MODEL), 'wk_up': jax.random.normal(ks[4], (D_LAT, HEAD_DIM), jnp.float32) * s(D_LAT), 'wv_up': jax.random.normal(ks[5], (D_LAT, HEAD_DIM), jnp.float32) * s(D_LAT), 'wo': jax.random.normal(ks[6], (N_HEADS * HEAD_DIM, D_MODEL), jnp.float32) * s(N_HEADS * HEAD_DIM)}
    _L1_attn_all = _L1_attn_setup()
    _L1_attn_in = {k: v for k, v in _L1_attn_all.items() if k in ('wq', 'wk_down', 'wv_down', 'wk_up', 'wv_up', 'wo')}
    del _L1_attn_all

    def _L1_xattn_setup():
        import jax, jax.numpy as jnp
        import numpy as np
        B, LQ, LK, D = (4, 256, 256, 128)
        H = 16
        HD = D // H

        def _split_heads(x):
            b, l, _ = x.shape
            return x.reshape(b, l, H, HD).transpose(0, 2, 1, 3)
        key = jax.random.key(seed)
        ks = jax.random.split(key, 10)
        s = 0.02
        return {'hidden_states': jax.random.normal(ks[0], (B, LQ, D), jnp.float32), 'context': jax.random.normal(ks[1], (B, LK, D), jnp.float32), 'attention_mask': jax.random.randint(ks[2], (B, LK), 0, 2, jnp.int32), 'q_w': jax.random.normal(ks[3], (D, D), jnp.float32) * s, 'q_b': jnp.zeros((D,), jnp.float32), 'k_w': jax.random.normal(ks[4], (D, D), jnp.float32) * s, 'k_b': jnp.zeros((D,), jnp.float32), 'v_w': jax.random.normal(ks[5], (D, D), jnp.float32) * s, 'v_b': jnp.zeros((D,), jnp.float32)}
    _L1_xattn_all = _L1_xattn_setup()
    _L1_xattn_in = {k: v for k, v in _L1_xattn_all.items() if k in ('q_w', 'q_b', 'k_w', 'k_b', 'v_w', 'v_b')}
    del _L1_xattn_all

    def _L1_ffn_setup():
        import jax, jax.numpy as jnp
        import numpy as np
        BLOCK = 16
        _GRID = jnp.array([0.0, 0.5, 1.0, 1.5, 2.0, 3.0, 4.0, 6.0], dtype=jnp.float32)
        _MID = jnp.array([0.25, 0.75, 1.25, 1.75, 2.5, 3.5, 5.0], dtype=jnp.float32)

        def fp4_quant_dequant(x):
            shape = x.shape
            xb = x.reshape(shape[:-1] + (shape[-1] // BLOCK, BLOCK))
            scale = jnp.max(jnp.abs(xb), axis=-1, keepdims=True) / 6.0
            scale = jnp.maximum(scale, jnp.float32(1e-12))
            xn = xb / scale
            idx = jnp.searchsorted(_MID, jnp.abs(xn))
            q = _GRID[idx] * jnp.sign(xn) * scale
            return q.reshape(shape)

        def fp4_linear(x, w):
            xq = fp4_quant_dequant(x)
            wq = fp4_quant_dequant(w)
            return jnp.einsum('bsk,nk->bsn', xq, wq)
        key = jax.random.key(seed)
        k1, k2, k3, k4 = jax.random.split(key, 4)
        H, I = (128, 352)
        x = jax.random.normal(k1, (4, 512, H), dtype=jnp.float32)
        w_gate = jax.random.normal(k2, (I, H), dtype=jnp.float32) * 0.02
        w_up = jax.random.normal(k3, (I, H), dtype=jnp.float32) * 0.02
        w_down = jax.random.normal(k4, (H, I), dtype=jnp.float32) * 0.02
        return {'x': x, 'w_gate': w_gate, 'w_up': w_up, 'w_down': w_down}
    _L1_ffn_all = _L1_ffn_setup()
    _L1_ffn_in = {k: v for k, v in _L1_ffn_all.items() if k in ('w_gate', 'w_up', 'w_down')}
    del _L1_ffn_all

    def _L2_attn_setup():
        import jax, jax.numpy as jnp
        import numpy as np
        NUM_HEADS = 16
        DIM = 128
        key = jax.random.key(seed)
        kx, kwq, kbq, kwk, kbk = jax.random.split(key, 5)
        B, N, C = (2, 256, DIM)
        s = 1.0 / np.sqrt(C)
        return {'x': jax.random.normal(kx, (B, N, C), dtype=jnp.float32), 'Wq': jax.random.normal(kwq, (C, C), dtype=jnp.float32) * s, 'bq': jax.random.normal(kbq, (C,), dtype=jnp.float32) * 0.01, 'Wk': jax.random.normal(kwk, (C, C), dtype=jnp.float32) * s, 'bk': jax.random.normal(kbk, (C,), dtype=jnp.float32) * 0.01}
    _L2_attn_all = _L2_attn_setup()
    _L2_attn_in = {k: v for k, v in _L2_attn_all.items() if k in ('Wq', 'bq', 'Wk', 'bk')}
    del _L2_attn_all

    def _L2_xattn_setup():
        import jax, jax.numpy as jnp
        import numpy as np
        D_MODEL = 128
        NUM_HEADS = 16
        HEAD_DIM = D_MODEL // NUM_HEADS
        B, S = (2, 256)
        key = jax.random.key(seed)
        ks = jax.random.split(key, 12)
        sc = 1.0 / np.sqrt(D_MODEL)
        inp = {'query': jax.random.normal(ks[0], (B, S, D_MODEL), jnp.float32), 'key': jax.random.normal(ks[1], (B, S, D_MODEL), jnp.float32), 'value': jax.random.normal(ks[2], (B, S, D_MODEL), jnp.float32), 'mask': jnp.tril(jnp.ones((S, S), jnp.int32))[None, None, :, :], 'Wq': jax.random.normal(ks[3], (D_MODEL, D_MODEL), jnp.float32) * sc, 'bq': jax.random.normal(ks[4], (D_MODEL,), jnp.float32) * 0.02, 'Wk': jax.random.normal(ks[5], (D_MODEL, D_MODEL), jnp.float32) * sc, 'bk': jax.random.normal(ks[6], (D_MODEL,), jnp.float32) * 0.02, 'Wv': jax.random.normal(ks[7], (D_MODEL, D_MODEL), jnp.float32) * sc, 'bv': jax.random.normal(ks[8], (D_MODEL,), jnp.float32) * 0.02, 'Wo': jax.random.normal(ks[9], (D_MODEL, D_MODEL), jnp.float32) * sc, 'bo': jax.random.normal(ks[10], (D_MODEL,), jnp.float32) * 0.02}
        return inp
    _L2_xattn_all = _L2_xattn_setup()
    _L2_xattn_in = {k: v for k, v in _L2_xattn_all.items() if k in ('Wq', 'bq', 'Wk', 'bk', 'Wv', 'bv', 'Wo', 'bo')}
    del _L2_xattn_all

    def _L2_ffn_setup():
        import jax, jax.numpy as jnp
        import numpy as np
        from jax import lax
        TOP_K = 1
        key = jax.random.key(seed)
        ks = jax.random.split(key, 9)
        B, N, C = (4, 256, 128)
        E, L, R = (6, 100, 16)
        return {'feats': jax.random.normal(ks[0], (B, N, C), jnp.float32), 'A': jax.random.normal(ks[1], (E, L, R), jnp.float32) * 0.05, 'B': jax.random.normal(ks[2], (E, R, C), jnp.float32) * 0.05, 'w_gate': jax.random.normal(ks[3], (C, E), jnp.float32) * 0.02, 'wt_w': jax.random.normal(ks[4], (C, C), jnp.float32) * (1.0 / np.sqrt(C)), 'wt_b': jax.random.normal(ks[5], (C,), jnp.float32) * 0.01, 'wd_w': jax.random.normal(ks[6], (C, C), jnp.float32) * (1.0 / np.sqrt(C)), 'wd_b': jax.random.normal(ks[7], (C,), jnp.float32) * 0.01, 'scale': jnp.full((1,), 0.001, jnp.float32)}
    _L2_ffn_all = _L2_ffn_setup()
    _L2_ffn_in = {k: v for k, v in _L2_ffn_all.items() if k in ('A', 'B', 'w_gate', 'wt_w', 'wt_b', 'wd_w', 'wd_b', 'scale')}
    del _L2_ffn_all

    def _L3_attn_setup():
        import jax, jax.numpy as jnp
        import numpy as np
        DIM = 128
        NUM_HEADS = 16
        HEAD_DIM = DIM // NUM_HEADS

        def _rope_tables(seq_len, dim, dtype):
            inv_freq = 1.0 / 10000.0 ** (jnp.arange(0, dim, 2, dtype=jnp.float32) / dim)
            t = jnp.arange(seq_len, dtype=jnp.float32)
            freqs = jnp.outer(t, inv_freq)
            return (jnp.cos(freqs).astype(dtype), jnp.sin(freqs).astype(dtype))

        def _apply_rope(x, cos_emb, sin_emb):
            x1 = x[..., 0::2]
            x2 = x[..., 1::2]
            return jnp.concatenate((x1 * cos_emb - x2 * sin_emb, x1 * sin_emb + x2 * cos_emb), axis=-1)
        key = jax.random.key(seed)
        k_x, k_qkv, k_out, k_b = jax.random.split(key, 4)
        B, S, D = (2, 256, DIM)
        x = jax.random.normal(k_x, (B, S, D), dtype=jnp.float32)
        w_qkv = jax.random.normal(k_qkv, (3 * D, D), dtype=jnp.float32) * (1.0 / np.sqrt(D))
        w_out = jax.random.normal(k_out, (D, D), dtype=jnp.float32) * (1.0 / np.sqrt(D))
        b_out = jax.random.normal(k_b, (D,), dtype=jnp.float32) * 0.01
        return {'x': x, 'w_qkv': w_qkv, 'w_out': w_out, 'b_out': b_out}
    _L3_attn_all = _L3_attn_setup()
    _L3_attn_in = {k: v for k, v in _L3_attn_all.items() if k in ('w_qkv', 'w_out', 'b_out')}
    del _L3_attn_all

    def _L3_xattn_setup():
        import jax, jax.numpy as jnp
        import numpy as np
        B, S, D_IN, D_MODEL = (4, 256, 128, 128)
        key = jax.random.key(seed)
        ks = jax.random.split(key, 8)
        glorot = np.sqrt(6.0 / (D_IN + D_MODEL))
        inp = {'q': jax.random.normal(ks[0], (B, S, D_IN), dtype=jnp.float32), 'k': jax.random.normal(ks[1], (B, S, D_IN), dtype=jnp.float32), 'v': jax.random.normal(ks[2], (B, S, D_IN), dtype=jnp.float32), 'mask': jnp.zeros((1, S, S), dtype=jnp.float32), 'kernel_q': jax.random.uniform(ks[3], (1, 1, D_IN, D_MODEL), jnp.float32, -glorot, glorot), 'kernel_k': jax.random.uniform(ks[4], (1, 1, D_IN, D_MODEL), jnp.float32, -glorot, glorot), 'kernel_v': jax.random.uniform(ks[5], (1, 1, D_IN, D_MODEL), jnp.float32, -glorot, glorot), 'bias_q': 0.05 * jax.random.normal(ks[6], (D_MODEL,), dtype=jnp.float32), 'bias_k': 0.05 * jax.random.normal(ks[7], (D_MODEL,), dtype=jnp.float32), 'bias_v': 0.05 * jax.random.normal(jax.random.fold_in(key, 7), (D_MODEL,), dtype=jnp.float32)}
        return inp
    _L3_xattn_all = _L3_xattn_setup()
    _L3_xattn_in = {k: v for k, v in _L3_xattn_all.items() if k in ('kernel_q', 'kernel_k', 'kernel_v', 'bias_q', 'bias_k', 'bias_v')}
    del _L3_xattn_all

    def _L3_ffn_setup():
        import jax, jax.numpy as jnp
        import numpy as np
        DIM, HEADS, EXPERTS, DFF = (128, 16, 8, 512)
        EPS = 1e-05

        def layernorm(x, g, b):
            mu = jnp.mean(x, -1, keepdims=True)
            var = jnp.mean(jnp.square(x - mu), -1, keepdims=True)
            return (x - mu) * jax.lax.rsqrt(var + EPS) * g + b
        key = jax.random.key(seed)
        ks = jax.random.split(key, 12)
        s = lambda d: 1.0 / np.sqrt(d)
        return {'x': jax.random.normal(ks[0], (2, 256, DIM), jnp.float32), 'conv_w': jax.random.normal(ks[1], (DIM, DIM, 3), jnp.float32) * s(DIM * 3), 'conv_b': jnp.zeros((DIM,), jnp.float32), 'wqkv': jax.random.normal(ks[2], (3 * DIM, DIM), jnp.float32) * s(DIM), 'bqkv': jnp.zeros((3 * DIM,), jnp.float32), 'wo': jax.random.normal(ks[3], (DIM, DIM), jnp.float32) * s(DIM), 'bo': jnp.zeros((DIM,), jnp.float32), 'ln1_g': jnp.ones((DIM,), jnp.float32), 'ln1_b': jnp.zeros((DIM,), jnp.float32), 'gate_w': jax.random.normal(ks[4], (DIM, EXPERTS), jnp.float32) * s(DIM), 'gate_b': jnp.zeros((EXPERTS,), jnp.float32), 'w1': jax.random.normal(ks[5], (EXPERTS, DIM, DFF), jnp.float32) * s(DIM), 'b1': jnp.zeros((EXPERTS, DFF), jnp.float32), 'w2': jax.random.normal(ks[6], (EXPERTS, DFF, DIM), jnp.float32) * s(DFF), 'b2': jnp.zeros((EXPERTS, DIM), jnp.float32), 'ln2_g': jnp.ones((DIM,), jnp.float32), 'ln2_b': jnp.zeros((DIM,), jnp.float32)}
    _L3_ffn_all = _L3_ffn_setup()
    _L3_ffn_in = {k: v for k, v in _L3_ffn_all.items() if k in ('conv_w', 'conv_b', 'wqkv', 'bqkv', 'wo', 'bo', 'ln1_g', 'ln1_b', 'gate_w', 'gate_b', 'w1', 'b1', 'w2', 'b2', 'ln2_g', 'ln2_b')}
    del _L3_ffn_all
    return {'x': x, 'ctx_1024': ctx_1024, 'mask_BxS2_ik0': mask_BxS2_ik0, 'mask_1x1xSxS2_ik0': mask_1x1xSxS2_ik0, 'mask_1xSxS2_ff0': mask_1xSxS2_ff0, 'L0_attn_Wq': _L0_attn_in['Wq'], 'L0_attn_bq': _L0_attn_in['bq'], 'L0_attn_Wk': _L0_attn_in['Wk'], 'L0_attn_bk': _L0_attn_in['bk'], 'L0_attn_Wv': _L0_attn_in['Wv'], 'L0_attn_bv': _L0_attn_in['bv'], 'L0_attn_Wo': _L0_attn_in['Wo'], 'L0_attn_bo': _L0_attn_in['bo'], 'L0_xattn_Wk': _L0_xattn_in['Wk'], 'L0_xattn_bk': _L0_xattn_in['bk'], 'L0_xattn_Wq': _L0_xattn_in['Wq'], 'L0_xattn_bq': _L0_xattn_in['bq'], 'L0_xattn_Wc': _L0_xattn_in['Wc'], 'L0_xattn_bc': _L0_xattn_in['bc'], 'L0_ffn_gate_w': _L0_ffn_in['gate_w'], 'L0_ffn_w1': _L0_ffn_in['w1'], 'L0_ffn_w2': _L0_ffn_in['w2'], 'L1_attn_wq': _L1_attn_in['wq'], 'L1_attn_wk_down': _L1_attn_in['wk_down'], 'L1_attn_wv_down': _L1_attn_in['wv_down'], 'L1_attn_wk_up': _L1_attn_in['wk_up'], 'L1_attn_wv_up': _L1_attn_in['wv_up'], 'L1_attn_wo': _L1_attn_in['wo'], 'L1_xattn_q_w': _L1_xattn_in['q_w'], 'L1_xattn_q_b': _L1_xattn_in['q_b'], 'L1_xattn_k_w': _L1_xattn_in['k_w'], 'L1_xattn_k_b': _L1_xattn_in['k_b'], 'L1_xattn_v_w': _L1_xattn_in['v_w'], 'L1_xattn_v_b': _L1_xattn_in['v_b'], 'L1_ffn_w_gate': _L1_ffn_in['w_gate'], 'L1_ffn_w_up': _L1_ffn_in['w_up'], 'L1_ffn_w_down': _L1_ffn_in['w_down'], 'L2_attn_Wq': _L2_attn_in['Wq'], 'L2_attn_bq': _L2_attn_in['bq'], 'L2_attn_Wk': _L2_attn_in['Wk'], 'L2_attn_bk': _L2_attn_in['bk'], 'L2_xattn_Wq': _L2_xattn_in['Wq'], 'L2_xattn_bq': _L2_xattn_in['bq'], 'L2_xattn_Wk': _L2_xattn_in['Wk'], 'L2_xattn_bk': _L2_xattn_in['bk'], 'L2_xattn_Wv': _L2_xattn_in['Wv'], 'L2_xattn_bv': _L2_xattn_in['bv'], 'L2_xattn_Wo': _L2_xattn_in['Wo'], 'L2_xattn_bo': _L2_xattn_in['bo'], 'L2_ffn_A': _L2_ffn_in['A'], 'L2_ffn_B': _L2_ffn_in['B'], 'L2_ffn_w_gate': _L2_ffn_in['w_gate'], 'L2_ffn_wt_w': _L2_ffn_in['wt_w'], 'L2_ffn_wt_b': _L2_ffn_in['wt_b'], 'L2_ffn_wd_w': _L2_ffn_in['wd_w'], 'L2_ffn_wd_b': _L2_ffn_in['wd_b'], 'L2_ffn_scale': _L2_ffn_in['scale'], 'L3_attn_w_qkv': _L3_attn_in['w_qkv'], 'L3_attn_w_out': _L3_attn_in['w_out'], 'L3_attn_b_out': _L3_attn_in['b_out'], 'L3_xattn_kernel_q': _L3_xattn_in['kernel_q'], 'L3_xattn_kernel_k': _L3_xattn_in['kernel_k'], 'L3_xattn_kernel_v': _L3_xattn_in['kernel_v'], 'L3_xattn_bias_q': _L3_xattn_in['bias_q'], 'L3_xattn_bias_k': _L3_xattn_in['bias_k'], 'L3_xattn_bias_v': _L3_xattn_in['bias_v'], 'L3_ffn_conv_w': _L3_ffn_in['conv_w'], 'L3_ffn_conv_b': _L3_ffn_in['conv_b'], 'L3_ffn_wqkv': _L3_ffn_in['wqkv'], 'L3_ffn_bqkv': _L3_ffn_in['bqkv'], 'L3_ffn_wo': _L3_ffn_in['wo'], 'L3_ffn_bo': _L3_ffn_in['bo'], 'L3_ffn_ln1_g': _L3_ffn_in['ln1_g'], 'L3_ffn_ln1_b': _L3_ffn_in['ln1_b'], 'L3_ffn_gate_w': _L3_ffn_in['gate_w'], 'L3_ffn_gate_b': _L3_ffn_in['gate_b'], 'L3_ffn_w1': _L3_ffn_in['w1'], 'L3_ffn_b1': _L3_ffn_in['b1'], 'L3_ffn_w2': _L3_ffn_in['w2'], 'L3_ffn_b2': _L3_ffn_in['b2'], 'L3_ffn_ln2_g': _L3_ffn_in['ln2_g'], 'L3_ffn_ln2_b': _L3_ffn_in['ln2_b']}

def reference(x, ctx_1024, mask_BxS2_ik0, mask_1x1xSxS2_ik0, mask_1xSxS2_ff0, L0_attn_Wq, L0_attn_bq, L0_attn_Wk, L0_attn_bk, L0_attn_Wv, L0_attn_bv, L0_attn_Wo, L0_attn_bo, L0_xattn_Wk, L0_xattn_bk, L0_xattn_Wq, L0_xattn_bq, L0_xattn_Wc, L0_xattn_bc, L0_ffn_gate_w, L0_ffn_w1, L0_ffn_w2, L1_attn_wq, L1_attn_wk_down, L1_attn_wv_down, L1_attn_wk_up, L1_attn_wv_up, L1_attn_wo, L1_xattn_q_w, L1_xattn_q_b, L1_xattn_k_w, L1_xattn_k_b, L1_xattn_v_w, L1_xattn_v_b, L1_ffn_w_gate, L1_ffn_w_up, L1_ffn_w_down, L2_attn_Wq, L2_attn_bq, L2_attn_Wk, L2_attn_bk, L2_xattn_Wq, L2_xattn_bq, L2_xattn_Wk, L2_xattn_bk, L2_xattn_Wv, L2_xattn_bv, L2_xattn_Wo, L2_xattn_bo, L2_ffn_A, L2_ffn_B, L2_ffn_w_gate, L2_ffn_wt_w, L2_ffn_wt_b, L2_ffn_wd_w, L2_ffn_wd_b, L2_ffn_scale, L3_attn_w_qkv, L3_attn_w_out, L3_attn_b_out, L3_xattn_kernel_q, L3_xattn_kernel_k, L3_xattn_kernel_v, L3_xattn_bias_q, L3_xattn_bias_k, L3_xattn_bias_v, L3_ffn_conv_w, L3_ffn_conv_b, L3_ffn_wqkv, L3_ffn_bqkv, L3_ffn_wo, L3_ffn_bo, L3_ffn_ln1_g, L3_ffn_ln1_b, L3_ffn_gate_w, L3_ffn_gate_b, L3_ffn_w1, L3_ffn_b1, L3_ffn_w2, L3_ffn_b2, L3_ffn_ln2_g, L3_ffn_ln2_b):
    import jax
    import jax.numpy as jnp

    def _L0_attn_ref(x, Wq, bq, Wk, bk, Wv, bv, Wo, bo):
        import jax, jax.numpy as jnp
        import numpy as np
        LAMBDA_0 = 1.0
        EPS = 1e-06
        B, T, D = x.shape
        H = Wq.shape[0]
        Q = jnp.einsum('btd,hd->bth', x, Wq) + bq
        K = jnp.einsum('btd,hd->bth', x, Wk) + bk
        V = jnp.einsum('btd,hd->bth', x, Wv) + bv
        A0 = jnp.broadcast_to(jnp.eye(H, dtype=jnp.float32) / LAMBDA_0, (B, H, H))
        M0 = jnp.zeros((B, H, H), jnp.float32)

        def step(carry, qkv):
            A, M = carry
            q, k, v = qkv
            s_t = jnp.sum(k * q, axis=-1, keepdims=True)
            u = k / (jnp.linalg.norm(k, axis=-1, keepdims=True) + EPS)
            Au = jnp.einsum('bij,bj->bi', A, u)
            denom = 1.0 + jnp.sum(u * Au, axis=-1, keepdims=True)
            A = A - jnp.einsum('bi,bj->bij', Au, Au) / denom[..., None]
            z = Au / denom
            alpha = s_t * z
            M = M + jnp.einsum('bi,bj->bij', v, alpha)
            o = jnp.einsum('bij,bj->bi', M, q)
            return ((A, M), o)
        qkv = (jnp.swapaxes(Q, 0, 1), jnp.swapaxes(K, 0, 1), jnp.swapaxes(V, 0, 1))
        _, O = jax.lax.scan(step, (A0, M0), qkv)
        O = jnp.swapaxes(O, 0, 1)
        return jnp.einsum('bth,dh->btd', O, Wo) + bo

    def _L0_xattn_ref(k, q, v, Wk, bk, Wq, bq, Wc, bc):
        import jax, jax.numpy as jnp
        import numpy as np
        D_MODEL = 128
        N_HEAD = 16
        HEAD_DIM = D_MODEL // N_HEAD
        B, T_v, C = v.shape
        T_q = q.shape[1]
        H, hd = (N_HEAD, C // N_HEAD)
        kp = k @ Wk.T + bk
        qp = q @ Wq.T + bq
        kh = kp.reshape(B, T_v, H, hd).transpose(0, 2, 1, 3)
        qh = qp.reshape(B, T_q, H, hd).transpose(0, 2, 1, 3)
        vh = v.reshape(B, T_v, H, hd).transpose(0, 2, 1, 3)
        scale = 1.0 / jnp.sqrt(jnp.asarray(hd, kh.dtype))
        att = jnp.einsum('bhqd,bhkd->bhqk', qh, kh) * scale
        att = jax.nn.softmax(att, axis=-1)
        y = jnp.einsum('bhqk,bhkd->bhqd', att, vh)
        y = y.transpose(0, 2, 1, 3).reshape(B, T_q, C)
        return y @ Wc.T + bc

    def _L0_ffn_ref(x, gate_w, w1, w2):
        import jax, jax.numpy as jnp
        import numpy as np
        NUM_EXPERTS = 8
        EXPERT_CAPACITY = 2.0
        B, T, C = x.shape
        E = gate_w.shape[1]
        cap = int(EXPERT_CAPACITY * T / E)
        scores = jnp.einsum('BTC,CE->BTE', x, gate_w)
        probs = jax.nn.softmax(scores, axis=-1)
        probs_et = jnp.transpose(probs, (0, 2, 1))
        top_p, top_idx = jax.lax.top_k(probs_et, cap)
        xin = jnp.take_along_axis(x[:, None, :, :], top_idx[..., None], axis=2)
        h = jax.nn.gelu(jnp.einsum('BElC,ECH->BElH', xin, w1), approximate=False)
        y = jnp.einsum('BElH,EHC->BElC', h, w2)
        y = y * top_p[..., None]
        b_idx = jnp.arange(B)[:, None, None]
        out = jnp.zeros((B, T, C), x.dtype).at[b_idx, top_idx].add(y)
        return out

    def _L1_attn_ref(x, wq, wk_down, wv_down, wk_up, wv_up, wo):
        import jax, jax.numpy as jnp
        import numpy as np
        D_MODEL, N_HEADS, N_KV, HEAD_DIM, D_LAT = (128, 8, 2, 128, 32)
        N_REP = N_HEADS // N_KV
        B, T = (2, 256)
        Bq, Tq, _ = x.shape
        scale = HEAD_DIM ** (-0.5)
        q = (x @ wq).reshape(Bq, Tq, N_KV, N_REP, HEAD_DIM)
        k_lat = (x @ wk_down).reshape(Bq, Tq, N_KV, D_LAT)
        v_lat = (x @ wv_down).reshape(Bq, Tq, N_KV, D_LAT)
        k = jnp.einsum('bkhl,ld->bkhd', k_lat, wk_up)
        v = jnp.einsum('bkhl,ld->bkhd', v_lat, wv_up)
        scores = jnp.einsum('bqhrd,bkhd->bhrqk', q, k) * scale
        causal = jnp.tril(jnp.ones((Tq, Tq), dtype=bool))
        scores = jnp.where(causal, scores, jnp.finfo(scores.dtype).min)
        probs = jax.nn.softmax(scores, axis=-1)
        y = jnp.einsum('bhrqk,bkhd->bqhrd', probs, v)
        y = y.reshape(Bq, Tq, N_HEADS * HEAD_DIM)
        return y @ wo

    def _L1_xattn_ref(hidden_states, context, attention_mask, q_w, q_b, k_w, k_b, v_w, v_b):
        import jax, jax.numpy as jnp
        import numpy as np
        B, LQ, LK, D = (4, 256, 256, 128)
        H = 16
        HD = D // H

        def _split_heads(x):
            b, l, _ = x.shape
            return x.reshape(b, l, H, HD).transpose(0, 2, 1, 3)
        q = _split_heads(hidden_states @ q_w.T + q_b)
        k = _split_heads(context @ k_w.T + k_b)
        v = _split_heads(context @ v_w.T + v_b)
        scores = jnp.einsum('bhqd,bhkd->bhqk', q, k) / jnp.sqrt(jnp.float32(HD))
        mask = (attention_mask > 0)[:, None, None, :]
        scores = jnp.where(mask, -jnp.inf, scores)
        probs = jax.nn.softmax(scores, axis=-1)
        ctx = jnp.einsum('bhqk,bhkd->bhqd', probs, v)
        ctx = ctx.transpose(0, 2, 1, 3).reshape(ctx.shape[0], ctx.shape[2], H * HD)
        return ctx

    def _L1_ffn_ref(x, w_gate, w_up, w_down):
        import jax, jax.numpy as jnp
        import numpy as np
        BLOCK = 16
        _GRID = jnp.array([0.0, 0.5, 1.0, 1.5, 2.0, 3.0, 4.0, 6.0], dtype=jnp.float32)
        _MID = jnp.array([0.25, 0.75, 1.25, 1.75, 2.5, 3.5, 5.0], dtype=jnp.float32)

        def fp4_quant_dequant(x):
            shape = x.shape
            xb = x.reshape(shape[:-1] + (shape[-1] // BLOCK, BLOCK))
            scale = jnp.max(jnp.abs(xb), axis=-1, keepdims=True) / 6.0
            scale = jnp.maximum(scale, jnp.float32(1e-12))
            xn = xb / scale
            idx = jnp.searchsorted(_MID, jnp.abs(xn))
            q = _GRID[idx] * jnp.sign(xn) * scale
            return q.reshape(shape)

        def fp4_linear(x, w):
            xq = fp4_quant_dequant(x)
            wq = fp4_quant_dequant(w)
            return jnp.einsum('bsk,nk->bsn', xq, wq)
        gate = fp4_linear(x, w_gate)
        y = fp4_linear(x, w_up)
        h = jax.nn.silu(gate) * y
        return fp4_linear(h, w_down)

    def _L2_attn_ref(x, Wq, bq, Wk, bk):
        import jax, jax.numpy as jnp
        import numpy as np
        NUM_HEADS = 16
        DIM = 128
        B, N, C = x.shape
        H = NUM_HEADS
        Dh = C // H
        q = (x @ Wq + bq).reshape(B, N, H, Dh).transpose(0, 2, 1, 3)
        k = (x @ Wk + bk).reshape(B, N, H, Dh).transpose(0, 2, 1, 3)
        v = k
        scale = C ** (-0.5)
        attn = jnp.einsum('bhnd,bhmd->bhnm', q, k) * scale
        attn = jax.nn.softmax(attn, axis=-1)
        out = jnp.einsum('bhnm,bhmd->bhnd', attn, v)
        return out.transpose(0, 2, 1, 3).reshape(B, N, C)

    def _L2_xattn_ref(query, key, value, mask, Wq, bq, Wk, bk, Wv, bv, Wo, bo):
        import jax, jax.numpy as jnp
        import numpy as np
        D_MODEL = 128
        NUM_HEADS = 16
        HEAD_DIM = D_MODEL // NUM_HEADS
        B, S = (2, 256)
        b = query.shape[0]
        Q = query @ Wq + bq
        K = key @ Wk + bk
        V = value @ Wv + bv

        def split_heads(x):
            return x.reshape(b, -1, NUM_HEADS, HEAD_DIM).transpose(0, 2, 1, 3)
        Qh, Kh, Vh = (split_heads(Q), split_heads(K), split_heads(V))
        scores = jnp.einsum('bhqd,bhkd->bhqk', Qh, Kh) / jnp.sqrt(jnp.asarray(HEAD_DIM, jnp.float32))
        scores = jnp.where(mask == 0, jnp.asarray(-1e+20, scores.dtype), scores)
        weights = jax.nn.softmax(scores, axis=-1)
        attn = jnp.einsum('bhqk,bhkd->bhqd', weights, Vh)
        attn = attn.transpose(0, 2, 1, 3).reshape(b, -1, D_MODEL)
        return attn @ Wo + bo

    def _L2_ffn_ref(feats, A, B, w_gate, wt_w, wt_b, wd_w, wd_b, scale):
        import jax, jax.numpy as jnp
        import numpy as np
        from jax import lax
        TOP_K = 1
        Bsz, N, C = feats.shape
        x = feats.reshape(-1, C)
        n = x.shape[0]
        logits = x @ w_gate
        top_vals, top_idx = lax.top_k(logits, TOP_K)
        top_g = jax.nn.softmax(top_vals, axis=-1)
        gates = jnp.zeros_like(logits).at[jnp.arange(n)[:, None], top_idx].set(top_g)
        tokens = jnp.einsum('elr,erc->elc', A, B)
        attn = jnp.einsum('nc,elc->nel', x, tokens) * C ** (-0.5)
        attn = jax.nn.softmax(attn, axis=-1)
        val = jnp.einsum('elc,dc->eld', tokens, wt_w) + wt_b
        delta_f = jnp.einsum('nel,eld->ned', attn[:, :, 1:], val[:, 1:, :])
        delta = (jnp.einsum('ned,cd->nec', delta_f + x[:, None, :], wd_w) + wd_b) * scale[0]
        combined = jnp.sum(jnp.exp(delta) * gates[:, :, None], axis=1)
        combined = jnp.where(combined == 0, jnp.finfo(jnp.float32).eps, combined)
        out = jnp.log(combined)
        return feats + out.reshape(Bsz, N, C)

    def _L3_attn_ref(x, w_qkv, w_out, b_out):
        import jax, jax.numpy as jnp
        import numpy as np
        DIM = 128
        NUM_HEADS = 16
        HEAD_DIM = DIM // NUM_HEADS

        def _rope_tables(seq_len, dim, dtype):
            inv_freq = 1.0 / 10000.0 ** (jnp.arange(0, dim, 2, dtype=jnp.float32) / dim)
            t = jnp.arange(seq_len, dtype=jnp.float32)
            freqs = jnp.outer(t, inv_freq)
            return (jnp.cos(freqs).astype(dtype), jnp.sin(freqs).astype(dtype))

        def _apply_rope(x, cos_emb, sin_emb):
            x1 = x[..., 0::2]
            x2 = x[..., 1::2]
            return jnp.concatenate((x1 * cos_emb - x2 * sin_emb, x1 * sin_emb + x2 * cos_emb), axis=-1)
        B, S, D = x.shape
        H, hd = (NUM_HEADS, HEAD_DIM)
        qkv = jnp.einsum('bsd,ed->bse', x, w_qkv)
        q, k, v = jnp.split(qkv, 3, axis=-1)
        q, k, v = (t.reshape(B, S, H, hd).transpose(0, 2, 1, 3) for t in (q, k, v))
        cos_emb, sin_emb = _rope_tables(S, hd, x.dtype)
        q = _apply_rope(q, cos_emb, sin_emb)
        k = _apply_rope(k, cos_emb, sin_emb)
        scores = jnp.einsum('bhqd,bhkd->bhqk', q, k) / jnp.sqrt(jnp.asarray(hd, x.dtype))
        attn = jax.nn.softmax(scores, axis=-1)
        out = jnp.einsum('bhqk,bhkd->bhqd', attn, v)
        out = out.transpose(0, 2, 1, 3).reshape(B, S, D)
        return jnp.einsum('bsd,ed->bse', out, w_out) + b_out

    def _L3_xattn_ref(q, k, v, mask, kernel_q, kernel_k, kernel_v, bias_q, bias_k, bias_v):
        import jax, jax.numpy as jnp
        import numpy as np
        B, S, D_IN, D_MODEL = (4, 256, 128, 128)
        Wq, Wk, Wv = (kernel_q[0, 0], kernel_k[0, 0], kernel_v[0, 0])
        qp = jax.nn.relu(jnp.einsum('bsd,de->bse', q, Wq) + bias_q)
        kp = jax.nn.relu(jnp.einsum('bsd,de->bse', k, Wk) + bias_k)
        vp = jax.nn.relu(jnp.einsum('bsd,de->bse', v, Wv) + bias_v)
        scores = jax.nn.relu(jnp.einsum('bqe,bke->bqk', qp, kp))
        dk = jnp.asarray(kp.shape[-1], dtype=scores.dtype)
        logits = scores / jnp.sqrt(dk) + mask
        out = jax.nn.relu(jnp.einsum('bqk,bke->bqe', logits, vp))
        return out

    def _L3_ffn_ref(x, conv_w, conv_b, wqkv, bqkv, wo, bo, ln1_g, ln1_b, gate_w, gate_b, w1, b1, w2, b2, ln2_g, ln2_b):
        import jax, jax.numpy as jnp
        import numpy as np
        DIM, HEADS, EXPERTS, DFF = (128, 16, 8, 512)
        EPS = 1e-05

        def layernorm(x, g, b):
            mu = jnp.mean(x, -1, keepdims=True)
            var = jnp.mean(jnp.square(x - mu), -1, keepdims=True)
            return (x - mu) * jax.lax.rsqrt(var + EPS) * g + b
        B, S, D = x.shape
        H, dh = (HEADS, D // HEADS)
        xt = jnp.transpose(x, (0, 2, 1))
        xt = jax.lax.conv_general_dilated(xt, conv_w, (1,), [(1, 1)], dimension_numbers=('NCH', 'OIH', 'NCH'))
        x = jnp.transpose(xt + conv_b[None, :, None], (0, 2, 1))
        qkv = x @ wqkv.T + bqkv
        q, k, v = jnp.split(qkv, 3, axis=-1)
        q = q.reshape(B, S, H, dh).transpose(0, 2, 1, 3)
        k = k.reshape(B, S, H, dh).transpose(0, 2, 1, 3)
        v = v.reshape(B, S, H, dh).transpose(0, 2, 1, 3)
        scores = jnp.einsum('bhqd,bhkd->bhqk', q, k) / jnp.sqrt(jnp.float32(dh))
        attn = jax.nn.softmax(scores, axis=-1)
        ctx = jnp.einsum('bhqk,bhkd->bhqd', attn, v)
        ctx = ctx.transpose(0, 2, 1, 3).reshape(B, S, D)
        attn_out = ctx @ wo.T + bo
        x = layernorm(x + attn_out, ln1_g, ln1_b)
        probs = jax.nn.softmax(x @ gate_w + gate_b, axis=-1)
        h = jax.nn.relu(jnp.einsum('bsd,edf->bsef', x, w1) + b1)
        y = jnp.einsum('bsef,efd->bsed', h, w2) + b2
        moe_out = jnp.einsum('bse,bsed->bsd', probs, y)
        x = layernorm(x + moe_out, ln2_g, ln2_b)
        return x
    x = _layernorm(x + _L0_attn_ref(x, L0_attn_Wq, L0_attn_bq, L0_attn_Wk, L0_attn_bk, L0_attn_Wv, L0_attn_bv, L0_attn_Wo, L0_attn_bo), axis=-1)
    x = _layernorm(x + _L0_xattn_ref(ctx_1024, x, ctx_1024, L0_xattn_Wk, L0_xattn_bk, L0_xattn_Wq, L0_xattn_bq, L0_xattn_Wc, L0_xattn_bc), axis=-1)
    x = _layernorm(x + _L0_ffn_ref(x, L0_ffn_gate_w, L0_ffn_w1, L0_ffn_w2), axis=-1)
    x = _layernorm(x + _L1_attn_ref(x, L1_attn_wq, L1_attn_wk_down, L1_attn_wv_down, L1_attn_wk_up, L1_attn_wv_up, L1_attn_wo), axis=-1)
    x = _layernorm(x + _L1_xattn_ref(x, ctx_1024, mask_BxS2_ik0, L1_xattn_q_w, L1_xattn_q_b, L1_xattn_k_w, L1_xattn_k_b, L1_xattn_v_w, L1_xattn_v_b), axis=-1)
    x = _layernorm(x + _L1_ffn_ref(x, L1_ffn_w_gate, L1_ffn_w_up, L1_ffn_w_down), axis=-1)
    x = _layernorm(x + _L2_attn_ref(x, L2_attn_Wq, L2_attn_bq, L2_attn_Wk, L2_attn_bk), axis=-1)
    x = _layernorm(x + _L2_xattn_ref(x, ctx_1024, ctx_1024, mask_1x1xSxS2_ik0, L2_xattn_Wq, L2_xattn_bq, L2_xattn_Wk, L2_xattn_bk, L2_xattn_Wv, L2_xattn_bv, L2_xattn_Wo, L2_xattn_bo), axis=-1)
    x = _layernorm(x + _L2_ffn_ref(x, L2_ffn_A, L2_ffn_B, L2_ffn_w_gate, L2_ffn_wt_w, L2_ffn_wt_b, L2_ffn_wd_w, L2_ffn_wd_b, L2_ffn_scale), axis=-1)
    x = _layernorm(x + _L3_attn_ref(x, L3_attn_w_qkv, L3_attn_w_out, L3_attn_b_out), axis=-1)
    x = _layernorm(x + _L3_xattn_ref(x, ctx_1024, ctx_1024, mask_1xSxS2_ff0, L3_xattn_kernel_q, L3_xattn_kernel_k, L3_xattn_kernel_v, L3_xattn_bias_q, L3_xattn_bias_k, L3_xattn_bias_v), axis=-1)
    x = _layernorm(x + _L3_ffn_ref(x, L3_ffn_conv_w, L3_ffn_conv_b, L3_ffn_wqkv, L3_ffn_bqkv, L3_ffn_wo, L3_ffn_bo, L3_ffn_ln1_g, L3_ffn_ln1_b, L3_ffn_gate_w, L3_ffn_gate_b, L3_ffn_w1, L3_ffn_b1, L3_ffn_w2, L3_ffn_b2, L3_ffn_ln2_g, L3_ffn_ln2_b), axis=-1)
    return x

_drawn_inputs = setup_inputs


def setup_inputs(seed=0):
    import zlib

    import numpy as np

    out = dict(_drawn_inputs(seed))
    spreads = {'L0_attn_bq': (0.0, 0.631),
     'L0_attn_bk': (0.0, 0.8),
     'L0_attn_bv': (0.0, 0.8),
     'L0_attn_bo': (0.0, 0.8),
     'L0_xattn_bk': (0.0, 0.8),
     'L0_xattn_bq': (0.0, 0.8),
     'L0_xattn_bc': (0.0, 0.677),
     'L1_xattn_q_b': (0.0, 0.8),
     'L1_xattn_k_b': (0.0, 0.8),
     'L1_xattn_v_b': (0.0, 0.757),
     'L3_ffn_conv_b': (0.0, 0.1),
     'L3_ffn_bqkv': (0.0, 0.1),
     'L3_ffn_bo': (0.0, 0.1),
     'L3_ffn_ln1_g': (1.0, 0.2),
     'L3_ffn_ln1_b': (0.0, 0.1),
     'L3_ffn_gate_b': (0.0, 0.44),
     'L3_ffn_b1': (0.0, 0.359),
     'L3_ffn_b2': (0.0, 0.1),
     'L3_ffn_ln2_g': (1.0, 0.2),
     'L3_ffn_ln2_b': (0.0, 0.1)}
    factors = {'L0_xattn_Wk': 8.0,
     'L0_xattn_Wq': 8.0,
     'L0_xattn_Wc': 3.092,
     'L0_ffn_gate_w': 8.0,
     'L0_ffn_w1': 8.0,
     'L0_ffn_w2': 8.0,
     'L1_attn_wq': 3.516,
     'L1_attn_wk_down': 3.4,
     'L1_attn_wk_up': 3.499,
     'L1_xattn_q_w': 8.0,
     'L1_xattn_k_w': 8.0,
     'L1_xattn_v_w': 4.079,
     'L1_ffn_w_gate': 8.0,
     'L1_ffn_w_up': 8.0,
     'L1_ffn_w_down': 8.0,
     'L2_attn_Wq': 8.0,
     'L2_attn_bq': 8.0,
     'L2_attn_bk': 8.0,
     'L2_xattn_Wq': 3.036,
     'L2_xattn_bq': 8.0,
     'L2_xattn_Wk': 3.014,
     'L2_xattn_bk': 8.0,
     'L2_xattn_bv': 8.0,
     'L2_xattn_bo': 8.0,
     'L2_ffn_A': 8.0,
     'L2_ffn_B': 8.0,
     'L2_ffn_w_gate': 8.0,
     'L2_ffn_wt_w': 8.0,
     'L2_ffn_wt_b': 8.0,
     'L2_ffn_wd_w': 8.0,
     'L2_ffn_wd_b': 8.0,
     'L3_attn_b_out': 8.0,
     'L3_xattn_bias_q': 8.0,
     'L3_xattn_bias_k': 8.0}
    for name, (base, spread) in spreads.items():
        noise = np.random.default_rng([zlib.crc32(name.encode()), seed]).standard_normal(out[name].shape)
        drawn = base * np.exp(spread * noise) if base else spread * noise
        out[name] = jnp.asarray(drawn.astype(out[name].dtype))
    for name, factor in factors.items():
        out[name] = (out[name] * factor).astype(out[name].dtype)
    return out
```

```python
from contextlib import ExitStack

import numpy as np

import concourse.bass as bass
from concourse import mybir

F32 = mybir.dt.float32
I32 = mybir.dt.int32
ALU = mybir.AluOpType
ACT = mybir.ActivationFunctionType
AX = mybir.AxisListType.X

P = 128
T = 128
D = 128
S2 = 77
HEADS = 16
HD = D // HEADS
HQ = 4
QUADS = HEADS // HQ
VW = 32
EXPERTS = 8
DFF = 512
HC = DFF // P
CAP = 2 * T // EXPERTS
LAT = 32
KV = 2
I_FF = 352
FP4_BLOCK = 16
E6, LT = 6, 100
LANES = 4
BLK = 32
NBLK = T // BLK
EPS = 1e-5
KEY_EPS = 1e-6
MASKED = -1e30


def constants():
    p = np.arange(P)
    f = np.arange(T)
    inv = 1.0 / 10000.0 ** (np.arange(0, HD, 2, dtype=np.float32) / np.float32(HD))
    ang = np.outer(f.astype(np.float32), inv.astype(np.float32)).astype(np.float32)
    half = HD // 2
    cos = np.cos(ang)[:, p % half].T
    sin = np.sin(ang)[:, p % half].T * np.where(p % HD < half, -1.0, 1.0)[:, None]
    return {
        "ident": np.eye(P),
        "quad_mask": (p[:, None] % 32 // HD == np.arange(HQ)[None, :]) * 1.0,
        "group_mask": (p[:, None] // 32 == np.arange(4)[None, :]) * 1.0,
        "upto": (p[:, None] <= f[None, :]) * 1.0,
        "causal": np.where(f[None, :] <= p[:, None], 0.0, MASKED),
        "slots": np.broadcast_to(np.arange(1, CAP + 1), (P, CAP)),
        "falling": np.broadcast_to(np.arange(E6, 0, -1), (P, E6)),
        "ones": np.ones((P, 32)),
        "rope": np.concatenate([cos, sin], axis=1),
    }


def rows_first(a):
    n = a.shape[0] // P
    return a.reshape(n, P, a.shape[1]).transpose(1, 0, 2).reshape(P, -1)


def column(a):
    return a.reshape(-1, 1)


def rope_order(second):
    first = [0, 2, 4, 6, 1, 3, 5, 7]
    order = first[4:] + first[:4] if second else first
    return [h * HD + r for h in range(HEADS) for r in order]


def weight_layouts(w):
    out = {}
    a = "L0_attn_"
    out["rec_qkT"] = np.concatenate([w[a + "Wq"].T, w[a + "Wk"].T], axis=1)
    out["rec_v"] = w[a + "Wv"].T
    out["rec_o"] = w[a + "Wo"].T
    out["rec_bq"] = column(w[a + "bq"])
    a = "L0_xattn_"
    out["x0_q"], out["x0_k"], out["x0_o"] = w[a + "Wq"].T, w[a + "Wk"].T, w[a + "Wc"].T
    out["x0_bq"], out["x0_bk"] = column(w[a + "bq"]), column(w[a + "bk"])
    out["f0_gate"] = w["L0_ffn_gate_w"]
    a = "L1_attn_"
    out["a1_qT"] = rows_first(w[a + "wq"].T)
    out["a1_kdown"], out["a1_vdown"] = w[a + "wk_down"], w[a + "wv_down"]
    out["a1_kupT"], out["a1_vupT"] = w[a + "wk_up"].T, w[a + "wv_up"].T
    out["a1_o"] = rows_first(w[a + "wo"])
    a = "L1_xattn_"
    out["x1_q"], out["x1_k"], out["x1_v"] = w[a + "q_w"].T, w[a + "k_w"].T, w[a + "v_w"].T
    out["x1_bq"], out["x1_bk"] = column(w[a + "q_b"]), column(w[a + "k_b"])
    a = "L1_ffn_"
    out["f1_gate"] = np.concatenate([w[a + "w_gate"][0:128], w[a + "w_gate"][128:256]], axis=1)
    out["f1_up"] = np.concatenate([w[a + "w_up"][0:128], w[a + "w_up"][128:256]], axis=1)
    out["f1_gate_rest"], out["f1_up_rest"] = w[a + "w_gate"][256:352], w[a + "w_up"][256:352]
    out["f1_down"] = w[a + "w_down"]
    a = "L2_attn_"
    out["a2_q"], out["a2_k"] = w[a + "Wq"], w[a + "Wk"]
    out["a2_bq"], out["a2_bk"] = column(w[a + "bq"]), column(w[a + "bk"])
    a = "L2_xattn_"
    out["x2_q"], out["x2_k"] = w[a + "Wq"], w[a + "Wk"]
    out["x2_v"], out["x2_o"] = w[a + "Wv"], w[a + "Wo"]
    out["x2_bq"], out["x2_bk"] = column(w[a + "bq"]), column(w[a + "bk"])
    a = "L2_ffn_"
    out["f2_A"] = w[a + "A"].transpose(2, 0, 1).reshape(16, E6 * LT)
    out["f2_B"] = w[a + "B"].transpose(1, 0, 2).reshape(16, E6 * D)
    out["f2_gate"], out["f2_wtT"], out["f2_wdT"] = w[a + "w_gate"], w[a + "wt_w"].T, w[a + "wd_w"].T
    out["f2_bt"] = column(w[a + "wt_b"])
    a = "L3_attn_"
    q, k, v = w[a + "w_qkv"][0:128], w[a + "w_qkv"][128:256], w[a + "w_qkv"][256:384]
    out["a3_qk"] = np.concatenate([q[rope_order(0)].T, q[rope_order(1)].T,
                                   k[rope_order(0)].T, k[rope_order(1)].T], axis=1)
    out["a3_v"], out["a3_o"] = v.T, w[a + "w_out"].T
    a = "L3_xattn_"
    for n in "qkv":
        out["x3_" + n] = w[a + "kernel_" + n][0, 0]
    out["x3_bq"], out["x3_bk"] = column(w[a + "bias_q"]), column(w[a + "bias_k"])
    out["x3_maskT"] = w["mask_1xSxS2_ff0"][0].T
    a = "L3_ffn_"
    out["f3_conv"] = w[a + "conv_w"].transpose(1, 2, 0).reshape(P, 3 * D)
    qkv = w[a + "wqkv"]
    out["f3_q"], out["f3_k"], out["f3_v"] = qkv[0:128].T, qkv[128:256].T, qkv[256:384].T
    out["f3_bq"], out["f3_bk"] = column(w[a + "bqkv"][0:128]), column(w[a + "bqkv"][128:256])
    out["f3_o"], out["f3_gate"] = w[a + "wo"].T, w[a + "gate_w"]
    out["f3_b1"] = w[a + "b1"].reshape(EXPERTS, HC, P).transpose(2, 0, 1).reshape(P, -1)
    out["f3_b2"] = w[a + "b2"]
    return out


def expert_layouts(w):
    out = {}
    for layer in ("L0", "L3"):
        w1, w2 = w[layer + "_ffn_w1"], w[layer + "_ffn_w2"]
        out[layer + "_w1"] = w1.transpose(1, 0, 2).reshape(P, EXPERTS * DFF)
        out[layer + "_w2"] = w2.reshape(EXPERTS, HC, P, D).transpose(2, 0, 1, 3).reshape(P, EXPERTS * DFF)
    return out


def row_layouts(w):
    out = {
        "rec_bqk": np.concatenate([w["L0_attn_bq"], w["L0_attn_bk"]]),
        "rec_bv": w["L0_attn_bv"], "rec_bo": w["L0_attn_bo"], "x0_bo": w["L0_xattn_bc"],
        "x1_bv": w["L1_xattn_v_b"], "a2_bv": w["L2_attn_bk"],
        "x2_bv": w["L2_xattn_bv"], "x2_bo": w["L2_xattn_bo"],
        "f2_bd": w["L2_ffn_wd_b"], "f2_scale": w["L2_ffn_scale"], "a3_bo": w["L3_attn_b_out"],
        "x3_bv": w["L3_xattn_bias_v"], "f3_bconv": w["L3_ffn_conv_b"],
        "f3_bv": w["L3_ffn_bqkv"][256:384], "f3_bo": w["L3_ffn_bo"],
        "f3_g1": w["L3_ffn_ln1_g"], "f3_n1": w["L3_ffn_ln1_b"], "f3_bgate": w["L3_ffn_gate_b"],
        "f3_g2": w["L3_ffn_ln2_g"], "f3_n2": w["L3_ffn_ln2_b"],
    }
    return out


PREPARED = ("a1_qT", "a1_kdown", "a1_kupT", "a1_vupT", "a1_o", "f1_gate", "f1_up", "f1_gate_rest",
            "f1_up_rest", "f1_down", "f2_A", "f2_B", "f2_wtT", "f2_wdT", "f2_bt")
"""Matrices that only the preparation reads, before the loop."""


class Signal:

    def __init__(self, sem):
        self.sem, self.count = sem, 0


class Steps:

    def __init__(self, queue, signal):
        self.queue, self.done = queue, signal

    def __call__(self, waits, emit):
        self.done.count += 1
        self.queue.append((waits, emit, self.done, 1))
        return self.done, self.done.count


def transfer(queue, signal, waits, emit):
    signal.count += 16
    queue.append((waits, emit, signal, 16))
    return signal, signal.count


def play(queue, eng, turn=None):
    for waits, emit, signal, by in queue:
        for s, count in waits:
            eng.wait_ge(s.sem, count)
        (emit(eng, turn) if by == 16 else emit(eng)).then_inc(signal.sem, by)


ENGINES = ("tensor", "scalar", "vector", "gpsimd", "sync")


def new_signal(nc, ctx, name, signals):
    signals.append(Signal(ctx.enter_context(nc.semaphore(name))))
    return signals[-1]


class Thread:
    pass


def new_thread(nc, ctx, name, queues, signals):
    parts = {short: Steps(queues[e], new_signal(nc, ctx, f"{name}_{e}_done", signals))
             for short, e in (("pe", "tensor"), ("act", "scalar"), ("dve", "vector"), ("pool", "gpsimd"))}
    thread = Thread()
    thread.dma = queues["sync"]
    thread.pe, thread.act, thread.dve, thread.pool = parts["pe"], parts["act"], parts["dve"], parts["pool"]
    return thread


def products(*each):
    def emit(e):
        for out, lhsT, rhs, first, last in each:
            ins = e.matmul(out, lhsT, rhs, start=first, stop=last)
        return ins
    return emit


def product(out, lhsT, rhs):
    return products((out, lhsT, rhs, True, True))


def transposes(ident, *each):
    def emit(e):
        for out, in_ in each:
            ins = e.transpose(out, in_, ident[0:in_.shape[0], 0:in_.shape[0]])
        return ins
    return emit


def over(ap, axis, n):
    ap = ap.unsqueeze(axis)
    shape = list(ap.shape)
    shape[axis] = n
    return ap.to_broadcast(shape)


def tt(out, a, b, op):
    return lambda e: e.tensor_tensor(out, a, b, op)


def copy(out, in_):
    return lambda e: e.tensor_copy(out, in_)


def recip(out, in_):
    return lambda e: e.reciprocal(out, in_)


def reduce_to(out, in_, op, magnitude=False):
    return lambda e: e.tensor_reduce(out, in_, AX, op, apply_absolute_value=magnitude)


def ts(out, in_, s1, op0, s2=None, op1=ALU.bypass):
    return lambda e: e.tensor_scalar(out, in_, s1, s2, op0, op1)


def stt(out, a, s, op0, b, op1):
    return lambda e: e.scalar_tensor_tensor(out=out, in0=a, scalar=s, in1=b, op0=op0, op1=op1)


def fill(out, value):
    return lambda e: e.memset(out, value)


def move(out, in_):
    return lambda e, i: e.dma_start(out, in_)


def act_copy(out, in_):
    return lambda e: e.activation(out, in_, ACT.Copy)


def act_bias(out, in_, bias):
    return lambda e: e.activation(out, in_, ACT.Identity, bias=bias)


def memory_phase(nc, dram, nb, w_off, w_total, rows_off, rows_total, c_off):
    nq = nb // 4
    queues, signals = {e: [] for e in ENGINES}, []
    with ExitStack() as ctx:
        def sb(name, shape):
            return ctx.enter_context(nc.sbuf_tensor("m_" + name, shape, F32))

        w = new_thread(nc, ctx, "m", queues, signals)
        bank = [ctx.enter_context(nc.psum_tensor(f"m_bank{i}", [P, 512], F32)) for i in range(8)]
        loaded = new_signal(nc, ctx, "m_weights_loaded", signals)
        x_loaded = [new_signal(nc, ctx, f"m_x_loaded{i}", signals) for i in range(2)]
        moved = new_signal(nc, ctx, "m_moved", signals)
        results = new_signal(nc, ctx, "m_results_stored", signals)
        ident = sb("ident", [P, P])
        qkw = sb("qkw", [P, 2 * D])
        qkb = sb("qkb", [P, 2 * D])
        xT = [sb(f"xT{i}", [P, 4, T]) for i in range(2)]
        qk = [sb(f"qk{i}", [P, 4, 2 * D]) for i in range(2)]
        tmp = sb("tmp", [P, 4, D])
        u = [sb(f"u{i}", [P, 4, D]) for i in range(2)]
        s_all = sb("s_all", [P, nb])
        norm = sb("norm", [P, nb])
        half = sb("half", [P, 4])
        uT = sb("uT", [P, nb, T])
        A = sb("A", [P, nb, D])
        yT = [sb(f"yT{i}", [P, 4, BLK]) for i in range(2)]
        y = sb("y", [P, nq, D])
        g = sb("g", [P, nq, BLK])
        E = sb("E", [nb, BLK, 2 * BLK])
        outer = sb("outer", [nb, BLK, BLK])
        col = sb("col", [nb, BLK])
        rd = sb("rd", [nb, BLK])
        xx = sb("xx", [nb, BLK, 2 * BLK])
        xs = sb("xs", [P, nq, 2, P])
        W = [sb(f"w{i}", [P, D]) for i in range(2)]
        Z = [sb(f"z{i}", [P, 4, D]) for i in range(2)]
        group_mask = sb("group_mask", [P, 4])

        def wslice(name):
            a, n = w_off[name]
            return dram["weights"][:, a:a + n]

        a, n = c_off["ident"]
        ld = transfer(w.dma, loaded, [], move(ident[:, :], dram["consts"][:, a:a + n]))
        ld = transfer(w.dma, loaded, [], move(qkw[:, :], wslice("rec_qkT")))
        a, n = c_off["group_mask"]
        ld = transfer(w.dma, loaded, [], move(group_mask[:, :], dram["consts"][:, a:a + n]))
        xs_zero = w.pool([], fill(xs[:, :, :, :], 0.0))
        ra, rn = rows_off["rec_bqk"]
        ld = transfer(w.dma, loaded, [], move(
            qkb[:, :], dram["rows"][0:1, ra:ra + rn].to_broadcast([P, rn])))
        half_set = w.pool([], fill(half[:, :], 0.5))
        A_set = {}
        for q in range(nq):
            A_set[q] = w.pool([ld], copy(A[:, 4 * q:4 * q + 4, :], over(ident[:, :], 1, 4)))

        x_read = [[], []]
        u_read = [[], []]
        uT_ready = {}
        tmp_read, turned_read = [], [[], []]
        for q in range(nq):
            i = q % 2
            xl = transfer(w.dma, x_loaded[i], x_read[i], move(
                xT[i][:, :, :], dram["xT"][:, 4 * q * T:4 * (q + 1) * T].rearrange("p (b t) -> p b t", b=4)))
            b0 = bank[2 * i], bank[2 * i + 1]
            projected = w.pe([ld, xl], products(*[
                (b0[b // 2][:, (b % 2) * 256:(b % 2) * 256 + 256], xT[i][:, b, :], qkw[:, :], True, True)
                for b in range(4)]))
            x_read[i] = [projected]
            for h in range(2):
                biased = w.dve([projected], tt(qk[i][:, 2 * h:2 * h + 2, :],
                               b0[h][:, :].rearrange("p (b c) -> p b c", b=2), over(qkb[:, :], 1, 2), ALU.add))
            kk, qq = qk[i][:, :, D:2 * D], qk[i][:, :, 0:D]
            r = slice(4 * q, 4 * q + 4)
            m = w.dve([biased] + tmp_read, tt(tmp[:, :, :], kk, qq, ALU.mult))
            m = s_ready = w.dve([m], reduce_to(s_all[:, r], tmp[:, :, :], ALU.add))
            m = w.dve([m], tt(tmp[:, :, :], kk, kk, ALU.mult))
            m = w.dve([m], reduce_to(norm[:, r], tmp[:, :, :], ALU.add))
            tmp_read = [m]
            m = w.pool([m, half_set], tt(norm[:, r], norm[:, r], half[:, :], ALU.pow))
            m = w.dve([m], ts(norm[:, r], norm[:, r], KEY_EPS, ALU.add))
            m = w.dve([m], recip(norm[:, r], norm[:, r]))
            m = w.dve([m] + u_read[i], tt(u[i][:, :, :], kk, over(norm[:, r], 2, D), ALU.mult))
            turned = w.pe([m] + turned_read[i], transposes(ident, *[
                (bank[4 + i][:, b * T:(b + 1) * T], u[i][:, b, :]) for b in range(4)]))
            u_read[i] = [turned]
            uT_ready[q] = w.act([turned], act_copy(uT[:, r, :], bank[4 + i][:, :].rearrange("p (b t) -> p b t", b=4)))
            turned_read[i] = [uT_ready[q]]

        z_ready = {q: [] for q in range(nq)}
        E_flat = E[:, :, :].rearrange("b r c -> b (r c)")
        step_of = 2 * BLK + 1
        diag = E_flat[:, 0:BLK * 2 * BLK:step_of]
        inv_diag = E_flat[:, BLK:BLK * 2 * BLK:step_of]
        y_read, xs_read, last_moved, yT_read, w_read, Yb_read, Tb_read = [], [], [], [[], []], [[], []], [[], []], [[], []]
        for blk in range(NBLK):
            cols = slice(blk * BLK, (blk + 1) * BLK)
            g_done = []
            for q in range(nq):
                i = q % 2
                Yb, Tb, Gb = bank[i], bank[2 + i], bank[4 + i]
                m = w.pe([uT_ready[q], A_set[q]] + Yb_read[i], products(*[
                    (Yb[32 * j:32 * j + 32, 0:D], uT[:, 4 * q + j, cols], A[:, 4 * q + j, :], True, True)
                    for j in range(4)] + [
                    (Tb[:, 32 * j:32 * j + 32], A[:, 4 * q + j, :], uT[:, 4 * q + j, cols], True, True)
                    for j in range(4)]))
                y_sb = w.act([m] + y_read, act_copy(y[:, q, :], Yb[:, 0:D]))
                Yb_read[i] = [y_sb]
                yT_sb = w.dve([m] + yT_read[i], copy(yT[i][:, :, :], Tb[:, 0:P].rearrange("p (j r) -> p j r", j=4)))
                m = w.pe([yT_sb] + turned_read[i], products(*[
                    (Gb[32 * j:32 * j + 32, 0:BLK], yT[i][:, j, :], uT[:, 4 * q + j, cols], True, True)
                    for j in range(4)]))
                yT_read[i] = [m]
                g_sb = w.dve([m] + last_moved, copy(g[:, q, :], Gb[:, 0:BLK]))
                g_done = [g_sb, y_sb]
            m = transfer(w.dma, moved, g_done, move(
                dram["g"].rearrange("(q j) r c -> (j r) q c", j=4), g[:, :, :]))
            cleared = w.dve([], fill(E[:, :, BLK:2 * BLK], 0.0))
            cleared = w.dve([cleared], fill(inv_diag, 1.0))
            m = transfer(w.dma, moved, [m, cleared], move(E[:, :, 0:BLK], dram["g"]))
            m = w.dve([m], ts(diag, diag, 1.0, ALU.add))
            for j in range(BLK - 1):
                n = BLK - 1 - j
                win = slice(j + 1, j + 1 + BLK)
                m = w.dve([m], recip(rd[:, 0:1], E[:, j, j:j + 1]))
                m = w.dve([m], ts(col[:, 0:n], E[:, j + 1:, j], rd[:, 0:1], ALU.mult))
                m = w.dve([m], tt(outer[:, 0:n, :], over(col[:, 0:n], 2, BLK), over(E[:, j, win], 1, n), ALU.mult))
                m = w.dve([m], tt(E[:, j + 1:, win], E[:, j + 1:, win], outer[:, 0:n, :], ALU.subtract))
            m = w.dve([m], recip(rd[:, :], diag))
            inv_T = E[:, :, BLK:2 * BLK].rearrange("b r k -> b k r")
            w.dve(last_moved, copy(xx[:, :, 0:BLK], inv_T))
            m = w.dve([m], tt(xx[:, :, BLK:2 * BLK], inv_T, over(rd[:, :], 1, BLK), ALU.mult))
            m = transfer(w.dma, moved, [m], move(dram["xx"], xx[:, :, :]))
            for j in range(4):
                for k in range(2):
                    last = transfer(w.dma, moved, [m, xs_zero] + xs_read, move(
                        xs[32 * j:32 * j + 32, :, k, 32 * j:32 * j + 32],
                        dram["xx"].rearrange("(q j) k (a m) -> j a k q m", j=4, a=2)[j, k]))
            m = last
            last_moved = [m]
            for q in range(nq):
                i = q % 2
                Wb, Zb, Tb, Ab = bank[i], bank[2 + i], bank[4 + i], bank[6 + i]
                m2 = w.pe([m, y_sb] + Tb_read[i], products(
                    (Wb[:, 0:D], xs[:, q, 0, :], y[:, q, :], True, True),
                    (Zb[:, 0:D], xs[:, q, 1, :], y[:, q, :], True, True),
                    (Tb[:, 0:P], y[:, q, :], xs[:, q, 1, :], True, True)))
                z_ready[q] = w.act([m2], act_copy(uT[:, 4 * q:4 * q + 4, cols],
                                   Tb[:, 0:P].rearrange("p (j r) -> p j r", j=4)))
                Tb_read[i] = [z_ready[q]]
                y_read = xs_read = [m2]
                if blk < NBLK - 1:
                    w_sb = w.act([m2] + w_read[i], act_copy(W[i][:, :], Wb[:, 0:D]))
                    z_sb = w.dve([m2] + w_read[i], tt(Z[i][:, :, :], over(Zb[:, 0:D], 1, 4),
                                 over(group_mask[:, :], 2, D), ALU.mult))
                    m3 = w.pe([w_sb, z_sb], product(Ab[:, :], W[i][:, :], Z[i][:, :, :]))
                    w_read[i] = [m3]
                    A_set[q] = w.dve([m3], tt(A[:, 4 * q:4 * q + 4, :], A[:, 4 * q:4 * q + 4, :],
                                       Ab[:, :].rearrange("p (j d) -> p j d", j=4), ALU.subtract))

        transfer(w.dma, results, [s_ready], move(dram["s"], s_all[:, :]))
        transfer(w.dma, results, [z_ready[nq - 1]], move(
            dram["z"].rearrange("p (b t) -> p b t", b=nb), uT[:, :, :]))

        with nc.Block() as block:
            block.tensor(lambda e: play(queues["tensor"], e))
            block.scalar(lambda e: play(queues["scalar"], e))
            block.vector(lambda e: play(queues["vector"], e))
            block.gpsimd(lambda e: play(queues["gpsimd"], e))

            @block.sync
            def _(e):
                play(queues["sync"], e)
                e.wait_ge(results.sem, results.count)


class Weights:

    def __init__(self, tensor, offsets):
        self.tensor, self.offsets = tensor, offsets

    def __getitem__(self, name):
        a, n = self.offsets[name]
        return self.tensor[:, a:a + n]

    def part(self, name, k, n=D):
        a, _ = self.offsets[name]
        return self.tensor[:, a + k * n:a + (k + 1) * n]


def new_lane(nc, ctx, n, queues, signals, shared):
    ln = new_thread(nc, ctx, f"lane{n}", queues, signals)
    ln.n = n
    ln.w, ln.r, ln.k, ln.s = shared["w"], shared["r"], shared["k"], shared

    def sb(name, *shape):
        return ctx.enter_context(nc.sbuf_tensor(f"lane{n}_{name}", list(shape), F32))

    ln.a = ctx.enter_context(nc.psum_tensor(f"lane{n}_a", [P, 512], F32))
    ln.b = ctx.enter_context(nc.psum_tensor(f"lane{n}_b", [P, 512], F32))
    ln.x = sb("x", P, D)
    ln.xT = shared["xT_all"][:, n, :]
    ln.base = sb("base", P, D)
    ln.ctxT, ln.ctx_in = sb("ctxT", P, S2), sb("ctx", S2, D)
    ln.zT, ln.kq_dot = sb("zT", P, T), shared["kq"][:, n:n + 1]
    ln.key_mask_int = ctx.enter_context(nc.sbuf_tensor(f"lane{n}_mask_int", [P, S2], I32))
    ln.key_mask = sb("mask", P, S2)
    ln.qT = sb("qT", P, T)
    ln.kq = sb("kq", P, HQ, T)
    ln.v = sb("v", P, HEADS, VW)
    ln.sc = sb("sc", P, HQ, T)
    ln.p = sb("p", P, HQ, T)
    ln.oT = sb("oT", P, QUADS, T)
    ln.o = sb("o", P, D)
    ln.wide = sb("wide", P, 600)
    ln.small = sb("small", P, 64)
    ln.mean_var = sb("mean_var", P, 2)
    ln.stats = sb("stats", P, 6)
    ln.gates = sb("gates", P, EXPERTS)
    return ln


def add_bias_to_x(ln, row, ready):
    return ln.pool(ready, tt(ln.base[:, :], ln.x[:, :], ln.r[row], ALU.add))


def normalize(ln, src, dst, ready, gain=None, shift=None):
    m = ln.dve(ready, lambda e: e.bn_stats(ln.stats[:, :], src))
    m = ln.dve([m], lambda e: e.bn_aggr(ln.mean_var[:, :], ln.stats[:, :]))
    rstd = ln.small[:, 60:61]
    m = ln.dve([m], ts(rstd, ln.mean_var[:, 1:2], EPS, ALU.add))
    m = ln.pool([m], tt(rstd, rstd, ln.s["minus_half"], ALU.pow))
    m = ln.dve([m], ts(dst, src, ln.mean_var[:, 0:1], ALU.subtract, rstd, ALU.mult))
    if gain is not None:
        m = ln.dve([m], tt(dst, dst, ln.r[gain], ALU.mult))
        m = ln.dve([m], tt(dst, dst, ln.r[shift], ALU.add))
    return m


def finish(ln, y, ready, plain=False):
    base = ln.x if plain else ln.base
    m = ln.dve(ready, tt(ln.x[:, :], base[:, :], y, ALU.add))
    m = normalize(ln, ln.x[:, :], ln.x[:, :], [m])
    yield
    m = ln.pe([m], transposes(ln.k["ident"], (ln.a[:, 0:T], ln.x[:, :])))
    m = ln.act([m], act_copy(ln.xT, ln.a[:, 0:T]))
    yield
    return m


def query_and_keys(ln, wq, bq, wk, bk, keysT, nk, ready):
    m = ln.pe(ready, products((ln.a[:, 0:T], ln.w[wq], ln.xT, True, True),
                                (ln.b[:, 0:nk], ln.w[wk], keysT, True, True)))
    q = ln.act([m], act_bias(ln.qT[:, :], ln.a[:, 0:T], ln.w[bq]))
    k = ln.dve([m], stt(ln.kq[:, :, 0:nk], over(ln.b[:, 0:nk], 1, HQ), ln.w[bk], ALU.add,
                          over(ln.k["quad_mask"], 2, nk), ALU.mult))
    return q, k


def values(ln, wv, bv, srcT, nk, ready):
    m = ln.pe(ready, product(ln.a[0:nk, 0:D], srcT, ln.w[wv]))
    return ln.dve([m], tt(ln.v[0:nk, :, 0:HD], heads(ln.a[0:nk, 0:D]),
                            heads(ln.r[bv][0:nk, :]), ALU.add))


def attention(ln, nk, scale, ready, bias=None):
    a, b = ln.a, ln.b
    a4 = a[:, :].rearrange("p (h k) -> p h k", h=HQ)
    b4 = b[:, :].rearrange("p (h q) -> p h q", h=HQ)
    top = ln.small[:, 0:HQ]
    b_read = []
    for quad in range(QUADS):
        rows = slice(32 * quad, 32 * quad + 32)
        m = ln.pe(ready, product(a4[:, :, 0:nk], ln.qT[rows, :], ln.kq[rows, :, 0:nk]))
        src, sc = a4[:, :, 0:nk], ln.sc[:, :, 0:nk]
        if bias is not None:
            m = ln.dve([m], tt(sc, src, over(bias, 1, HQ), ALU.add))
            src = sc
        m = ln.dve([m], reduce_to(top, src, ALU.max))
        m = ln.dve([m], tt(sc, src, over(top, 2, nk), ALU.subtract))
        yield
        m = ln.pe([m] + b_read, transposes(ln.k["ident"], *[
            (b4[0:nk, h, :], ln.sc[:, h, 0:nk]) for h in range(HQ)]))
        m = ln.act([m], lambda e: e.activation(ln.p[0:nk, :, :], b4[0:nk, :, :], ACT.Exp, scale=scale))
        yield
        m = ln.pe([m], products(*[
            (b[32 * h:32 * h + 32, 0:T], ln.v[0:nk, HQ * quad + h, :], ln.p[0:nk, h, :], True, True)
            for h in range(HQ)]))
        m = ln.act([m], act_copy(ln.oT[:, quad, :], b[:, 0:T]))
        b_read = [m]
        yield
    m = ln.pe([m], transposes(ln.k["ident"], *[
        (a4[:, quad, :], ln.oT[:, quad, :]) for quad in range(QUADS)]))
    out = a[:, :].rearrange("p (h c) -> p h c", h=HEADS)
    total = ln.small[:, 0:HEADS]
    m = ln.dve([m], recip(total, out[:, :, HD]))
    m = ln.dve([m], tt(heads(ln.o[:, :]), out[:, :, 0:HD], over(total, 2, HD), ALU.mult))
    yield
    return m


def project_out(ln, wo, ready):
    m = ln.pe([ready], transposes(ln.k["ident"], (ln.b[:, 0:T], ln.o[:, :])))
    m = ln.act([m], act_copy(ln.oT[:, 0, :], ln.b[:, 0:T]))
    yield
    return ln.pe([m], product(ln.a[:, 0:D], ln.oT[:, 0, :], ln.w[wo]))

def recurrent_attention(ln, loaded, s_loaded):
    a, b = ln.a, ln.b
    base = add_bias_to_x(ln, "rec_bo", [loaded])
    m = ln.pe([loaded], products((a[:, 0:D], ln.xT, ln.w["rec_v"], True, True),
                                   (b[:, 0:T], ln.w.part("rec_qkT", 0), ln.xT, True, True)))
    v = ln.dve([m], tt(ln.o[:, :], a[:, 0:D], ln.r["rec_bv"], ALU.add))
    q = ln.act([m], act_bias(ln.qT[:, :], b[:, 0:T], ln.w["rec_bq"]))
    yield
    m = ln.pe([q, v], product(a[:, 0:T], ln.zT[:, :], ln.qT[:, :]))
    m = ln.dve([m, s_loaded], stt(ln.sc[:, 0, :], a[:, 0:T], ln.kq_dot, ALU.mult, ln.k["upto"], ALU.mult))
    yield
    m = ln.pe([v, m], product(b[:, 0:T], ln.o[:, :], ln.sc[:, 0, :]))
    m = ln.act([m], act_copy(ln.oT[:, 0, :], b[:, 0:T]))
    yield
    m = ln.pe([m], product(a[:, 0:D], ln.oT[:, 0, :], ln.w["rec_o"]))
    return (yield from finish(ln, a[:, 0:D], [m, base]))


def context_attention(ln, ready, name, scale, bias=None, out=True, raw_values=False):
    if out:
        base = add_bias_to_x(ln, name + "_bo", ready)
    if raw_values:
        v = ln.pool(ready, copy(ln.v[0:S2, :, 0:HD], heads(ln.ctx_in[:, :])))
    else:
        v = values(ln, name + "_v", name + "_bv", ln.ctxT[:, :], S2, ready)
    q, k = query_and_keys(ln, name + "_q", name + "_bq", name + "_k", name + "_bk", ln.ctxT[:, :], S2, ready + [v])
    yield
    o = yield from attention(ln, S2, scale, [q, k, v], bias)
    if out:
        y = yield from project_out(ln, name + "_o", o)
        return (yield from finish(ln, ln.a[:, 0:D], [y, base]))
    return (yield from finish(ln, ln.o[:, :], [o], plain=True))


def route(ln, ready):
    m = ln.pe(ready, product(ln.a[:, 0:EXPERTS], ln.xT, ln.w["f0_gate"]))
    m = gate_softmax(ln, m, ln.s["probs"][:, ln.n, :])
    yield
    return m


def gate_softmax(ln, m, out):
    logits = ln.small[:, 0:EXPERTS]
    top, total = ln.small[:, 16:17], ln.small[:, 17:18]
    m = ln.dve([m], reduce_to(top, ln.a[:, 0:EXPERTS], ALU.max))
    m = ln.dve([m], ts(logits, ln.a[:, 0:EXPERTS], top, ALU.subtract))
    m = ln.act([m], lambda e: e.activation(logits, logits, ACT.Exp))
    m = ln.dve([m], reduce_to(total, logits, ALU.add))
    m = ln.dve([m], recip(total, total))
    return ln.dve([m], ts(out, logits, total, ALU.mult))


def latent_attention(ln, ready):
    a, b = ln.a, ln.b
    a4 = a[:, :].rearrange("p (h k) -> p h k", h=HQ)
    b4 = b[:, :].rearrange("p (h q) -> p h q", h=HQ)
    top = ln.small[:, 0:HQ]
    for kv in range(KV):
        start = ready if kv == 0 else [o]
        m = ln.pe(start, products((a[:, 0:T], ln.s["a1_q"][:, kv, :], ln.xT, True, True),
                                    (b[:, 0:T], ln.s["a1_k"][:, kv, :], ln.xT, True, True)))
        q = ln.act([m], act_copy(ln.qT[:, :], a[:, 0:T]))
        k = ln.dve([m], tt(ln.kq[:, :, :], over(b[:, 0:T], 1, HQ), over(ln.k["group_mask"], 2, T), ALU.mult))
        yield
        if kv == 0:
            m = ln.pe([k], product(b[:, 0:KV * LAT], ln.xT, ln.w["a1_vdown"]))
            v = ln.act([m], act_copy(ln.wide[:, 0:KV * LAT], b[:, 0:KV * LAT]))
        m = ln.pe([q, k], product(a[:, :], ln.qT[:, :], ln.kq[:, :, :]))
        m = ln.dve([m], tt(ln.sc[:, :, :], a4, over(ln.k["causal"], 1, HQ), ALU.add))
        m = ln.dve([m], reduce_to(top, ln.sc[:, :, :], ALU.max))
        m = ln.dve([m], tt(ln.sc[:, :, :], ln.sc[:, :, :], over(top, 2, T), ALU.subtract))
        yield
        m = ln.pe([m, v], transposes(ln.k["ident"], *[
            (b4[:, h, :], ln.sc[:, h, :]) for h in range(HQ)]))
        m = ln.act([m], lambda e: e.activation(ln.p[:, :, :], b4, ACT.Exp, scale=float(P) ** -0.5))
        yield
        m = ln.pe([m, v], products(*[
            (b[32 * h:32 * h + 32, 0:T], ln.wide[:, kv * LAT:(kv + 1) * LAT], ln.p[:, h, :], True, True)
            for h in range(HQ)] + [
            (b[32 * h:32 * h + 32, T:2 * T], ln.k["ones"], ln.p[:, h, :], True, True)
            for h in range(HQ)]))
        m = ln.dve([m], recip(ln.sc[:, 0, :], b[:, T:2 * T]))
        o = ln.dve([m], tt(ln.oT[:, kv, :], b[:, 0:T], ln.sc[:, 0, :], ALU.mult))
        yield
    m = ln.pe([o], products(*[(a[:, 0:D], ln.oT[:, kv, :], ln.s["a1_vo"][:, kv, :], kv == 0, kv == KV - 1)
                                for kv in range(KV)]))
    return (yield from finish(ln, a[:, 0:D], [m], plain=True))


def fp4_feed_forward(ln, ready):
    a, b = ln.a, ln.b
    x_rounded = ln.o
    m = fp4_round(ln, ln.x[:, :], x_rounded[:, :], D // FP4_BLOCK, ready, fp4_buffers(ln))
    yield
    m = ln.pe([m], transposes(ln.k["ident"], (a[:, 0:T], x_rounded[:, :])))
    m = ln.act([m], act_copy(ln.qT[:, :], a[:, 0:T]))
    yield
    m = ln.pe([m], products((a[:, 0:I_FF], ln.qT[:, :], ln.s["f1_gateT"][:, :], True, True),
                              (b[:, 0:I_FF], ln.qT[:, :], ln.s["f1_upT"][:, :], True, True)))
    h = ln.wide[:, 0:I_FF]
    m = ln.act([m], lambda e: e.activation(h, a[:, 0:I_FF], ACT.Silu))
    yield
    m = ln.dve([m], tt(h, h, b[:, 0:I_FF], ALU.mult))
    m = fp4_round(ln, h, h, I_FF // FP4_BLOCK, [m], fp4_buffers(ln))
    yield
    chunks = [(c, min(P, I_FF - c * P)) for c in range(3)]
    m = ln.pe([m], transposes(ln.k["ident"], *[
        (a[0:n, c * T:(c + 1) * T], ln.wide[:, c * P:c * P + n]) for c, n in chunks]))
    m = ln.act([m], act_copy(ln.p[:, 0:2, :], a[:, 0:2 * T].rearrange("p (c t) -> p c t", c=2)))
    n = chunks[2][1]
    m = ln.act([m], act_copy(ln.p[0:n, 2, :], a[0:n, 2 * T:3 * T]))
    yield
    m = ln.pe([m], products(*[(b[:, 0:D], ln.p[0:n, c, :], ln.s["f1_downT"][0:n, c, :], c == 0, c == 2)
                                for c, n in chunks]))
    return (yield from finish(ln, b[:, 0:D], [m], plain=True))


def self_attention_shared_values(ln, ready):
    v = values(ln, "a2_k", "a2_bv", ln.xT, T, ready)
    q, k = query_and_keys(ln, "a2_q", "a2_bq", "a2_k", "a2_bk", ln.xT, T, ready + [v])
    yield
    o = yield from attention(ln, T, float(D) ** -0.5, [q, k, v])
    return (yield from finish(ln, ln.o[:, :], [o], plain=True))


def low_rank_feed_forward(ln, ready):
    a, b = ln.a, ln.b
    half = E6 // 2 * LT
    tokT = ln.s["f2_tokT"]
    m = ln.pe(ready, products(
        (a[:, 0:half], ln.xT, tokT[:, 0:half], True, True),
        (a[:, half:half + E6], ln.xT, ln.w["f2_gate"], True, True),
        (b[:, 0:half], ln.xT, tokT[:, half:2 * half], True, True)))
    g, top, tie = ln.small[:, 0:E6], ln.small[:, 16:17], ln.small[:, 8:8 + E6]
    g_m = ln.dve([m], reduce_to(top, a[:, half:half + E6], ALU.max))
    g_m = ln.dve([g_m], ts(tie, a[:, half:half + E6], top, ALU.is_equal))
    g_m = ln.dve([g_m], tt(tie, tie, ln.k["falling"], ALU.mult))
    g_m = ln.dve([g_m], reduce_to(top, tie, ALU.max))
    g_m = ln.dve([g_m], tt(g, tie, top.to_broadcast([P, E6]), ALU.is_equal))
    wide = ln.wide[:, :].rearrange("p (e l) -> p e l", e=E6)
    m = ln.dve([g_m], tt(wide[:, 0:3, :], a[:, 0:half].rearrange("p (e l) -> p e l", e=3),
                           over(ln.small[:, 0:3], 2, LT), ALU.mult))
    m = ln.dve([g_m], tt(wide[:, 3:6, :], b[:, 0:half].rearrange("p (e l) -> p e l", e=3),
                           over(ln.small[:, 3:6], 2, LT), ALU.mult))
    own = ln.sc[:, 0, 0:LT]
    m = ln.dve([m], reduce_to(own, ln.wide[:, :].rearrange("p (e l) -> p l e", e=E6), ALU.add))
    m = ln.dve([m], reduce_to(top, own, ALU.max))
    m = ln.dve([m], ts(top, top, -float(D) ** -0.5, ALU.mult))
    total = ln.small[:, 17:18]
    m = ln.act([m], lambda e: e.activation(own, own, ACT.Exp, bias=top, scale=float(D) ** -0.5, accum_out=total))
    m = ln.dve([m], recip(total, total))
    m = ln.dve([m], ts(own, own, total, ALU.mult))
    yield
    m = ln.pe([m], transposes(ln.k["ident"], (a[0:LT, 0:T], own)))
    m = ln.act([m], act_copy(ln.p[0:LT, 0, :], a[0:LT, 0:T]))
    yield
    val = ln.s["f2_val"]
    m = ln.pe([m], products(
        (a[:, 0:3 * D], ln.p[0:LT, 0, :], val[0:LT, 0:3 * D], True, True),
        (a[:, 3 * D:4 * D], ln.xT, ln.s["f2_wd"][:, :], True, True),
        (b[:, 0:3 * D], ln.p[0:LT, 0, :], val[0:LT, 3 * D:6 * D], True, True)))
    acc = ln.o[:, :]
    m = ln.dve([m], tt(acc, a[:, 3 * D:4 * D], ln.s["f2_bd"], ALU.add))
    for e in range(E6):
        bank = a if e < 3 else b
        m = ln.dve([m], stt(acc, bank[:, e % 3 * D:(e % 3 + 1) * D], ln.small[:, e:e + 1], ALU.mult,
                              acc, ALU.add))
    m = ln.act([m], lambda e: e.activation(acc, acc, ACT.Exp))
    zero = ln.sc[:, 0, :]
    m = ln.dve([m], ts(zero, acc, 0.0, ALU.is_equal, float(np.finfo(np.float32).eps), ALU.mult))
    m = ln.dve([m], tt(acc, acc, zero, ALU.add))
    yield
    m = ln.act([m], lambda e: e.activation(acc, acc, ACT.Ln))
    m = ln.dve([m], tt(acc, acc, ln.x[:, :], ALU.add))
    return (yield from finish(ln, acc, [m], plain=True))


def rotary_attention(ln, ready):
    a, b = ln.a, ln.b
    base = add_bias_to_x(ln, "a3_bo", ready)
    m = ln.pe(ready, product(b[:, 0:D], ln.xT, ln.w["a3_v"]))
    v = ln.act([m], act_copy(ln.v[:, :, 0:HD], heads(b[:, 0:D])))
    m = ln.pe(ready, products(*[(a[:, i * T:(i + 1) * T], ln.w.part("a3_qk", i), ln.xT, True, True)
                                  for i in range(4)]))
    rot = ln.sc[:, :, :].rearrange("p (n f) t -> p n f t", n=2)
    m = ln.dve([m], tt(rot, a[:, :].rearrange("p (n f t) -> p n f t", n=2, f=2),
                         over(ln.k["rope"].rearrange("p (f t) -> p f t", f=2), 1, 2), ALU.mult))
    q = ln.dve([m], tt(ln.qT[:, :], ln.sc[:, 0, :], ln.sc[:, 1, :], ALU.add))
    k = ln.dve([m], tt(ln.o[:, :], ln.sc[:, 2, :], ln.sc[:, 3, :], ALU.add))
    k = ln.dve([k], tt(ln.kq[:, :, :], over(ln.o[:, :], 1, HQ), over(ln.k["quad_mask"], 2, T), ALU.mult))
    yield
    o = yield from attention(ln, T, float(HD) ** -0.5, [q, k, v])
    y = yield from project_out(ln, "a3_o", o)
    return (yield from finish(ln, a[:, 0:D], [y, base]))


def relu_attention(ln, ready):
    a, b = ln.a, ln.b
    m = ln.pe(ready, products((a[:, 0:T], ln.w["x3_q"], ln.xT, True, True),
                                (b[:, 0:S2], ln.w["x3_k"], ln.ctxT[:, :], True, True)))
    q = ln.act([m], lambda e: e.activation(ln.qT[:, :], a[:, 0:T], ACT.Relu, bias=ln.w["x3_bq"]))
    kT = ln.kq[:, 0, 0:S2]
    k = ln.dve([m], ts(kT, b[:, 0:S2], ln.w["x3_bk"], ALU.add, 0.0, ALU.max))
    yield
    m = ln.pe([q], product(a[0:S2, 0:D], ln.ctxT[:, :], ln.w["x3_v"]))
    vals = ln.wide[0:S2, 0:D]
    v = ln.dve([m], tt(vals, a[0:S2, 0:D], ln.r["x3_bv"][0:S2, :], ALU.add))
    v = ln.dve([v], ts(vals, vals, 0.0, ALU.max))
    m = ln.pe([q, k], product(b[0:S2, 0:T], kT, ln.qT[:, :]))
    lg = ln.p[0:S2, 0, :]
    m = ln.dve([m], ts(lg, b[0:S2, 0:T], 0.0, ALU.max, float(D) ** -0.5, ALU.mult))
    m = ln.dve([m], tt(lg, lg, ln.w["x3_maskT"][0:S2, :], ALU.add))
    yield
    m = ln.pe([m, v], product(b[:, 0:D], lg, vals))
    m = ln.act([m], lambda e: e.activation(ln.o[:, :], b[:, 0:D], ACT.Relu))
    return (yield from finish(ln, ln.o[:, :], [m], plain=True))


def conv_and_attention(ln, ready):
    a, b = ln.a, ln.b
    ends = ln.pool(ready, fill(ln.wide[:, 0:T + 2:T + 1], 0.0))
    m = ln.pool(ready, copy(ln.wide[:, 1:T + 1], ln.xT))
    conv = ln.pe([m, ends], products(*[
        (a[:, 0:D], ln.wide[:, i:i + T], ln.w.part("f3_conv", i), i == 0, i == 2) for i in range(3)]))
    conv_out = ln.oT[:, 3, :]
    m = ln.dve([conv], tt(conv_out, a[:, 0:D], ln.r["f3_bconv"], ALU.add))
    base = ln.pool([m], tt(ln.base[:, :], conv_out, ln.r["f3_bo"], ALU.add))
    yield
    m = ln.pe([m], transposes(ln.k["ident"], (b[:, 0:T], conv_out)))
    y_ready = ln.act([m], act_copy(ln.xT, b[:, 0:T]))
    yield
    v = values(ln, "f3_v", "f3_bv", ln.xT, T, [y_ready])
    q, k = query_and_keys(ln, "f3_q", "f3_bq", "f3_k", "f3_bk", ln.xT, T, [y_ready, v])
    yield
    o = yield from attention(ln, T, float(HD) ** -0.5, [q, k, v, base])
    y = yield from project_out(ln, "f3_o", o)
    m = ln.dve([y, base], tt(ln.o[:, :], ln.base[:, :], a[:, 0:D], ALU.add))
    mid = ln.base
    m = normalize(ln, ln.o[:, :], mid[:, :], [m], "f3_g1", "f3_n1")
    yield
    m = ln.pe([m], transposes(ln.k["ident"], (a[:, 0:T], mid[:, :])))
    midT = ln.act([m], act_copy(ln.xT, a[:, 0:T]))
    yield
    m = ln.pe([midT], product(a[:, 0:EXPERTS], ln.xT, ln.w["f3_gate"]))
    logits = ln.small[:, 0:EXPERTS]
    top, total = ln.small[:, 16:17], ln.small[:, 17:18]
    m = ln.dve([m], tt(logits, a[:, 0:EXPERTS], ln.r["f3_bgate"], ALU.add))
    m = ln.dve([m], reduce_to(top, logits, ALU.max))
    m = ln.dve([m], ts(logits, logits, top, ALU.subtract))
    m = ln.act([m], lambda e: e.activation(logits, logits, ACT.Exp))
    m = ln.dve([m], reduce_to(total, logits, ALU.add))
    m = ln.dve([m], recip(total, total))
    m = ln.dve([m], ts(ln.gates[:, :], logits, total, ALU.mult))
    yield
    m = ln.pe([m], transposes(ln.k["ident"], (a[0:EXPERTS, 0:T], ln.gates[:, :])))
    m = ln.act([m], act_copy(ln.o[0:EXPERTS, :], a[0:EXPERTS, 0:T]))
    yield
    m = ln.pe([m], product(b[:, 0:D], ln.o[0:EXPERTS, :], ln.w["f3_b2"][0:EXPERTS, :]))
    m = ln.dve([m], tt(mid[:, :], mid[:, :], b[:, 0:D], ALU.add))
    yield
    return midT, m


def end_of_mixture(ln, mixed):
    m = normalize(ln, ln.base[:, :], ln.o[:, :], [mixed], "f3_g2", "f3_n2")
    m = ln.dve([m], tt(ln.x[:, :], ln.x[:, :], ln.o[:, :], ALU.add))
    yield
    m = normalize(ln, ln.x[:, :], ln.x[:, :], [m])
    yield
    return m


def heads(ap):
    return ap.rearrange("p (h c) -> p h c", h=HEADS)


def blocks(ap, n):
    return ap.rearrange("p (b c) -> p b c", b=n)


def fp4_buffers(lane):
    flat = [t[:, :, :].rearrange("p h t -> p (h t)") for t in (lane.sc, lane.p, lane.oT)]
    return flat + [lane.small]


def fp4_round(w, src, dst, n, ready, buffers, rows=P):
    mag, sign, level, small = buffers
    size = n * FP4_BLOCK
    mag, sign, level = mag[0:rows, 0:size], sign[0:rows, 0:size], level[0:rows, 0:size]
    scale, inv = small[0:rows, 0:n], small[0:rows, 32:32 + n]
    m = w.dve(ready, reduce_to(scale, blocks(src, n), ALU.max, magnitude=True))
    m = w.dve([m], ts(scale, scale, 1.0 / 6.0, ALU.mult, 1e-12, ALU.max))
    m2 = w.dve([m], recip(inv, scale))
    m2 = w.dve([m2], tt(blocks(mag, n), blocks(src, n), over(inv, 2, FP4_BLOCK), ALU.mult))
    s = w.act([m2], lambda e: e.activation(sign, mag, ACT.Sign))
    s = w.pool([s, m], tt(blocks(sign, n), blocks(sign, n), over(scale, 2, FP4_BLOCK), ALU.mult))
    m2 = w.act([m2], lambda e: e.activation(mag, mag, ACT.Abs))
    m = w.dve([m2], ts(level, mag, 5.0, ALU.is_gt, 2.0, ALU.mult))
    for mid in (3.5, 2.5):
        m = w.dve([m], stt(level, mag, mid, ALU.is_gt, level, ALU.add))
    m = w.dve([m], ts(level, level, 2.0, ALU.mult))
    for mid in (1.75, 1.25, 0.75, 0.25):
        m = w.dve([m], stt(level, mag, mid, ALU.is_gt, level, ALU.add))
    return w.dve([m, s], stt(dst, level, 0.5, ALU.mult, sign, ALU.mult))


def routed_mixture(w, lanes, s, banks, x_ready, probs_ready):
    k = s["k"]
    probs = s["probs"][:, :, :].rearrange("p n e -> p (n e)")
    ne = LANES * EXPERTS
    m = w.pe(probs_ready, transposes(k["ident"], (banks[0][0:ne, 0:T], probs)))
    left, best = s["left"], s["best"]
    m = w.dve([m], copy(left[:, :], banks[0][0:ne, 0:T]))
    for _ in range(CAP // 8):
        m = w.dve([m], lambda e: e.max(best[:, :], left[:, :]))
        m = w.dve([m], lambda e: e.match_replace(left[:, :], best[:, :], left[:, :], -1.0))
    m = w.dve([m], ts(left[:, :], left[:, :], 0.0, ALU.is_lt))
    m = w.pe([m], transposes(k["ident"], (banks[1][:, 0:ne], left[:, :])))
    taken, place = s["taken"], s["place"]
    taken_m = w.dve([m], copy(taken[:, :], banks[1][:, 0:ne]))
    m = w.pe([taken_m], product(banks[2][:, 0:ne], k["upto"], taken[:, :]))
    m = w.dve([m], tt(place[:, :], banks[2][:, 0:ne], taken[:, :], ALU.mult))
    pick, weighted = s["pick"], s["weighted"]
    by_expert = [t.rearrange("p (n e) -> p e n", n=LANES) for t in (place[:, :], probs)]
    picked = w.dve([m], tt(pick[:, :, :, :], over(by_expert[0], 3, CAP),
                           k["slots"].unsqueeze(1).unsqueeze(1).to_broadcast([P, EXPERTS, LANES, CAP]), ALU.is_equal))
    weighed = w.pool([picked], tt(weighted[:, :, :, :], pick[:, :, :, :], over(by_expert[1], 3, CAP), ALU.mult))
    xin = s["xin"]
    for ln in lanes:
        bank = banks[ln.n]
        m = w.pe([picked] + x_ready[ln.n], product(bank[:, 0:EXPERTS * CAP].rearrange("p (e s) -> p e s", e=EXPERTS),
                 ln.x[:, :], pick[:, :, ln.n, :]))
        xin_m = w.act([m], act_copy(xin[:, :, ln.n, :], bank[:, 0:EXPERTS * CAP].rearrange("p (e s) -> p e s", e=EXPERTS)))
    back = s["back"]
    for h in range(2):
        bank = banks[4 + h]
        m = w.pe([weighed], transposes(k["ident"], *[
            (bank[:, i * T:(i + 1) * T], weighted[:, 4 * h + i, :, :].rearrange("p n s -> p (n s)"))
            for i in range(4)]))
        back_m = w.dve([m], copy(back[:, 4 * h:4 * h + 4, :], bank[:, :].rearrange("p (e t) -> p e t", e=4)))
    hid, y = s["hid"], s["moe_y"]
    hid_read, out_read = [[], []], [[], []]
    w1, w2 = s["L0_w1"], s["L0_w2"]
    for e in range(EXPERTS):
        i, bank, out = e % 2, banks[e % 2], banks[2 + e % 2]
        m = w.pe([xin_m], products(*[
            (bank[:, c * P:(c + 1) * P], w1[:, e, c * P:(c + 1) * P], xin[:, e, :, :], True, True)
            for c in range(HC)]))
        hidden = hid[:, i, 0:DFF]
        m = w.act([m] + hid_read[i], lambda g, hidden=hidden, bank=bank: g.activation(hidden, bank[:, :], ACT.Gelu))
        m = w.pe([m] + out_read[i], products(*[
            (out[:, 0:D], hid[:, i, c * P:(c + 1) * P], w2[:, e, c, :], c == 0, c == HC - 1)
            for c in range(HC)]))
        hid_read[i] = [m]
        y_m = w.dve([m], copy(y[:, e, :], out[:, 0:D]))
        out_read[i] = [y_m]
    mixed = []
    for ln in lanes:
        rows = slice(CAP * ln.n, CAP * (ln.n + 1))
        mixed.append(ln.pe([y_m, back_m], products(*[
            (ln.a[:, 0:D], back[rows, e, :], y[rows, e, :], e == 0, e == EXPERTS - 1)
            for e in range(EXPERTS)])))
    return mixed


def gated_mixture(w, lanes, s, banks, ready, mix_ready):
    hid, w1, w2 = s["hid"], s["L3_w1"], s["L3_w2"]
    acc = list(mix_ready)
    read = [[], []]
    for e in range(EXPERTS):
        i = e % 2
        done = []
        for c in range(HC):
            bank = banks[c]
            m = w.pe(ready, product(bank[:, :], w1[:, e, c * P:(c + 1) * P], s["xT_all"][:, :, :]))
            bias = w.dve if c % 2 else w.act
            out, col = hid[:, i, c * 512:(c + 1) * 512], s["w"].part("f3_b1", e * HC + c, 1)
            if c % 2:
                done.append(w.dve([m] + read[i], ts(out, bank[:, :], col, ALU.add, 0.0, ALU.max)))
            else:
                done.append(w.act([m] + read[i], lambda g, out=out, bank=bank, col=col: g.activation(
                    out, bank[:, :], ACT.Relu, bias=col)))
        bank = banks[4 + i]
        m = w.pe(done + mix_ready, products(*[
            (bank[:, ln.n * D:(ln.n + 1) * D], hid[:, i, c * 512 + ln.n * T:c * 512 + (ln.n + 1) * T],
             w2[:, e, c, :], c == 0, c == HC - 1) for ln in lanes for c in range(HC)]))
        read[i] = [m]
        for ln in lanes:
            acc[ln.n] = w.dve([m, acc[ln.n]], stt(ln.base[:, :], bank[:, ln.n * D:(ln.n + 1) * D],
                              ln.gates[:, e:e + 1], ALU.mult, ln.base[:, :], ALU.add))
    return acc


def alternate(threads):
    threads = dict(enumerate(threads))
    returned = [None] * len(threads)
    while threads:
        for n in list(threads):
            try:
                next(threads[n])
            except StopIteration as end:
                returned[n] = end.value
                del threads[n]
    return returned


def prepare(w, s, wt, ready, banks, temp):
    k = s["k"]
    w.dve(ready, fill(temp["small"][:, :], 0.0))
    w.act(ready, act_copy(temp["first"][:, :], k["ident"]))
    w.pe(ready, transposes(k["ident"], (banks[7][:, 0:P], k["ident"])))
    m = w.pe([], products(*[
        (banks[0][:, h * LAT:(h + 1) * LAT], wt.part("a1_qT", h), wt["a1_kupT"], True, True) for h in range(8)]))
    w.dve([m], copy(s["a1_q"][:, :, :], banks[0][:, 0:8 * LAT].rearrange("p (n c) -> p n c", n=KV)))
    vo = []
    for kv in range(KV):
        w.dve([], copy(s["a1_k"][:, kv, :].rearrange("p (h c) -> p h c", h=HQ),
                       over(wt["a1_kdown"][:, kv * LAT:(kv + 1) * LAT], 1, HQ)))
        m = w.pe(vo, products(*[
            (banks[1][32 * h:32 * h + 32, 0:D], wt["a1_vupT"], wt.part("a1_o", kv * HQ + h), True, True)
            for h in range(HQ)]))
        vo = [w.dve([m], copy(s["a1_vo"][:, kv, :], banks[1][:, 0:D]))]
    scale = s["r"]["f2_scale"]
    wd = w.dve([], ts(s["f2_wd"][:, :], wt["f2_wdT"], scale, ALU.mult))
    w.dve([], ts(s["f2_bd"], s["r"]["f2_bd"], scale, ALU.mult))
    valT = temp["valT"]
    for e in range(E6):
        m = w.pe([], product(banks[2][:, 0:LT], wt["f2_B"][0:16, e * D:(e + 1) * D],
                             wt["f2_A"][0:16, e * LT:(e + 1) * LT]))
        tokT = s["f2_tokT"][:, e * LT:(e + 1) * LT]
        m = w.dve([m], copy(tokT, banks[2][:, 0:LT]))
        m = w.pe([m], product(banks[3][:, 0:LT], wt["f2_wtT"], tokT))
        m = w.act([m], act_bias(valT[:, 0:LT], banks[3][:, 0:LT], wt["f2_bt"]))
        m = w.pe([m, wd], product(banks[4][0:LT, 0:D], valT[:, 0:LT], s["f2_wd"][:, :]))
        val = w.dve([m], copy(s["f2_val"][0:LT, e * D:(e + 1) * D], banks[4][0:LT, 0:D]))
    w.dve([val], fill(s["f2_val"][0:1, :], 0.0))
    w.dve([], ts(s["x2_mask"][:, :], s["x2_mask_int"][:, :], 0.0, ALU.is_equal, MASKED, ALU.mult))
    buffers = (temp["mag"], temp["sign"], temp["level"], temp["small"])
    m = None
    for name in ("gate", "up"):
        tiles = [(wt.part("f1_" + name, 0), P, 0), (wt.part("f1_" + name, 1), P, P),
                 (wt[f"f1_{name}_rest"][0:96, :], 96, 2 * P)]
        for tile, rows, at in tiles:
            m = fp4_round(w, tile, tile, D // FP4_BLOCK, [m] if m else [], buffers, rows)
            t = w.pe([m], transposes(k["ident"], (banks[5][:, 0:rows], tile)))
            w.act([t], act_copy(s[f"f1_{name}T"][:, at:at + rows], banks[5][:, 0:rows]))
    m = fp4_round(w, wt["f1_down"], wt["f1_down"], I_FF // FP4_BLOCK, [m], buffers)
    bank_read = []
    for c in range(3):
        n = min(P, I_FF - c * P)
        t = w.pe([m] + bank_read, transposes(k["ident"], (banks[6][0:n, 0:D], wt["f1_down"][:, c * P:c * P + n])))
        bank_read = [w.act([t], act_copy(s["f1_downT"][0:n, c, :], banks[6][0:n, 0:D]))]


def decoder_phase(nc, dram, nb, w_off, w_total, p_off, p_total, rows_off, rows_total, c_off, c_total):
    with ExitStack() as ctx:
        def sb(name, *shape, dt=F32):
            return ctx.enter_context(nc.sbuf_tensor(name, list(shape), dt))

        queues, signals = {e: [] for e in ENGINES}, []
        experts_loaded = Signal(ctx.enter_context(nc.semaphore("experts_loaded")))
        weights, rows, consts = sb("weights_sb", P, w_total), sb("rows_sb", P, rows_total), sb("consts_sb", P, c_total)
        s = {
            "w": Weights(weights, w_off), "r": Weights(rows, rows_off), "k": Weights(consts, c_off),
            "xT_all": sb("xT_all", P, LANES, T),
            "a1_q": sb("a1_q", P, KV, P), "a1_k": sb("a1_k", P, KV, P), "a1_vo": sb("a1_vo", P, KV, D),
            "f1_gateT": sb("f1_gateT", P, I_FF), "f1_upT": sb("f1_upT", P, I_FF), "f1_downT": sb("f1_downT", P, 3, D),
            "f2_tokT": sb("f2_tokT", P, E6 * LT), "f2_val": sb("f2_val", P, E6 * D), "f2_wd": sb("f2_wd", P, D),
            "x2_mask": sb("x2_mask", P, S2), "x2_mask_int": sb("x2_mask_int", P, S2, dt=I32),
            "kq": sb("kq_dots", P, LANES),
            "probs": sb("probs", P, LANES, EXPERTS), "left": sb("left", LANES * EXPERTS, T),
            "best": sb("best", LANES * EXPERTS, 8), "taken": sb("taken", P, LANES * EXPERTS),
            "place": sb("place", P, LANES * EXPERTS),
        }
        s["f2_bd"] = sb("f2_bd_scaled", P, D)[:, :]
        s["minus_half"] = sb("minus_half", P, 1)[:, :]
        for layer in ("L0", "L3"):
            s[layer + "_w1"] = sb(layer + "_w1", P, EXPERTS, DFF)
            s[layer + "_w2"] = sb(layer + "_w2", P, EXPERTS, HC, D)
        scratch = sb("mixture_scratch", P, 6144)
        quarters = [scratch[:, i * 1024:(i + 1) * 1024] for i in range(6)]
        split = "p (e n s) -> p e n s"
        s["pick"], s["weighted"], s["xin"] = [
            q.rearrange(split, e=EXPERTS, n=LANES) for q in quarters[0:3]]
        s["back"], s["moe_y"] = [q.rearrange("p (e t) -> p e t", e=EXPERTS) for q in quarters[3:5]]
        routed_hid = quarters[5].rearrange("p (i f) -> p i f", i=2)
        gated_hid = scratch[:, 0:4096].rearrange("p (i f) -> p i f", i=2)
        with ExitStack() as own:
            def setup_sb(name, *shape):
                return own.enter_context(nc.sbuf_tensor("setup_" + name, list(shape), F32))

            setup, once = {e: [] for e in ENGINES}, []
            w = new_thread(nc, own, "setup", setup, once)
            banks = [own.enter_context(nc.psum_tensor(f"setup_bank{i}", [P, 512], F32)) for i in range(8)]
            raw = setup_sb("weights", P, p_total)
            temp = {"small": setup_sb("small", P, 64), "first": setup_sb("first", P, P), "valT": setup_sb("valT", P, LT)}
            temp.update({n: setup_sb(n, P, I_FF) for n in ("mag", "sign", "level")})
            loaded = new_signal(nc, own, "weights_loaded", once)
            for out, in_ in [(weights[:, :], dram["weights"]), (consts[:, :], dram["consts"]),
                             (raw[:, :], dram["prepared"]),
                             (rows[:, :], dram["rows"].to_broadcast([P, rows_total])),
                             (s["x2_mask_int"][:, :], dram["x2_mask"])]:
                m = transfer(w.dma, loaded, [], move(out, in_))
            for layer in ("L0", "L3"):
                for out, name in ((s[layer + "_w1"][:, :, :].rearrange("p e f -> p (e f)"), "_w1"),
                                  (s[layer + "_w2"][:, :, :, :].rearrange("p e c d -> p (e c d)"), "_w2")):
                    experts = transfer(w.dma, experts_loaded, [], move(out, dram[layer + name]))
            w.pool([], fill(s["minus_half"], -0.5))
            prepare(w, s, Weights(raw, p_off), [m], banks, temp)
            with nc.Block() as block:
                block.sync(lambda e: play(setup["sync"], e))
                block.tensor(lambda e: play(setup["tensor"], e))
                block.scalar(lambda e: play(setup["scalar"], e))
                block.vector(lambda e: play(setup["vector"], e))
                block.gpsimd(lambda e: play(setup["gpsimd"], e))

        lanes = [new_lane(nc, ctx, n, queues, signals, s) for n in range(LANES)]
        banks = [ln.a for ln in lanes] + [ln.b for ln in lanes]
        both = new_thread(nc, ctx, "lanes", queues, signals)

        store = new_signal(nc, ctx, "out_stored", signals)
        s_arrived = transfer(both.dma, new_signal(nc, ctx, "s_arrived", signals), [], lambda e, step: e.dma_start(
            s["kq"][:, :], dram["s"][:, bass.ds(step * LANES, LANES)]))
        for ln in lanes:
            arrived = new_signal(nc, ctx, f"lane{ln.n}_arrived", signals)

            def load(out, src, ln=ln, arrived=arrived):
                return transfer(ln.dma, arrived, [], lambda e, step: e.dma_start(out, src(step * LANES + ln.n)))

            load(ln.x[:, :], lambda b: dram["x"][bass.ds(b, 1)].rearrange("a t d -> (a t) d"))
            load(ln.xT, lambda b: dram["xT"][:, bass.ds(b * T, T)])
            load(ln.zT[:, :], lambda b: dram["z"][:, bass.ds(b * T, T)])
            load(ln.ctxT[:, :], lambda b: dram["ctxT"][:, bass.ds(b * S2, S2)])
            load(ln.ctx_in[:, :], lambda b: dram["ctx"][bass.ds(b, 1)].rearrange("a t d -> (a t) d"))
            ln.arrived = load(ln.key_mask_int[:, :], lambda b: dram["key_mask"][bass.ds(b, 1), :].to_broadcast([P, S2]))

        def first_part(ln, s_arrived=s_arrived):
            ready = yield from recurrent_attention(ln, ln.arrived, s_arrived)
            ready = yield from context_attention(ln, [ready], "x0", float(HD) ** -0.5, raw_values=True)
            probs = yield from route(ln, [ready])
            return [ready], probs

        def second_part(ln, mixed):
            mask = ln.pool([ln.arrived], ts(ln.key_mask[:, :], ln.key_mask_int[:, :], 0.0, ALU.is_gt, MASKED, ALU.mult))
            ready = yield from finish(ln, ln.a[:, 0:D], [mixed], plain=True)
            ready = yield from latent_attention(ln, [ready])
            ready = yield from context_attention(ln, [ready, mask], "x1", float(HD) ** -0.5,
                                                 bias=ln.key_mask[:, :], out=False)
            ready = yield from fp4_feed_forward(ln, [ready])
            ready = yield from self_attention_shared_values(ln, [ready])
            ready = yield from context_attention(ln, [ready], "x2", float(HD) ** -0.5, bias=s["x2_mask"][:, :])
            ready = yield from low_rank_feed_forward(ln, [ready])
            ready = yield from rotary_attention(ln, [ready])
            ready = yield from relu_attention(ln, [ready])
            return (yield from conv_and_attention(ln, [ready]))

        marks = alternate(first_part(ln) for ln in lanes)
        s["hid"] = routed_hid
        mixed = routed_mixture(both, lanes, s, banks, [x for x, _ in marks], [p for _, p in marks])
        marks = alternate(second_part(ln, mixed[ln.n]) for ln in lanes)
        s["hid"] = gated_hid
        mixed = gated_mixture(both, lanes, s, banks, [x for x, _ in marks], [acc for _, acc in marks])
        ended = alternate(end_of_mixture(ln, mixed[ln.n]) for ln in lanes)
        for ln in lanes:
            transfer(ln.dma, store, [ended[ln.n]], lambda e, step, ln=ln: e.dma_start(
                dram["out"][bass.ds(step * LANES + ln.n, 1)].rearrange("a t d -> (a t) d"), ln.x[:, :]))

        met = ctx.enter_context(nc.semaphore("engines_met"))
        go = {e: ctx.enter_context(nc.semaphore(f"{e}_goes_on")) for e in ENGINES[:4]}
        counted = [sig for sig in signals if sig.count]

        ones_set = ctx.enter_context(nc.semaphore("value_columns_set"))

        def run(name, eng):
            if name == "gpsimd":
                for n, ln in enumerate(lanes):
                    eng.memset(ln.v[:, :, :], 0.0).then_inc(ones_set, 1)
                    eng.wait_ge(ones_set, 2 * n + 1)
                    eng.memset(ln.v[:, :, HD:HD + 1], 1.0).then_inc(ones_set, 1)
            else:
                eng.wait_ge(ones_set, 2 * LANES)
            if name == "tensor":
                eng.wait_ge(experts_loaded.sem, experts_loaded.count)
            with eng.Fori(0, nb // LANES) as step:
                play(queues[name], eng)
                for thread in lanes + [both]:
                    sig = {"tensor": thread.pe, "scalar": thread.act, "vector": thread.dve,
                           "gpsimd": thread.pool}[name].done
                    if sig.count:
                        eng.wait_ge(sig.sem, sig.count)
                eng.sem_inc(met, 1)
                eng.wait_ge(go[name], 1)
                eng.sem_clear(go[name])

        with nc.Block() as block:
            @block.sync
            def _(e):
                with e.Fori(0, nb // LANES) as step:
                    play(queues["sync"], e, step)
                    e.wait_ge(store.sem, store.count)
                    e.wait_ge(met, 4)
                    e.sem_clear(met)
                    for sig in counted:
                        e.sem_clear(sig.sem)
                    for name in ENGINES[:4]:
                        e.sem_inc(go[name], 1)

            block.tensor(lambda e: run("tensor", e))
            block.scalar(lambda e: run("scalar", e))
            block.vector(lambda e: run("vector", e))
            block.gpsimd(lambda e: run("gpsimd", e))


def offsets(widths):
    found, at = {}, 0
    for name, n in widths:
        found[name] = (at, n)
        at += n
    return found, at


def build(nc, dram, nb, w_widths, p_widths, r_widths, c_widths):
    w_off, w_total = offsets(w_widths)
    p_off, p_total = offsets(p_widths)
    r_off, r_total = offsets(r_widths)
    c_off, c_total = offsets(c_widths)
    memory_phase(nc, dram, nb, w_off, w_total, r_off, r_total, c_off)
    decoder_phase(nc, dram, nb, w_off, w_total, p_off, p_total, r_off, r_total, c_off, c_total)


def lay_out(inputs):
    w = {name: np.asarray(a) for name, a in inputs.items()}
    nb = w["x"].shape[0]
    mats, rows, consts = weight_layouts(w), row_layouts(w), constants()
    prepared = {name: mats.pop(name) for name in PREPARED}

    def padded(a):
        a = np.asarray(a)
        return np.pad(a, ((0, P - a.shape[0]), (0, 0)))

    arrays = {
        "weights": np.concatenate([padded(a) for a in mats.values()], axis=1),
        "prepared": np.concatenate([padded(a) for a in prepared.values()], axis=1),
        "rows": np.concatenate(list(rows.values())).reshape(1, -1),
        "consts": np.concatenate(list(consts.values()), axis=1).astype(np.float32),
        "x": w["x"],
        "xT": w["x"].transpose(2, 0, 1).reshape(P, nb * T),
        "ctx": w["ctx_1024"],
        "ctxT": w["ctx_1024"].transpose(2, 0, 1).reshape(P, nb * S2),
        "key_mask": w["mask_BxS2_ik0"],
        "x2_mask": w["mask_1x1xSxS2_ik0"][0, 0],
    }
    arrays.update(expert_layouts(w))
    arrays = {name: np.ascontiguousarray(a) for name, a in arrays.items()}
    widths = [[(name, a.shape[-1]) for name, a in group.items()] for group in (mats, prepared, rows, consts)]
    return arrays, widths, nb


def kernel(**inputs):
    import concourse.bacc as bacc
    from concourse.bass_utils import run_bass_kernel_spmd

    arrays, widths, nb = lay_out(inputs)
    nc = bacc.Bacc("TRN2", target_bir_lowering=False, num_devices=1)
    dram = {name: nc.dram_tensor(name + "_in", a.shape, mybir.dt.from_np(a.dtype), kind="ExternalInput").ap()
            for name, a in arrays.items()}
    dram["out"] = nc.dram_tensor("out", (nb, T, D), F32, kind="ExternalOutput").ap()
    dram.update(scratch_tensors(nc, nb))
    build(nc, dram, nb, *widths)
    result = run_bass_kernel_spmd(nc, [{name + "_in": a for name, a in arrays.items()}], core_ids=[0])
    return result.results[0]["out"]


def scratch_tensors(nc, nb):
    shapes = {"g": (nb, BLK, BLK), "xx": (nb, BLK, 2 * BLK), "z": (P, nb * T), "s": (P, nb)}
    return {name: nc.dram_tensor(name + "_scratch", shape, F32, kind="Internal").ap() for name, shape in shapes.items()}
```

```python
from contextlib import ExitStack

import numpy as np

import concourse.bass as bass
from concourse import mybir

F32 = mybir.dt.float32
I32 = mybir.dt.int32
ALU = mybir.AluOpType
ACT = mybir.ActivationFunctionType
AX = mybir.AxisListType.X

P = 128
T = 128
D = 128
S2 = 77
HEADS = 16
HD = D // HEADS
HQ = 4
QUADS = HEADS // HQ
VW = 32
EXPERTS = 8
DFF = 512
HC = DFF // P
CAP = 2 * T // EXPERTS
LAT = 32
KV = 2
I_FF = 352
FP4_BLOCK = 16
E6, LT = 6, 100
LANES = 4
BLK = 32
NBLK = T // BLK
EPS = 1e-5
KEY_EPS = 1e-6
MASKED = -1e30


def constants():
    p = np.arange(P)
    f = np.arange(T)
    inv = 1.0 / 10000.0 ** (np.arange(0, HD, 2, dtype=np.float32) / np.float32(HD))
    ang = np.outer(f.astype(np.float32), inv.astype(np.float32)).astype(np.float32)
    half = HD // 2
    cos = np.cos(ang)[:, p % half].T
    sin = np.sin(ang)[:, p % half].T * np.where(p % HD < half, -1.0, 1.0)[:, None]
    return {
        "ident": np.eye(P),
        "quad_mask": (p[:, None] % 32 // HD == np.arange(HQ)[None, :]) * 1.0,
        "group_mask": (p[:, None] // 32 == np.arange(4)[None, :]) * 1.0,
        "upto": (p[:, None] <= f[None, :]) * 1.0,
        "causal": np.where(f[None, :] <= p[:, None], 0.0, MASKED),
        "slots": np.broadcast_to(np.arange(1, CAP + 1), (P, CAP)),
        "falling": np.broadcast_to(np.arange(E6, 0, -1), (P, E6)),
        "ones": np.ones((P, 32)),
        "rope": np.concatenate([cos, sin], axis=1),
    }


def rows_first(a):
    n = a.shape[0] // P
    return a.reshape(n, P, a.shape[1]).transpose(1, 0, 2).reshape(P, -1)


def column(a):
    return a.reshape(-1, 1)


def rope_order(second):
    first = [0, 2, 4, 6, 1, 3, 5, 7]
    order = first[4:] + first[:4] if second else first
    return [h * HD + r for h in range(HEADS) for r in order]


def weight_layouts(w):
    out = {}
    a = "L0_attn_"
    out["rec_qkT"] = np.concatenate([w[a + "Wq"].T, w[a + "Wk"].T], axis=1)
    out["rec_v"] = w[a + "Wv"].T
    out["rec_o"] = w[a + "Wo"].T
    out["rec_bq"] = column(w[a + "bq"])
    a = "L0_xattn_"
    out["x0_q"], out["x0_k"], out["x0_o"] = w[a + "Wq"].T, w[a + "Wk"].T, w[a + "Wc"].T
    out["x0_bq"], out["x0_bk"] = column(w[a + "bq"]), column(w[a + "bk"])
    out["f0_gate"] = w["L0_ffn_gate_w"]
    a = "L1_attn_"
    out["a1_qT"] = rows_first(w[a + "wq"].T)
    out["a1_kdown"], out["a1_vdown"] = w[a + "wk_down"], w[a + "wv_down"]
    out["a1_kupT"], out["a1_vupT"] = w[a + "wk_up"].T, w[a + "wv_up"].T
    out["a1_o"] = rows_first(w[a + "wo"])
    a = "L1_xattn_"
    out["x1_q"], out["x1_k"], out["x1_v"] = w[a + "q_w"].T, w[a + "k_w"].T, w[a + "v_w"].T
    out["x1_bq"], out["x1_bk"] = column(w[a + "q_b"]), column(w[a + "k_b"])
    a = "L1_ffn_"
    out["f1_gate"] = np.concatenate([w[a + "w_gate"][0:128], w[a + "w_gate"][128:256]], axis=1)
    out["f1_up"] = np.concatenate([w[a + "w_up"][0:128], w[a + "w_up"][128:256]], axis=1)
    out["f1_gate_rest"], out["f1_up_rest"] = w[a + "w_gate"][256:352], w[a + "w_up"][256:352]
    out["f1_down"] = w[a + "w_down"]
    a = "L2_attn_"
    out["a2_q"], out["a2_k"] = w[a + "Wq"], w[a + "Wk"]
    out["a2_bq"], out["a2_bk"] = column(w[a + "bq"]), column(w[a + "bk"])
    a = "L2_xattn_"
    out["x2_q"], out["x2_k"] = w[a + "Wq"], w[a + "Wk"]
    out["x2_v"], out["x2_o"] = w[a + "Wv"], w[a + "Wo"]
    out["x2_bq"], out["x2_bk"] = column(w[a + "bq"]), column(w[a + "bk"])
    a = "L2_ffn_"
    out["f2_A"] = w[a + "A"].transpose(2, 0, 1).reshape(16, E6 * LT)
    out["f2_B"] = w[a + "B"].transpose(1, 0, 2).reshape(16, E6 * D)
    out["f2_gate"], out["f2_wtT"], out["f2_wdT"] = w[a + "w_gate"], w[a + "wt_w"].T, w[a + "wd_w"].T
    out["f2_bt"] = column(w[a + "wt_b"])
    a = "L3_attn_"
    q, k, v = w[a + "w_qkv"][0:128], w[a + "w_qkv"][128:256], w[a + "w_qkv"][256:384]
    out["a3_qk"] = np.concatenate([q[rope_order(0)].T, q[rope_order(1)].T,
                                   k[rope_order(0)].T, k[rope_order(1)].T], axis=1)
    out["a3_v"], out["a3_o"] = v.T, w[a + "w_out"].T
    a = "L3_xattn_"
    for n in "qkv":
        out["x3_" + n] = w[a + "kernel_" + n][0, 0]
    out["x3_bq"], out["x3_bk"] = column(w[a + "bias_q"]), column(w[a + "bias_k"])
    out["x3_maskT"] = w["mask_1xSxS2_ff0"][0].T
    a = "L3_ffn_"
    out["f3_conv"] = w[a + "conv_w"].transpose(1, 2, 0).reshape(P, 3 * D)
    qkv = w[a + "wqkv"]
    out["f3_q"], out["f3_k"], out["f3_v"] = qkv[0:128].T, qkv[128:256].T, qkv[256:384].T
    out["f3_bq"], out["f3_bk"] = column(w[a + "bqkv"][0:128]), column(w[a + "bqkv"][128:256])
    out["f3_o"], out["f3_gate"] = w[a + "wo"].T, w[a + "gate_w"]
    out["f3_b1"] = w[a + "b1"].reshape(EXPERTS, HC, P).transpose(2, 0, 1).reshape(P, -1)
    out["f3_b2"] = w[a + "b2"]
    return out


def expert_layouts(w):
    out = {}
    for layer in ("L0", "L3"):
        w1, w2 = w[layer + "_ffn_w1"], w[layer + "_ffn_w2"]
        out[layer + "_w1"] = w1.transpose(1, 0, 2).reshape(P, EXPERTS * DFF)
        out[layer + "_w2"] = w2.reshape(EXPERTS, HC, P, D).transpose(2, 0, 1, 3).reshape(P, EXPERTS * DFF)
    return out


def row_layouts(w):
    out = {
        "rec_bqk": np.concatenate([w["L0_attn_bq"], w["L0_attn_bk"]]),
        "rec_bv": w["L0_attn_bv"], "rec_bo": w["L0_attn_bo"], "x0_bo": w["L0_xattn_bc"],
        "x1_bv": w["L1_xattn_v_b"], "a2_bv": w["L2_attn_bk"],
        "x2_bv": w["L2_xattn_bv"], "x2_bo": w["L2_xattn_bo"],
        "f2_bd": w["L2_ffn_wd_b"], "f2_scale": w["L2_ffn_scale"], "a3_bo": w["L3_attn_b_out"],
        "x3_bv": w["L3_xattn_bias_v"], "f3_bconv": w["L3_ffn_conv_b"],
        "f3_bv": w["L3_ffn_bqkv"][256:384], "f3_bo": w["L3_ffn_bo"],
        "f3_g1": w["L3_ffn_ln1_g"], "f3_n1": w["L3_ffn_ln1_b"], "f3_bgate": w["L3_ffn_gate_b"],
        "f3_g2": w["L3_ffn_ln2_g"], "f3_n2": w["L3_ffn_ln2_b"],
    }
    return out


PREPARED = ("a1_qT", "a1_kdown", "a1_kupT", "a1_vupT", "a1_o", "f1_gate", "f1_up", "f1_gate_rest",
            "f1_up_rest", "f1_down", "f2_A", "f2_B", "f2_wtT", "f2_wdT", "f2_bt")
"""Matrices that only the preparation reads, before the loop."""


class Signal:

    def __init__(self, sem):
        self.sem, self.count = sem, 0


class Steps:

    def __init__(self, thread, engine, done):
        self.thread, self.engine, self.done, self.noted = thread, engine, done, []

    def __call__(self, waits, work):
        self.done.count += 1
        emit, ns = work
        mark = (self.done, self.done.count)
        self.noted.append((waits, emit, mark, 1, ns))
        return mark


def interleave(threads, queues):
    rest = [steps for t in threads for steps in (t.pe, t.act, t.dve, t.pool, t.dma)]
    open_marks = {mark for steps in rest for _, _, mark, _, _ in steps.noted}
    left = {}
    for steps in rest:
        left[steps.thread] = left.get(steps.thread, 0) + sum(one[4] for one in steps.noted)
    for i, t in enumerate(left):
        left[t] -= LAG_NS * i
    free, ends = {e: 0 for e in ENGINES}, {}
    while open_marks:
        best = None
        for steps in rest:
            if steps.noted and not any(mark in open_marks for mark in steps.noted[0][0]):
                start = max([free[steps.engine]] + [ends[mark] for mark in steps.noted[0][0]])
                key = (start, -left[steps.thread])
                if best is None or key < best[0]:
                    best = key, steps, start
        _, steps, start = best
        waits, emit, mark, by, ns = steps.noted.pop(0)
        free[steps.engine] = start + ns
        left[steps.thread] -= ns
        ends[mark] = start + ns + (HOP_NS if by == 1 else DMA_NS)
        open_marks.remove(mark)
        queues[steps.engine].append((waits, emit, mark[0], by))


def transfer(steps, signal, waits, emit):
    signal.count += 16
    mark = (signal, signal.count)
    steps.noted.append((waits, emit, mark, 16, 50))
    return mark


def play(queue, eng, turn=None):
    for waits, emit, signal, by in queue:
        for s, count in waits:
            eng.wait_ge(s.sem, count)
        (emit(eng, turn) if by == 16 else emit(eng)).then_inc(signal.sem, by)


ENGINES = ("tensor", "scalar", "vector", "gpsimd", "sync")


def new_signal(nc, ctx, name, signals):
    signals.append(Signal(ctx.enter_context(nc.semaphore(name))))
    return signals[-1]


class Thread:
    pass


def new_thread(nc, ctx, name, signals):
    parts = {short: Steps(name, e, new_signal(nc, ctx, f"{name}_{e}_done", signals))
             for short, e in (("pe", "tensor"), ("act", "scalar"), ("dve", "vector"), ("pool", "gpsimd"))}
    thread = Thread()
    thread.dma = Steps(name, "sync", None)
    thread.pe, thread.act, thread.dve, thread.pool = parts["pe"], parts["act"], parts["dve"], parts["pool"]
    return thread


HOP_NS = 250
DMA_NS = 2500
LAG_NS = 5000


def row_ns(out):
    return 70 + int(np.prod(list(out.shape)[1:]))


def matmul_ns(out):
    columns = int(np.prod(list(out.shape)[1:]))
    return max(64, 2.2 * columns) * (0.3 if out.shape[0] == 32 else 1)


def products(*each):
    def emit(e):
        for out, lhsT, rhs, first, last in each:
            ins = e.matmul(out, lhsT, rhs, start=first, stop=last)
        return ins
    return emit, sum(matmul_ns(one[0]) for one in each)


def product(out, lhsT, rhs):
    return products((out, lhsT, rhs, True, True))


def transposes(ident, *each):
    def emit(e):
        for out, in_ in each:
            ins = e.transpose(out, in_, ident[0:in_.shape[0], 0:in_.shape[0]])
        return ins
    return emit, sum(150 for _ in each)


def over(ap, axis, n):
    ap = ap.unsqueeze(axis)
    shape = list(ap.shape)
    shape[axis] = n
    return ap.to_broadcast(shape)


def tt(out, a, b, op):
    return lambda e: e.tensor_tensor(out, a, b, op), row_ns(out)


def copy(out, in_):
    return lambda e: e.tensor_copy(out, in_), row_ns(out)


def recip(out, in_):
    return lambda e: e.reciprocal(out, in_), row_ns(out)


def reduce_to(out, in_, op, magnitude=False):
    return lambda e: e.tensor_reduce(out, in_, AX, op, apply_absolute_value=magnitude), row_ns(in_)


def ts(out, in_, s1, op0, s2=None, op1=ALU.bypass):
    return lambda e: e.tensor_scalar(out, in_, s1, s2, op0, op1), row_ns(out)


def stt(out, a, s, op0, b, op1):
    return lambda e: e.scalar_tensor_tensor(out=out, in0=a, scalar=s, in1=b, op0=op0, op1=op1), row_ns(out)


def fill(out, value):
    return lambda e: e.memset(out, value), row_ns(out)


def move(out, in_):
    return lambda e, i: e.dma_start(out, in_)


def activate(out, in_, func, **more):
    return lambda e: e.activation(out, in_, func, **more), 100 + row_ns(out)


def act_copy(out, in_):
    return activate(out, in_, ACT.Copy)


def act_bias(out, in_, bias):
    return activate(out, in_, ACT.Identity, bias=bias)


def memory_phase(nc, dram, nb, w_off, w_total, rows_off, rows_total, c_off):
    nq = nb // 4
    queues, signals = {e: [] for e in ENGINES}, []
    with ExitStack() as ctx:
        def sb(name, shape):
            return ctx.enter_context(nc.sbuf_tensor("m_" + name, shape, F32))

        w = new_thread(nc, ctx, "m", signals)
        bank = [ctx.enter_context(nc.psum_tensor(f"m_bank{i}", [P, 512], F32)) for i in range(8)]
        loaded = new_signal(nc, ctx, "m_weights_loaded", signals)
        x_loaded = [new_signal(nc, ctx, f"m_x_loaded{i}", signals) for i in range(2)]
        moved = new_signal(nc, ctx, "m_moved", signals)
        results = new_signal(nc, ctx, "m_results_stored", signals)
        ident = sb("ident", [P, P])
        qkw = sb("qkw", [P, 2 * D])
        qkb = sb("qkb", [P, 2 * D])
        xT = [sb(f"xT{i}", [P, 4, T]) for i in range(2)]
        qk = [sb(f"qk{i}", [P, 4, 2 * D]) for i in range(2)]
        tmp = sb("tmp", [P, 4, D])
        u = [sb(f"u{i}", [P, 4, D]) for i in range(2)]
        s_all = sb("s_all", [P, nb])
        norm = sb("norm", [P, nb])
        half = sb("half", [P, 4])
        uT = sb("uT", [P, nb, T])
        A = sb("A", [P, nb, D])
        yT = [sb(f"yT{i}", [P, 4, BLK]) for i in range(2)]
        y = sb("y", [P, nq, D])
        g = sb("g", [P, nq, BLK])
        E = sb("E", [nb, BLK, 2 * BLK])
        outer = sb("outer", [nb, BLK, BLK])
        col = sb("col", [nb, BLK])
        rd = sb("rd", [nb, BLK])
        xx = sb("xx", [nb, BLK, 2 * BLK])
        xs = sb("xs", [P, nq, 2, P])
        W = [sb(f"w{i}", [P, D]) for i in range(2)]
        Z = [sb(f"z{i}", [P, 4, D]) for i in range(2)]
        group_mask = sb("group_mask", [P, 4])

        def wslice(name):
            a, n = w_off[name]
            return dram["weights"][:, a:a + n]

        a, n = c_off["ident"]
        ld = transfer(w.dma, loaded, [], move(ident[:, :], dram["consts"][:, a:a + n]))
        ld = transfer(w.dma, loaded, [], move(qkw[:, :], wslice("rec_qkT")))
        a, n = c_off["group_mask"]
        ld = transfer(w.dma, loaded, [], move(group_mask[:, :], dram["consts"][:, a:a + n]))
        xs_zero = w.pool([], fill(xs[:, :, :, :], 0.0))
        ra, rn = rows_off["rec_bqk"]
        ld = transfer(w.dma, loaded, [], move(
            qkb[:, :], dram["rows"][0:1, ra:ra + rn].to_broadcast([P, rn])))
        half_set = w.pool([], fill(half[:, :], 0.5))
        A_set = {}
        for q in range(nq):
            A_set[q] = w.pool([ld], copy(A[:, 4 * q:4 * q + 4, :], over(ident[:, :], 1, 4)))

        x_read = [[], []]
        u_read = [[], []]
        uT_ready = {}
        tmp_read, turned_read = [], [[], []]
        for q in range(nq):
            i = q % 2
            xl = transfer(w.dma, x_loaded[i], x_read[i], move(
                xT[i][:, :, :], dram["xT"][:, 4 * q * T:4 * (q + 1) * T].rearrange("p (b t) -> p b t", b=4)))
            b0 = bank[2 * i], bank[2 * i + 1]
            projected = w.pe([ld, xl], products(*[
                (b0[b // 2][:, (b % 2) * 256:(b % 2) * 256 + 256], xT[i][:, b, :], qkw[:, :], True, True)
                for b in range(4)]))
            x_read[i] = [projected]
            for h in range(2):
                biased = w.dve([projected], tt(qk[i][:, 2 * h:2 * h + 2, :],
                               b0[h][:, :].rearrange("p (b c) -> p b c", b=2), over(qkb[:, :], 1, 2), ALU.add))
            kk, qq = qk[i][:, :, D:2 * D], qk[i][:, :, 0:D]
            r = slice(4 * q, 4 * q + 4)
            m = w.dve([biased] + tmp_read, tt(tmp[:, :, :], kk, qq, ALU.mult))
            m = s_ready = w.dve([m], reduce_to(s_all[:, r], tmp[:, :, :], ALU.add))
            m = w.dve([m], tt(tmp[:, :, :], kk, kk, ALU.mult))
            m = w.dve([m], reduce_to(norm[:, r], tmp[:, :, :], ALU.add))
            tmp_read = [m]
            m = w.pool([m, half_set], tt(norm[:, r], norm[:, r], half[:, :], ALU.pow))
            m = w.dve([m], ts(norm[:, r], norm[:, r], KEY_EPS, ALU.add))
            m = w.dve([m], recip(norm[:, r], norm[:, r]))
            m = w.dve([m] + u_read[i], tt(u[i][:, :, :], kk, over(norm[:, r], 2, D), ALU.mult))
            turned = w.pe([m] + turned_read[i], transposes(ident, *[
                (bank[4 + i][:, b * T:(b + 1) * T], u[i][:, b, :]) for b in range(4)]))
            u_read[i] = [turned]
            uT_ready[q] = w.act([turned], act_copy(uT[:, r, :], bank[4 + i][:, :].rearrange("p (b t) -> p b t", b=4)))
            turned_read[i] = [uT_ready[q]]

        z_ready = {q: [] for q in range(nq)}
        E_flat = E[:, :, :].rearrange("b r c -> b (r c)")
        step_of = 2 * BLK + 1
        diag = E_flat[:, 0:BLK * 2 * BLK:step_of]
        inv_diag = E_flat[:, BLK:BLK * 2 * BLK:step_of]
        y_read, xs_read, last_moved, yT_read, w_read, Yb_read, Tb_read = [], [], [], [[], []], [[], []], [[], []], [[], []]
        for blk in range(NBLK):
            cols = slice(blk * BLK, (blk + 1) * BLK)
            g_done = []
            for q in range(nq):
                i = q % 2
                Yb, Tb, Gb = bank[i], bank[2 + i], bank[4 + i]
                m = w.pe([uT_ready[q], A_set[q]] + Yb_read[i], products(*[
                    (Yb[32 * j:32 * j + 32, 0:D], uT[:, 4 * q + j, cols], A[:, 4 * q + j, :], True, True)
                    for j in range(4)] + [
                    (Tb[:, 32 * j:32 * j + 32], A[:, 4 * q + j, :], uT[:, 4 * q + j, cols], True, True)
                    for j in range(4)]))
                y_sb = w.act([m] + y_read, act_copy(y[:, q, :], Yb[:, 0:D]))
                Yb_read[i] = [y_sb]
                yT_sb = w.dve([m] + yT_read[i], copy(yT[i][:, :, :], Tb[:, 0:P].rearrange("p (j r) -> p j r", j=4)))
                m = w.pe([yT_sb] + turned_read[i], products(*[
                    (Gb[32 * j:32 * j + 32, 0:BLK], yT[i][:, j, :], uT[:, 4 * q + j, cols], True, True)
                    for j in range(4)]))
                yT_read[i] = [m]
                g_sb = w.dve([m] + last_moved, copy(g[:, q, :], Gb[:, 0:BLK]))
                g_done = [g_sb, y_sb]
            m = transfer(w.dma, moved, g_done, move(
                dram["g"].rearrange("(q j) r c -> (j r) q c", j=4), g[:, :, :]))
            cleared = w.dve([], fill(E[:, :, BLK:2 * BLK], 0.0))
            cleared = w.dve([cleared], fill(inv_diag, 1.0))
            m = transfer(w.dma, moved, [m, cleared], move(E[:, :, 0:BLK], dram["g"]))
            m = w.dve([m], ts(diag, diag, 1.0, ALU.add))
            for j in range(BLK - 1):
                n = BLK - 1 - j
                win = slice(j + 1, j + 1 + BLK)
                m = w.dve([m], recip(rd[:, 0:1], E[:, j, j:j + 1]))
                m = w.dve([m], ts(col[:, 0:n], E[:, j + 1:, j], rd[:, 0:1], ALU.mult))
                m = w.dve([m], tt(outer[:, 0:n, :], over(col[:, 0:n], 2, BLK), over(E[:, j, win], 1, n), ALU.mult))
                m = w.dve([m], tt(E[:, j + 1:, win], E[:, j + 1:, win], outer[:, 0:n, :], ALU.subtract))
            m = w.dve([m], recip(rd[:, :], diag))
            inv_T = E[:, :, BLK:2 * BLK].rearrange("b r k -> b k r")
            w.dve(last_moved, copy(xx[:, :, 0:BLK], inv_T))
            m = w.dve([m], tt(xx[:, :, BLK:2 * BLK], inv_T, over(rd[:, :], 1, BLK), ALU.mult))
            m = transfer(w.dma, moved, [m], move(dram["xx"], xx[:, :, :]))
            for j in range(4):
                for k in range(2):
                    last = transfer(w.dma, moved, [m, xs_zero] + xs_read, move(
                        xs[32 * j:32 * j + 32, :, k, 32 * j:32 * j + 32],
                        dram["xx"].rearrange("(q j) k (a m) -> j a k q m", j=4, a=2)[j, k]))
            m = last
            last_moved = [m]
            for q in range(nq):
                i = q % 2
                Wb, Zb, Tb, Ab = bank[i], bank[2 + i], bank[4 + i], bank[6 + i]
                m2 = w.pe([m, y_sb] + Tb_read[i], products(
                    (Wb[:, 0:D], xs[:, q, 0, :], y[:, q, :], True, True),
                    (Zb[:, 0:D], xs[:, q, 1, :], y[:, q, :], True, True),
                    (Tb[:, 0:P], y[:, q, :], xs[:, q, 1, :], True, True)))
                z_ready[q] = w.act([m2], act_copy(uT[:, 4 * q:4 * q + 4, cols],
                                   Tb[:, 0:P].rearrange("p (j r) -> p j r", j=4)))
                Tb_read[i] = [z_ready[q]]
                y_read = xs_read = [m2]
                if blk < NBLK - 1:
                    w_sb = w.act([m2] + w_read[i], act_copy(W[i][:, :], Wb[:, 0:D]))
                    z_sb = w.dve([m2] + w_read[i], tt(Z[i][:, :, :], over(Zb[:, 0:D], 1, 4),
                                 over(group_mask[:, :], 2, D), ALU.mult))
                    m3 = w.pe([w_sb, z_sb], product(Ab[:, :], W[i][:, :], Z[i][:, :, :]))
                    w_read[i] = [m3]
                    A_set[q] = w.dve([m3], tt(A[:, 4 * q:4 * q + 4, :], A[:, 4 * q:4 * q + 4, :],
                                       Ab[:, :].rearrange("p (j d) -> p j d", j=4), ALU.subtract))

        transfer(w.dma, results, [s_ready], move(dram["s"], s_all[:, :]))
        transfer(w.dma, results, [z_ready[nq - 1]], move(
            dram["z"].rearrange("p (b t) -> p b t", b=nb), uT[:, :, :]))

        interleave([w], queues)
        with nc.Block() as block:
            block.tensor(lambda e: play(queues["tensor"], e))
            block.scalar(lambda e: play(queues["scalar"], e))
            block.vector(lambda e: play(queues["vector"], e))
            block.gpsimd(lambda e: play(queues["gpsimd"], e))

            @block.sync
            def _(e):
                play(queues["sync"], e)
                e.wait_ge(results.sem, results.count)


class Weights:

    def __init__(self, tensor, offsets):
        self.tensor, self.offsets = tensor, offsets

    def __getitem__(self, name):
        a, n = self.offsets[name]
        return self.tensor[:, a:a + n]

    def part(self, name, k, n=D):
        a, _ = self.offsets[name]
        return self.tensor[:, a + k * n:a + (k + 1) * n]


def new_lane(nc, ctx, n, signals, shared):
    ln = new_thread(nc, ctx, f"lane{n}", signals)
    ln.n = n
    ln.w, ln.r, ln.k, ln.s = shared["w"], shared["r"], shared["k"], shared

    def sb(name, *shape):
        return ctx.enter_context(nc.sbuf_tensor(f"lane{n}_{name}", list(shape), F32))

    ln.a = ctx.enter_context(nc.psum_tensor(f"lane{n}_a", [P, 512], F32))
    ln.b = ctx.enter_context(nc.psum_tensor(f"lane{n}_b", [P, 512], F32))
    ln.x = sb("x", P, D)
    ln.xT = shared["xT_all"][:, n, :]
    ln.base = sb("base", P, D)
    ln.ctxT, ln.ctx_in = sb("ctxT", P, S2), sb("ctx", S2, D)
    ln.zT, ln.kq_dot = sb("zT", P, T), shared["kq"][:, n:n + 1]
    ln.key_mask_int = ctx.enter_context(nc.sbuf_tensor(f"lane{n}_mask_int", [P, S2], I32))
    ln.key_mask = sb("mask", P, S2)
    ln.qT = sb("qT", P, T)
    ln.kq = sb("kq", P, HQ, T)
    ln.v = sb("v", P, HEADS, VW)
    ln.sc = sb("sc", P, HQ, T)
    ln.p = sb("p", P, HQ, T)
    ln.oT = sb("oT", P, QUADS, T)
    ln.o = sb("o", P, D)
    ln.wide = sb("wide", P, 600)
    ln.small = sb("small", P, 64)
    ln.mean_var = sb("mean_var", P, 2)
    ln.stats = sb("stats", P, 6)
    ln.gates = sb("gates", P, EXPERTS)
    ln.hid = shared["gated_hid"][:, n, :, :, :]
    ln.out_stored = new_signal(nc, ctx, f"lane{n}_out_stored", signals)
    ln.arrived = {name: new_signal(nc, ctx, f"lane{n}_{name}_arrived", signals) for name in ("x", "ctx", "mask")}
    return ln


def add_bias_to_x(ln, row, ready):
    return ln.pool(ready, tt(ln.base[:, :], ln.x[:, :], ln.r[row], ALU.add))


def normalize(ln, src, dst, ready, gain=None, shift=None):
    m = ln.dve(ready, (lambda e: e.bn_stats(ln.stats[:, :], src), row_ns(src)))
    m = ln.dve([m], (lambda e: e.bn_aggr(ln.mean_var[:, :], ln.stats[:, :]), 70))
    rstd = ln.small[:, 60:61]
    m = ln.dve([m], ts(rstd, ln.mean_var[:, 1:2], EPS, ALU.add))
    m = ln.pool([m], tt(rstd, rstd, ln.s["minus_half"], ALU.pow))
    m = ln.dve([m], ts(dst, src, ln.mean_var[:, 0:1], ALU.subtract, rstd, ALU.mult))
    if gain is not None:
        m = ln.dve([m], tt(dst, dst, ln.r[gain], ALU.mult))
        m = ln.dve([m], tt(dst, dst, ln.r[shift], ALU.add))
    return m


def finish(ln, y, ready, plain=False):
    base = ln.x if plain else ln.base
    m = ln.dve(ready, tt(ln.x[:, :], base[:, :], y, ALU.add))
    m = normalize(ln, ln.x[:, :], ln.x[:, :], [m])
    m = ln.pe([m], transposes(ln.k["ident"], (ln.a[:, 0:T], ln.x[:, :])))
    m = ln.act([m], act_copy(ln.xT, ln.a[:, 0:T]))
    return m


def query_and_keys(ln, wq, bq, wk, bk, keysT, nk, ready):
    m = ln.pe(ready, products((ln.a[:, 0:T], ln.w[wq], ln.xT, True, True),
                                (ln.b[:, 0:nk], ln.w[wk], keysT, True, True)))
    q = ln.act([m], act_bias(ln.qT[:, :], ln.a[:, 0:T], ln.w[bq]))
    k = ln.dve([m], stt(ln.kq[:, :, 0:nk], over(ln.b[:, 0:nk], 1, HQ), ln.w[bk], ALU.add,
                          over(ln.k["quad_mask"], 2, nk), ALU.mult))
    return q, k


def values(ln, wv, bv, srcT, nk, ready):
    m = ln.pe(ready, product(ln.a[0:nk, 0:D], srcT, ln.w[wv]))
    return ln.dve([m], tt(ln.v[0:nk, :, 0:HD], heads(ln.a[0:nk, 0:D]),
                            heads(ln.r[bv][0:nk, :]), ALU.add))


def attention(ln, nk, scale, ready, bias=None):
    a, b = ln.a, ln.b
    a4 = a[:, :].rearrange("p (h k) -> p h k", h=HQ)
    b4 = b[:, :].rearrange("p (h q) -> p h q", h=HQ)
    top = ln.small[:, 0:HQ]
    src, sc = a4[:, :, 0:nk], ln.sc[:, :, 0:nk]

    def scores(quad, ready):
        rows = slice(32 * quad, 32 * quad + 32)
        m = ln.pe(ready, product(src, ln.qT[rows, :], ln.kq[rows, :, 0:nk]))
        if bias is not None:
            m = ln.dve([m], tt(sc, src, over(bias, 1, HQ), ALU.add))
        biased = src if bias is None else sc
        m = ln.dve([m], reduce_to(top, biased, ALU.max))
        return ln.dve([m], tt(sc, biased, over(top, 2, nk), ALU.subtract))

    shifted = scores(0, ready)
    m = shifted
    for quad in range(QUADS):
        turned = ln.pe([shifted, m], transposes(ln.k["ident"], *[
            (b4[0:nk, h, :], ln.sc[:, h, 0:nk]) for h in range(HQ)]))
        m = ln.act([turned], activate(ln.p[0:nk, :, :], b4[0:nk, :, :], ACT.Exp, scale=scale))
        if quad < QUADS - 1:
            shifted = scores(quad + 1, [shifted])
        m = ln.pe([m], products(*[
            (b[32 * h:32 * h + 32, 0:T], ln.v[0:nk, HQ * quad + h, :], ln.p[0:nk, h, :], True, True)
            for h in range(HQ)]))
        m = ln.act([m], act_copy(ln.oT[:, quad, :], b[:, 0:T]))
    m = ln.pe([m], transposes(ln.k["ident"], *[
        (a4[:, quad, :], ln.oT[:, quad, :]) for quad in range(QUADS)]))
    out = a[:, :].rearrange("p (h c) -> p h c", h=HEADS)
    total = ln.small[:, 0:HEADS]
    m = ln.dve([m], recip(total, out[:, :, HD]))
    m = ln.dve([m], tt(heads(ln.o[:, :]), out[:, :, 0:HD], over(total, 2, HD), ALU.mult))
    return m


def project_out(ln, wo, ready):
    m = ln.pe([ready], transposes(ln.k["ident"], (ln.b[:, 0:T], ln.o[:, :])))
    m = ln.act([m], act_copy(ln.oT[:, 0, :], ln.b[:, 0:T]))
    return ln.pe([m], product(ln.a[:, 0:D], ln.oT[:, 0, :], ln.w[wo]))

def recurrent_attention(ln, loaded, s_loaded):
    a, b = ln.a, ln.b
    base = add_bias_to_x(ln, "rec_bo", loaded)
    m = ln.pe(loaded, products((a[:, 0:D], ln.xT, ln.w["rec_v"], True, True),
                                   (b[:, 0:T], ln.w.part("rec_qkT", 0), ln.xT, True, True)))
    v = ln.dve([m], tt(ln.o[:, :], a[:, 0:D], ln.r["rec_bv"], ALU.add))
    q = ln.act([m], act_bias(ln.qT[:, :], b[:, 0:T], ln.w["rec_bq"]))
    m = ln.pe([q, v], product(a[:, 0:T], ln.zT[:, :], ln.qT[:, :]))
    m = ln.dve([m, s_loaded], stt(ln.sc[:, 0, :], a[:, 0:T], ln.kq_dot, ALU.mult, ln.k["upto"], ALU.mult))
    m = ln.pe([v, m], product(b[:, 0:T], ln.o[:, :], ln.sc[:, 0, :]))
    m = ln.act([m], act_copy(ln.oT[:, 0, :], b[:, 0:T]))
    m = ln.pe([m], product(a[:, 0:D], ln.oT[:, 0, :], ln.w["rec_o"]))
    return finish(ln, a[:, 0:D], [m, base])


def context_attention(ln, ready, name, scale, bias=None, out=True, raw_values=False):
    if out:
        base = add_bias_to_x(ln, name + "_bo", ready)
    if raw_values:
        v = ln.pool(ready, copy(ln.v[0:S2, :, 0:HD], heads(ln.ctx_in[:, :])))
    else:
        v = values(ln, name + "_v", name + "_bv", ln.ctxT[:, :], S2, ready)
    q, k = query_and_keys(ln, name + "_q", name + "_bq", name + "_k", name + "_bk", ln.ctxT[:, :], S2, ready + [v])
    o = attention(ln, S2, scale, [q, k, v], bias)
    if out:
        y = project_out(ln, name + "_o", o)
        return finish(ln, ln.a[:, 0:D], [y, base])
    return finish(ln, ln.o[:, :], [o], plain=True)


def route(ln, ready):
    m = ln.pe(ready, product(ln.a[:, 0:EXPERTS], ln.xT, ln.w["f0_gate"]))
    m = gate_softmax(ln, m, ln.s["probs"][:, ln.n, :])
    return m


def gate_softmax(ln, m, out):
    logits = ln.small[:, 0:EXPERTS]
    top, total = ln.small[:, 16:17], ln.small[:, 17:18]
    m = ln.dve([m], reduce_to(top, ln.a[:, 0:EXPERTS], ALU.max))
    m = ln.dve([m], ts(logits, ln.a[:, 0:EXPERTS], top, ALU.subtract))
    m = ln.act([m], activate(logits, logits, ACT.Exp))
    m = ln.dve([m], reduce_to(total, logits, ALU.add))
    m = ln.dve([m], recip(total, total))
    return ln.dve([m], ts(out, logits, total, ALU.mult))


def latent_attention(ln, ready):
    a, b = ln.a, ln.b
    a4 = a[:, :].rearrange("p (h k) -> p h k", h=HQ)
    b4 = b[:, :].rearrange("p (h q) -> p h q", h=HQ)
    top = ln.small[:, 0:HQ]
    for kv in range(KV):
        start = ready if kv == 0 else [o]
        m = ln.pe(start, products((a[:, 0:T], ln.s["a1_q"][:, kv, :], ln.xT, True, True),
                                    (b[:, 0:T], ln.s["a1_k"][:, kv, :], ln.xT, True, True)))
        q = ln.act([m], act_copy(ln.qT[:, :], a[:, 0:T]))
        k = ln.dve([m], tt(ln.kq[:, :, :], over(b[:, 0:T], 1, HQ), over(ln.k["group_mask"], 2, T), ALU.mult))
        if kv == 0:
            m = ln.pe([k], product(b[:, 0:KV * LAT], ln.xT, ln.w["a1_vdown"]))
            v = ln.act([m], act_copy(ln.wide[:, 0:KV * LAT], b[:, 0:KV * LAT]))
        m = ln.pe([q, k], product(a[:, :], ln.qT[:, :], ln.kq[:, :, :]))
        m = ln.dve([m], tt(ln.sc[:, :, :], a4, over(ln.k["causal"], 1, HQ), ALU.add))
        m = ln.dve([m], reduce_to(top, ln.sc[:, :, :], ALU.max))
        m = ln.dve([m], tt(ln.sc[:, :, :], ln.sc[:, :, :], over(top, 2, T), ALU.subtract))
        m = ln.pe([m, v], transposes(ln.k["ident"], *[
            (b4[:, h, :], ln.sc[:, h, :]) for h in range(HQ)]))
        m = ln.act([m], activate(ln.p[:, :, :], b4, ACT.Exp, scale=float(P) ** -0.5))
        m = ln.pe([m, v], products(*[
            (b[32 * h:32 * h + 32, 0:T], ln.wide[:, kv * LAT:(kv + 1) * LAT], ln.p[:, h, :], True, True)
            for h in range(HQ)] + [
            (b[32 * h:32 * h + 32, T:2 * T], ln.k["ones"], ln.p[:, h, :], True, True)
            for h in range(HQ)]))
        m = ln.dve([m], recip(ln.sc[:, 0, :], b[:, T:2 * T]))
        o = ln.dve([m], tt(ln.oT[:, kv, :], b[:, 0:T], ln.sc[:, 0, :], ALU.mult))
    m = ln.pe([o], products(*[(a[:, 0:D], ln.oT[:, kv, :], ln.s["a1_vo"][:, kv, :], kv == 0, kv == KV - 1)
                                for kv in range(KV)]))
    return finish(ln, a[:, 0:D], [m], plain=True)


def fp4_feed_forward(ln, ready):
    a, b = ln.a, ln.b
    x_rounded = ln.o
    m = fp4_round(ln, ln.x[:, :], x_rounded[:, :], D // FP4_BLOCK, ready, fp4_buffers(ln))
    m = ln.pe([m], transposes(ln.k["ident"], (a[:, 0:T], x_rounded[:, :])))
    m = ln.act([m], act_copy(ln.qT[:, :], a[:, 0:T]))
    m = ln.pe([m], products((a[:, 0:I_FF], ln.qT[:, :], ln.s["f1_gateT"][:, :], True, True),
                              (b[:, 0:I_FF], ln.qT[:, :], ln.s["f1_upT"][:, :], True, True)))
    h = ln.wide[:, 0:I_FF]
    m = ln.act([m], activate(h, a[:, 0:I_FF], ACT.Silu))
    m = ln.dve([m], tt(h, h, b[:, 0:I_FF], ALU.mult))
    m = fp4_round(ln, h, h, I_FF // FP4_BLOCK, [m], fp4_buffers(ln))
    chunks = [(c, min(P, I_FF - c * P)) for c in range(3)]
    m = ln.pe([m], transposes(ln.k["ident"], *[
        (a[0:n, c * T:(c + 1) * T], ln.wide[:, c * P:c * P + n]) for c, n in chunks]))
    m = ln.act([m], act_copy(ln.p[:, 0:2, :], a[:, 0:2 * T].rearrange("p (c t) -> p c t", c=2)))
    n = chunks[2][1]
    m = ln.act([m], act_copy(ln.p[0:n, 2, :], a[0:n, 2 * T:3 * T]))
    m = ln.pe([m], products(*[(b[:, 0:D], ln.p[0:n, c, :], ln.s["f1_downT"][0:n, c, :], c == 0, c == 2)
                                for c, n in chunks]))
    return finish(ln, b[:, 0:D], [m], plain=True)


def self_attention_shared_values(ln, ready):
    v = values(ln, "a2_k", "a2_bv", ln.xT, T, ready)
    q, k = query_and_keys(ln, "a2_q", "a2_bq", "a2_k", "a2_bk", ln.xT, T, ready + [v])
    o = attention(ln, T, float(D) ** -0.5, [q, k, v])
    return finish(ln, ln.o[:, :], [o], plain=True)


def low_rank_feed_forward(ln, ready):
    a, b = ln.a, ln.b
    half = E6 // 2 * LT
    tokT = ln.s["f2_tokT"]
    m = ln.pe(ready, products(
        (a[:, 0:half], ln.xT, tokT[:, 0:half], True, True),
        (a[:, half:half + E6], ln.xT, ln.w["f2_gate"], True, True),
        (b[:, 0:half], ln.xT, tokT[:, half:2 * half], True, True)))
    g, top, tie = ln.small[:, 0:E6], ln.small[:, 16:17], ln.small[:, 8:8 + E6]
    g_m = ln.dve([m], reduce_to(top, a[:, half:half + E6], ALU.max))
    g_m = ln.dve([g_m], ts(tie, a[:, half:half + E6], top, ALU.is_equal))
    g_m = ln.dve([g_m], tt(tie, tie, ln.k["falling"], ALU.mult))
    g_m = ln.dve([g_m], reduce_to(top, tie, ALU.max))
    g_m = ln.dve([g_m], tt(g, tie, top.to_broadcast([P, E6]), ALU.is_equal))
    wide = ln.wide[:, :].rearrange("p (e l) -> p e l", e=E6)
    m = ln.dve([g_m], tt(wide[:, 0:3, :], a[:, 0:half].rearrange("p (e l) -> p e l", e=3),
                           over(ln.small[:, 0:3], 2, LT), ALU.mult))
    m = ln.dve([g_m], tt(wide[:, 3:6, :], b[:, 0:half].rearrange("p (e l) -> p e l", e=3),
                           over(ln.small[:, 3:6], 2, LT), ALU.mult))
    own = ln.sc[:, 0, 0:LT]
    m = ln.dve([m], reduce_to(own, ln.wide[:, :].rearrange("p (e l) -> p l e", e=E6), ALU.add))
    m = ln.dve([m], reduce_to(top, own, ALU.max))
    m = ln.dve([m], ts(top, top, -float(D) ** -0.5, ALU.mult))
    total = ln.small[:, 17:18]
    m = ln.act([m], activate(own, own, ACT.Exp, bias=top, scale=float(D) ** -0.5, accum_out=total))
    m = ln.dve([m], recip(total, total))
    m = ln.dve([m], ts(own, own, total, ALU.mult))
    m = ln.pe([m], transposes(ln.k["ident"], (a[0:LT, 0:T], own)))
    m = ln.act([m], act_copy(ln.p[0:LT, 0, :], a[0:LT, 0:T]))
    val = ln.s["f2_val"]
    m = ln.pe([m], products(
        (a[:, 0:3 * D], ln.p[0:LT, 0, :], val[0:LT, 0:3 * D], True, True),
        (a[:, 3 * D:4 * D], ln.xT, ln.s["f2_wd"][:, :], True, True),
        (b[:, 0:3 * D], ln.p[0:LT, 0, :], val[0:LT, 3 * D:6 * D], True, True)))
    acc = ln.o[:, :]
    m = ln.dve([m], tt(acc, a[:, 3 * D:4 * D], ln.s["f2_bd"], ALU.add))
    for e in range(E6):
        bank = a if e < 3 else b
        m = ln.dve([m], stt(acc, bank[:, e % 3 * D:(e % 3 + 1) * D], ln.small[:, e:e + 1], ALU.mult,
                              acc, ALU.add))
    m = ln.act([m], activate(acc, acc, ACT.Exp))
    zero = ln.sc[:, 0, :]
    m = ln.dve([m], ts(zero, acc, 0.0, ALU.is_equal, float(np.finfo(np.float32).eps), ALU.mult))
    m = ln.dve([m], tt(acc, acc, zero, ALU.add))
    m = ln.act([m], activate(acc, acc, ACT.Ln))
    m = ln.dve([m], tt(acc, acc, ln.x[:, :], ALU.add))
    return finish(ln, acc, [m], plain=True)


def rotary_attention(ln, ready):
    a, b = ln.a, ln.b
    base = add_bias_to_x(ln, "a3_bo", ready)
    m = ln.pe(ready, product(b[:, 0:D], ln.xT, ln.w["a3_v"]))
    v = ln.act([m], act_copy(ln.v[:, :, 0:HD], heads(b[:, 0:D])))
    m = ln.pe(ready, products(*[(a[:, i * T:(i + 1) * T], ln.w.part("a3_qk", i), ln.xT, True, True)
                                  for i in range(4)]))
    rot = ln.sc[:, :, :].rearrange("p (n f) t -> p n f t", n=2)
    m = ln.dve([m], tt(rot, a[:, :].rearrange("p (n f t) -> p n f t", n=2, f=2),
                         over(ln.k["rope"].rearrange("p (f t) -> p f t", f=2), 1, 2), ALU.mult))
    q = ln.dve([m], tt(ln.qT[:, :], ln.sc[:, 0, :], ln.sc[:, 1, :], ALU.add))
    k = ln.dve([m], tt(ln.o[:, :], ln.sc[:, 2, :], ln.sc[:, 3, :], ALU.add))
    k = ln.dve([k], tt(ln.kq[:, :, :], over(ln.o[:, :], 1, HQ), over(ln.k["quad_mask"], 2, T), ALU.mult))
    o = attention(ln, T, float(HD) ** -0.5, [q, k, v])
    y = project_out(ln, "a3_o", o)
    return finish(ln, a[:, 0:D], [y, base])


def relu_attention(ln, ready):
    a, b = ln.a, ln.b
    m = ln.pe(ready, products((a[:, 0:T], ln.w["x3_q"], ln.xT, True, True),
                                (b[:, 0:S2], ln.w["x3_k"], ln.ctxT[:, :], True, True)))
    q = ln.act([m], activate(ln.qT[:, :], a[:, 0:T], ACT.Relu, bias=ln.w["x3_bq"]))
    kT = ln.kq[:, 0, 0:S2]
    k = ln.dve([m], ts(kT, b[:, 0:S2], ln.w["x3_bk"], ALU.add, 0.0, ALU.max))
    m = ln.pe([q], product(a[0:S2, 0:D], ln.ctxT[:, :], ln.w["x3_v"]))
    vals = ln.wide[0:S2, 0:D]
    v = ln.dve([m], tt(vals, a[0:S2, 0:D], ln.r["x3_bv"][0:S2, :], ALU.add))
    v = ln.dve([v], ts(vals, vals, 0.0, ALU.max))
    m = ctx_read = ln.pe([q, k], product(b[0:S2, 0:T], kT, ln.qT[:, :]))
    lg = ln.p[0:S2, 0, :]
    m = ln.dve([m], ts(lg, b[0:S2, 0:T], 0.0, ALU.max, float(D) ** -0.5, ALU.mult))
    m = ln.dve([m], tt(lg, lg, ln.w["x3_maskT"][0:S2, :], ALU.add))
    m = ln.pe([m, v], product(b[:, 0:D], lg, vals))
    m = ln.act([m], activate(ln.o[:, :], b[:, 0:D], ACT.Relu))
    return finish(ln, ln.o[:, :], [m], plain=True), ctx_read


def conv_and_attention(ln, ready):
    a, b = ln.a, ln.b
    ends = ln.pool(ready, fill(ln.wide[:, 0:T + 2:T + 1], 0.0))
    m = ln.pool(ready, copy(ln.wide[:, 1:T + 1], ln.xT))
    conv = ln.pe([m, ends], products(*[
        (a[:, 0:D], ln.wide[:, i:i + T], ln.w.part("f3_conv", i), i == 0, i == 2) for i in range(3)]))
    conv_out = ln.oT[:, 3, :]
    m = ln.dve([conv], tt(conv_out, a[:, 0:D], ln.r["f3_bconv"], ALU.add))
    base = ln.pool([m], tt(ln.base[:, :], conv_out, ln.r["f3_bo"], ALU.add))
    m = ln.pe([m], transposes(ln.k["ident"], (b[:, 0:T], conv_out)))
    y_ready = ln.act([m], act_copy(ln.xT, b[:, 0:T]))
    v = values(ln, "f3_v", "f3_bv", ln.xT, T, [y_ready])
    q, k = query_and_keys(ln, "f3_q", "f3_bq", "f3_k", "f3_bk", ln.xT, T, [y_ready, v])
    o = attention(ln, T, float(HD) ** -0.5, [q, k, v, base])
    y = project_out(ln, "f3_o", o)
    m = ln.dve([y, base], tt(ln.o[:, :], ln.base[:, :], a[:, 0:D], ALU.add))
    mid = ln.base
    m = normalize(ln, ln.o[:, :], mid[:, :], [m], "f3_g1", "f3_n1")
    m = ln.pe([m], transposes(ln.k["ident"], (a[:, 0:T], mid[:, :])))
    midT = ln.act([m], act_copy(ln.xT, a[:, 0:T]))
    m = ln.pe([midT], product(a[:, 0:EXPERTS], ln.xT, ln.w["f3_gate"]))
    logits = ln.small[:, 0:EXPERTS]
    top, total = ln.small[:, 16:17], ln.small[:, 17:18]
    m = ln.dve([m], tt(logits, a[:, 0:EXPERTS], ln.r["f3_bgate"], ALU.add))
    m = ln.dve([m], reduce_to(top, logits, ALU.max))
    m = ln.dve([m], ts(logits, logits, top, ALU.subtract))
    m = ln.act([m], activate(logits, logits, ACT.Exp))
    m = ln.dve([m], reduce_to(total, logits, ALU.add))
    m = ln.dve([m], recip(total, total))
    m = ln.dve([m], ts(ln.gates[:, :], logits, total, ALU.mult))
    m = ln.pe([m], transposes(ln.k["ident"], (a[0:EXPERTS, 0:T], ln.gates[:, :])))
    m = a_read = ln.act([m], act_copy(ln.o[0:EXPERTS, :], a[0:EXPERTS, 0:T]))
    m = ln.pe([m], product(b[:, 0:D], ln.o[0:EXPERTS, :], ln.w["f3_b2"][0:EXPERTS, :]))
    m = ln.dve([m], tt(mid[:, :], mid[:, :], b[:, 0:D], ALU.add))
    return [midT, a_read], m


def end_of_layer(ln, mixed):
    m = normalize(ln, ln.base[:, :], ln.o[:, :], [mixed], "f3_g2", "f3_n2")
    m = ln.dve([m], tt(ln.x[:, :], ln.x[:, :], ln.o[:, :], ALU.add))
    return normalize(ln, ln.x[:, :], ln.o[:, :], [m])


def heads(ap):
    return ap.rearrange("p (h c) -> p h c", h=HEADS)


def blocks(ap, n):
    return ap.rearrange("p (b c) -> p b c", b=n)


def fp4_buffers(lane):
    flat = [t[:, :, :].rearrange("p h t -> p (h t)") for t in (lane.sc, lane.p, lane.oT)]
    return flat + [lane.small]


def fp4_round(w, src, dst, n, ready, buffers, rows=P):
    mag, sign, level, small = buffers
    size = n * FP4_BLOCK
    mag, sign, level = mag[0:rows, 0:size], sign[0:rows, 0:size], level[0:rows, 0:size]
    scale, inv = small[0:rows, 0:n], small[0:rows, 32:32 + n]
    m = w.dve(ready, reduce_to(scale, blocks(src, n), ALU.max, magnitude=True))
    m = w.dve([m], ts(scale, scale, 1.0 / 6.0, ALU.mult, 1e-12, ALU.max))
    m2 = w.dve([m], recip(inv, scale))
    m2 = w.dve([m2], tt(blocks(mag, n), blocks(src, n), over(inv, 2, FP4_BLOCK), ALU.mult))
    s = w.act([m2], activate(sign, mag, ACT.Sign))
    s = w.pool([s, m], tt(blocks(sign, n), blocks(sign, n), over(scale, 2, FP4_BLOCK), ALU.mult))
    m2 = w.act([m2], activate(mag, mag, ACT.Abs))
    m = w.dve([m2], ts(level, mag, 5.0, ALU.is_gt, 2.0, ALU.mult))
    for mid in (3.5, 2.5):
        m = w.dve([m], stt(level, mag, mid, ALU.is_gt, level, ALU.add))
    m = w.dve([m], ts(level, level, 2.0, ALU.mult))
    for mid in (1.75, 1.25, 0.75, 0.25):
        m = w.dve([m], stt(level, mag, mid, ALU.is_gt, level, ALU.add))
    return w.dve([m, s], stt(dst, level, 0.5, ALU.mult, sign, ALU.mult))


def routed_mixture(w, lanes, s, banks):
    k = s["k"]
    probs = s["probs"][:, :, :].rearrange("p n e -> p (n e)")
    ne = LANES * EXPERTS
    m = w.pe([], transposes(k["ident"], (banks[0][0:ne, 0:T], probs)))
    left, best = s["left"], s["best"]
    m = w.dve([m], copy(left[:, :], banks[0][0:ne, 0:T]))
    for _ in range(CAP // 8):
        m = w.dve([m], (lambda e: e.max(best[:, :], left[:, :]), row_ns(left)))
        m = w.dve([m], (lambda e: e.match_replace(left[:, :], best[:, :], left[:, :], -1.0), row_ns(left)))
    m = w.dve([m], ts(left[:, :], left[:, :], 0.0, ALU.is_lt))
    m = w.pe([m], transposes(k["ident"], (banks[1][:, 0:ne], left[:, :])))
    taken, place = s["taken"], s["place"]
    taken_m = w.dve([m], copy(taken[:, :], banks[1][:, 0:ne]))
    m = w.pe([taken_m], product(banks[2][:, 0:ne], k["upto"], taken[:, :]))
    m = w.dve([m], tt(place[:, :], banks[2][:, 0:ne], taken[:, :], ALU.mult))
    pick, weighted = s["pick"], s["weighted"]
    by_expert = [t.rearrange("p (n e) -> p e n", n=LANES) for t in (place[:, :], probs)]
    picked = w.dve([m], tt(pick[:, :, :, :], over(by_expert[0], 3, CAP),
                           k["slots"].unsqueeze(1).unsqueeze(1).to_broadcast([P, EXPERTS, LANES, CAP]), ALU.is_equal))
    weighed = w.pool([picked], tt(weighted[:, :, :, :], pick[:, :, :, :], over(by_expert[1], 3, CAP), ALU.mult))
    xin = s["xin"]
    for ln in lanes:
        bank = banks[ln.n]
        m = w.pe([picked], product(bank[:, 0:EXPERTS * CAP].rearrange("p (e s) -> p e s", e=EXPERTS),
                 ln.x[:, :], pick[:, :, ln.n, :]))
        xin_m = w.act([m], act_copy(xin[:, :, ln.n, :], bank[:, 0:EXPERTS * CAP].rearrange("p (e s) -> p e s", e=EXPERTS)))
    back = s["back"]
    for h in range(2):
        bank = banks[4 + h]
        m = w.pe([weighed], transposes(k["ident"], *[
            (bank[:, i * T:(i + 1) * T], weighted[:, 4 * h + i, :, :].rearrange("p n s -> p (n s)"))
            for i in range(4)]))
        back_m = w.dve([m], copy(back[:, 4 * h:4 * h + 4, :], bank[:, :].rearrange("p (e t) -> p e t", e=4)))
    hid, y = s["hid"], s["moe_y"]
    hid_read, out_read = [[], []], [[], []]
    w1, w2 = s["L0_w1"], s["L0_w2"]
    for e in range(EXPERTS):
        i, bank, out = e % 2, banks[e % 2], banks[2 + e % 2]
        m = w.pe([xin_m], products(*[
            (bank[:, c * P:(c + 1) * P], w1[:, e, c * P:(c + 1) * P], xin[:, e, :, :], True, True)
            for c in range(HC)]))
        hidden = hid[:, i, 0:DFF]
        m = w.act([m] + hid_read[i], activate(hidden, bank[:, :], ACT.Gelu))
        m = w.pe([m] + out_read[i], products(*[
            (out[:, 0:D], hid[:, i, c * P:(c + 1) * P], w2[:, e, c, :], c == 0, c == HC - 1)
            for c in range(HC)]))
        hid_read[i] = [m]
        y_m = w.dve([m], copy(y[:, e, :], out[:, 0:D]))
        out_read[i] = [y_m]
    mixed = []
    for ln in lanes:
        rows = slice(CAP * ln.n, CAP * (ln.n + 1))
        mixed.append(ln.pe([y_m, back_m], products(*[
            (ln.a[:, 0:D], back[rows, e, :], y[rows, e, :], e == 0, e == EXPERTS - 1)
            for e in range(EXPERTS)])))
    return mixed


def gated_mixture(ln, ready, acc, scratch_free):
    a, b, w1, w2 = ln.a, ln.b, ln.s["L3_w1"], ln.s["L3_w2"]
    a4 = a[:, :].rearrange("p (c t) -> p c t", c=HC)

    def hidden(e, ready):
        return ln.pe(ready, products(*[
            (a4[:, c, :], w1[:, e, c * P:(c + 1) * P], ln.xT, True, True) for c in range(HC)]))

    m = hidden(0, ready)
    read = [scratch_free, scratch_free]
    for e in range(EXPERTS):
        hid = ln.hid[:, e % 2, :, :]
        m = ln.dve([m] + read[e % 2], tt(hid, a4, over(ln.w.part("f3_b1", e, HC), 2, T), ALU.add))
        relu = ln.act([m], activate(hid, hid, ACT.Relu))
        if e < EXPERTS - 1:
            m = xT_read = hidden(e + 1, [m])
        out = ln.pe([relu, acc], products(*[
            (b[:, 0:D], hid[:, c, :], w2[:, e, c, :], c == 0, c == HC - 1) for c in range(HC)]))
        read[e % 2] = [out]
        acc = ln.dve([out, acc], stt(ln.base[:, :], b[:, 0:D], ln.gates[:, e:e + 1], ALU.mult,
                                     ln.base[:, :], ALU.add))
    return acc, xT_read


def prepare(w, s, wt, ready, banks, temp):
    k = s["k"]
    w.dve(ready, fill(temp["small"][:, :], 0.0))
    w.act(ready, act_copy(temp["first"][:, :], k["ident"]))
    w.pe(ready, transposes(k["ident"], (banks[7][:, 0:P], k["ident"])))
    m = w.pe([], products(*[
        (banks[0][:, h * LAT:(h + 1) * LAT], wt.part("a1_qT", h), wt["a1_kupT"], True, True) for h in range(8)]))
    w.dve([m], copy(s["a1_q"][:, :, :], banks[0][:, 0:8 * LAT].rearrange("p (n c) -> p n c", n=KV)))
    vo = []
    for kv in range(KV):
        w.dve([], copy(s["a1_k"][:, kv, :].rearrange("p (h c) -> p h c", h=HQ),
                       over(wt["a1_kdown"][:, kv * LAT:(kv + 1) * LAT], 1, HQ)))
        m = w.pe(vo, products(*[
            (banks[1][32 * h:32 * h + 32, 0:D], wt["a1_vupT"], wt.part("a1_o", kv * HQ + h), True, True)
            for h in range(HQ)]))
        vo = [w.dve([m], copy(s["a1_vo"][:, kv, :], banks[1][:, 0:D]))]
    scale = s["r"]["f2_scale"]
    wd = w.dve([], ts(s["f2_wd"][:, :], wt["f2_wdT"], scale, ALU.mult))
    w.dve([], ts(s["f2_bd"], s["r"]["f2_bd"], scale, ALU.mult))
    valT = temp["valT"]
    for e in range(E6):
        m = w.pe([], product(banks[2][:, 0:LT], wt["f2_B"][0:16, e * D:(e + 1) * D],
                             wt["f2_A"][0:16, e * LT:(e + 1) * LT]))
        tokT = s["f2_tokT"][:, e * LT:(e + 1) * LT]
        m = w.dve([m], copy(tokT, banks[2][:, 0:LT]))
        m = w.pe([m], product(banks[3][:, 0:LT], wt["f2_wtT"], tokT))
        m = w.act([m], act_bias(valT[:, 0:LT], banks[3][:, 0:LT], wt["f2_bt"]))
        m = w.pe([m, wd], product(banks[4][0:LT, 0:D], valT[:, 0:LT], s["f2_wd"][:, :]))
        val = w.dve([m], copy(s["f2_val"][0:LT, e * D:(e + 1) * D], banks[4][0:LT, 0:D]))
    w.dve([val], fill(s["f2_val"][0:1, :], 0.0))
    w.dve([], ts(s["x2_mask"][:, :], s["x2_mask_int"][:, :], 0.0, ALU.is_equal, MASKED, ALU.mult))
    buffers = (temp["mag"], temp["sign"], temp["level"], temp["small"])
    m = None
    for name in ("gate", "up"):
        tiles = [(wt.part("f1_" + name, 0), P, 0), (wt.part("f1_" + name, 1), P, P),
                 (wt[f"f1_{name}_rest"][0:96, :], 96, 2 * P)]
        for tile, rows, at in tiles:
            m = fp4_round(w, tile, tile, D // FP4_BLOCK, [m] if m else [], buffers, rows)
            t = w.pe([m], transposes(k["ident"], (banks[5][:, 0:rows], tile)))
            w.act([t], act_copy(s[f"f1_{name}T"][:, at:at + rows], banks[5][:, 0:rows]))
    m = fp4_round(w, wt["f1_down"], wt["f1_down"], I_FF // FP4_BLOCK, [m], buffers)
    bank_read = []
    for c in range(3):
        n = min(P, I_FF - c * P)
        t = w.pe([m] + bank_read, transposes(k["ident"], (banks[6][0:n, 0:D], wt["f1_down"][:, c * P:c * P + n])))
        bank_read = [w.act([t], act_copy(s["f1_downT"][0:n, c, :], banks[6][0:n, 0:D]))]


def decoder_phase(nc, dram, nb, w_off, w_total, p_off, p_total, rows_off, rows_total, c_off, c_total):
    with ExitStack() as ctx:
        def sb(name, *shape, dt=F32):
            return ctx.enter_context(nc.sbuf_tensor(name, list(shape), dt))

        signals = []
        experts_loaded = Signal(ctx.enter_context(nc.semaphore("experts_loaded")))
        weights, rows, consts = sb("weights_sb", P, w_total), sb("rows_sb", P, rows_total), sb("consts_sb", P, c_total)
        s = {
            "w": Weights(weights, w_off), "r": Weights(rows, rows_off), "k": Weights(consts, c_off),
            "xT_all": sb("xT_all", P, LANES, T),
            "a1_q": sb("a1_q", P, KV, P), "a1_k": sb("a1_k", P, KV, P), "a1_vo": sb("a1_vo", P, KV, D),
            "f1_gateT": sb("f1_gateT", P, I_FF), "f1_upT": sb("f1_upT", P, I_FF), "f1_downT": sb("f1_downT", P, 3, D),
            "f2_tokT": sb("f2_tokT", P, E6 * LT), "f2_val": sb("f2_val", P, E6 * D), "f2_wd": sb("f2_wd", P, D),
            "x2_mask": sb("x2_mask", P, S2), "x2_mask_int": sb("x2_mask_int", P, S2, dt=I32),
            "kq": sb("kq_dots", P, LANES),
            "probs": sb("probs", P, LANES, EXPERTS), "left": sb("left", LANES * EXPERTS, T),
            "best": sb("best", LANES * EXPERTS, 8), "taken": sb("taken", P, LANES * EXPERTS),
            "place": sb("place", P, LANES * EXPERTS),
        }
        s["f2_bd"] = sb("f2_bd_scaled", P, D)[:, :]
        s["minus_half"] = sb("minus_half", P, 1)[:, :]
        for layer in ("L0", "L3"):
            s[layer + "_w1"] = sb(layer + "_w1", P, EXPERTS, DFF)
            s[layer + "_w2"] = sb(layer + "_w2", P, EXPERTS, HC, D)
        scratch = sb("mixture_scratch", P, 6144)
        quarters = [scratch[:, i * 1024:(i + 1) * 1024] for i in range(6)]
        split = "p (e n s) -> p e n s"
        s["pick"], s["weighted"], s["xin"] = [
            q.rearrange(split, e=EXPERTS, n=LANES) for q in quarters[0:3]]
        s["back"], s["moe_y"] = [q.rearrange("p (e t) -> p e t", e=EXPERTS) for q in quarters[3:5]]
        routed_hid = quarters[5].rearrange("p (i f) -> p i f", i=2)
        s["hid"] = routed_hid
        s["gated_hid"] = scratch[:, 0:4096].rearrange("p (n i c t) -> p n i c t", n=LANES, i=2, c=HC)
        with ExitStack() as own:
            def setup_sb(name, *shape):
                return own.enter_context(nc.sbuf_tensor("setup_" + name, list(shape), F32))

            setup, once = {e: [] for e in ENGINES}, []
            w = new_thread(nc, own, "setup", once)
            banks = [own.enter_context(nc.psum_tensor(f"setup_bank{i}", [P, 512], F32)) for i in range(8)]
            raw = setup_sb("weights", P, p_total)
            temp = {"small": setup_sb("small", P, 64), "first": setup_sb("first", P, P), "valT": setup_sb("valT", P, LT)}
            temp.update({n: setup_sb(n, P, I_FF) for n in ("mag", "sign", "level")})
            loaded = new_signal(nc, own, "weights_loaded", once)
            for out, in_ in [(weights[:, :], dram["weights"]), (consts[:, :], dram["consts"]),
                             (raw[:, :], dram["prepared"]),
                             (rows[:, :], dram["rows"].to_broadcast([P, rows_total])),
                             (s["x2_mask_int"][:, :], dram["x2_mask"])]:
                m = transfer(w.dma, loaded, [], move(out, in_))
            for layer in ("L0", "L3"):
                for out, name in ((s[layer + "_w1"][:, :, :].rearrange("p e f -> p (e f)"), "_w1"),
                                  (s[layer + "_w2"][:, :, :, :].rearrange("p e c d -> p (e c d)"), "_w2")):
                    experts = transfer(w.dma, experts_loaded, [], move(out, dram[layer + name]))
            w.pool([], fill(s["minus_half"], -0.5))
            prepare(w, s, Weights(raw, p_off), [m], banks, temp)
            interleave([w], setup)
            with nc.Block() as block:
                block.sync(lambda e: play(setup["sync"], e))
                block.tensor(lambda e: play(setup["tensor"], e))
                block.scalar(lambda e: play(setup["scalar"], e))
                block.vector(lambda e: play(setup["vector"], e))
                block.gpsimd(lambda e: play(setup["gpsimd"], e))

        lanes = [new_lane(nc, ctx, n, signals, s) for n in range(LANES)]
        banks = [ln.a for ln in lanes] + [ln.b for ln in lanes]
        both = new_thread(nc, ctx, "lanes", signals)
        s_signal = new_signal(nc, ctx, "s_arrived", signals)

        def load_s(ahead):
            return transfer(both.dma, s_signal, [], lambda e, turn: e.dma_start(
                s["kq"][:, :], dram["s"][:, bass.ds(turn * LANES + ahead * LANES, LANES)]))

        def load(ln, signal, ahead, waits, out, src):
            return transfer(ln.dma, ln.arrived[signal], waits, lambda e, turn: e.dma_start(
                out, src(turn * LANES + (ahead * LANES + ln.n))))

        def load_first(ln, ahead):
            load(ln, "x", ahead, [], ln.zT[:, :], lambda b: dram["z"][:, bass.ds(b * T, T)])
            return load(ln, "x", ahead, [], ln.ctx_in[:, :],
                        lambda b: dram["ctx"][bass.ds(b, 1)].rearrange("a t d -> (a t) d"))

        def load_context(ln, ahead, waits):
            return load(ln, "ctx", ahead, waits, ln.ctxT[:, :], lambda b: dram["ctxT"][:, bass.ds(b * S2, S2)])

        def load_mask(ln, ahead, waits):
            return load(ln, "mask", ahead, waits, ln.key_mask_int[:, :],
                        lambda b: dram["key_mask"][bass.ds(b, 1), :].to_broadcast([P, S2]))

        def load_x(ln, ahead, x_read, xT_read):
            load(ln, "x", ahead, x_read, ln.x[:, :], lambda b: dram["x"][bass.ds(b, 1)].rearrange("a t d -> (a t) d"))
            return load(ln, "x", ahead, xT_read, ln.xT, lambda b: dram["xT"][:, bass.ds(b * T, T)])

        def first_part(ln, arrived, s_arrived):
            m = recurrent_attention(ln, arrived, s_arrived)
            m = context_attention(ln, [m], "x0", float(HD) ** -0.5, raw_values=True)
            route(ln, [m])

        def second_part(ln, mixed):
            mask = ln.pool([], ts(ln.key_mask[:, :], ln.key_mask_int[:, :], 0.0, ALU.is_gt, MASKED, ALU.mult))
            m = finish(ln, ln.a[:, 0:D], [mixed[ln.n]], plain=True)
            m = latent_attention(ln, [m])
            m = context_attention(ln, [m, mask], "x1", float(HD) ** -0.5, bias=ln.key_mask[:, :], out=False)
            m = fp4_feed_forward(ln, [m])
            m = self_attention_shared_values(ln, [m])
            m = context_attention(ln, [m], "x2", float(HD) ** -0.5, bias=s["x2_mask"][:, :])
            m = low_rank_feed_forward(ln, [m])
            m = rotary_attention(ln, [m])
            m, ctx_read = relu_attention(ln, [m])
            ready, acc = conv_and_attention(ln, [m])
            m, xT_read = gated_mixture(ln, ready, acc, mixed)
            ended = end_of_layer(ln, m)
            stored = transfer(ln.dma, ln.out_stored, [ended], lambda e, turn: e.dma_start(
                dram["out"][bass.ds(turn * LANES + ln.n, 1)].rearrange("a t d -> (a t) d"), ln.o[:, :]))
            return mask, ctx_read, ended, xT_read, stored

        def close():
            queues = {e: [] for e in ENGINES}
            interleave(lanes + [both], queues)
            counts = [(sig, sig.count) for sig in signals if sig.count]
            ends = {e: [] for e in ENGINES}
            for thread in lanes + [both]:
                for steps in (thread.pe, thread.act, thread.dve, thread.pool):
                    if steps.done.count:
                        ends[steps.engine].append((steps.done, steps.done.count))
            engines_own = [sig for e in ENGINES for sig, _ in ends[e]]
            ends["sync"] = [one for one in counts if one[0] not in engines_own]
            for sig in signals:
                sig.count = 0
            return queues, ends, [sig for sig, _ in counts]

        s_arrived = load_s(0)
        for ln in lanes:
            load_first(ln, 0)
            load_mask(ln, 0, [])
            first_part(ln, [load_x(ln, 0, [], []), load_context(ln, 0, [])], s_arrived)
        opening = close()

        s_arrived = load_s(1)
        for ln in lanes:
            load_first(ln, 1)
        mixed = routed_mixture(both, lanes, s, banks)
        for ln in lanes:
            mask, ctx_read, x_read, xT_read, stored = second_part(ln, mixed)
            load_mask(ln, 1, [mask])
            context = load_context(ln, 1, [ctx_read])
            first_part(ln, [load_x(ln, 1, [x_read], [xT_read]), context, stored], s_arrived)
        body = close()

        mixed = routed_mixture(both, lanes, s, banks)
        for ln in lanes:
            second_part(ln, mixed)
        closing = close()

        met = ctx.enter_context(nc.semaphore("engines_met"))
        go = {e: ctx.enter_context(nc.semaphore(f"{e}_goes_on")) for e in ENGINES[:4]}
        ones_set = ctx.enter_context(nc.semaphore("value_columns_set"))
        turns = nb // LANES

        def step(name, eng, phase, turn):
            queues, ends, counted = phase
            play(queues[name], eng, turn)
            for sig, count in ends[name]:
                eng.wait_ge(sig.sem, count)
            if name == "sync":
                eng.wait_ge(met, 4)
                eng.sem_clear(met)
                for sig in counted:
                    eng.sem_clear(sig.sem)
                for other in ENGINES[:4]:
                    eng.sem_inc(go[other], 1)
            else:
                eng.sem_inc(met, 1)
                eng.wait_ge(go[name], 1)
                eng.sem_clear(go[name])

        def run(name, eng):
            if name == "gpsimd":
                for n, ln in enumerate(lanes):
                    eng.memset(ln.v[:, :, :], 0.0).then_inc(ones_set, 1)
                    eng.wait_ge(ones_set, 2 * n + 1)
                    eng.memset(ln.v[:, :, HD:HD + 1], 1.0).then_inc(ones_set, 1)
            elif name != "sync":
                eng.wait_ge(ones_set, 2 * LANES)
            if name == "tensor":
                eng.wait_ge(experts_loaded.sem, experts_loaded.count)
            step(name, eng, opening, 0)
            if turns > 1:
                with eng.Fori(0, turns - 1) as turn:
                    step(name, eng, body, turn)
            step(name, eng, closing, turns - 1)

        with nc.Block() as block:
            block.sync(lambda e: run("sync", e))
            block.tensor(lambda e: run("tensor", e))
            block.scalar(lambda e: run("scalar", e))
            block.vector(lambda e: run("vector", e))
            block.gpsimd(lambda e: run("gpsimd", e))


def offsets(widths):
    found, at = {}, 0
    for name, n in widths:
        found[name] = (at, n)
        at += n
    return found, at


def build(nc, dram, nb, w_widths, p_widths, r_widths, c_widths):
    w_off, w_total = offsets(w_widths)
    p_off, p_total = offsets(p_widths)
    r_off, r_total = offsets(r_widths)
    c_off, c_total = offsets(c_widths)
    memory_phase(nc, dram, nb, w_off, w_total, r_off, r_total, c_off)
    decoder_phase(nc, dram, nb, w_off, w_total, p_off, p_total, r_off, r_total, c_off, c_total)


def lay_out(inputs):
    w = {name: np.asarray(a) for name, a in inputs.items()}
    nb = w["x"].shape[0]
    mats, rows, consts = weight_layouts(w), row_layouts(w), constants()
    prepared = {name: mats.pop(name) for name in PREPARED}

    def padded(a):
        a = np.asarray(a)
        return np.pad(a, ((0, P - a.shape[0]), (0, 0)))

    arrays = {
        "weights": np.concatenate([padded(a) for a in mats.values()], axis=1),
        "prepared": np.concatenate([padded(a) for a in prepared.values()], axis=1),
        "rows": np.concatenate(list(rows.values())).reshape(1, -1),
        "consts": np.concatenate(list(consts.values()), axis=1).astype(np.float32),
        "x": w["x"],
        "xT": w["x"].transpose(2, 0, 1).reshape(P, nb * T),
        "ctx": w["ctx_1024"],
        "ctxT": w["ctx_1024"].transpose(2, 0, 1).reshape(P, nb * S2),
        "key_mask": w["mask_BxS2_ik0"],
        "x2_mask": w["mask_1x1xSxS2_ik0"][0, 0],
    }
    arrays.update(expert_layouts(w))
    arrays = {name: np.ascontiguousarray(a) for name, a in arrays.items()}
    widths = [[(name, a.shape[-1]) for name, a in group.items()] for group in (mats, prepared, rows, consts)]
    return arrays, widths, nb


def kernel(**inputs):
    import concourse.bacc as bacc
    from concourse.bass_utils import run_bass_kernel_spmd

    arrays, widths, nb = lay_out(inputs)
    nc = bacc.Bacc("TRN2", target_bir_lowering=False, num_devices=1)
    dram = {name: nc.dram_tensor(name + "_in", a.shape, mybir.dt.from_np(a.dtype), kind="ExternalInput").ap()
            for name, a in arrays.items()}
    dram["out"] = nc.dram_tensor("out", (nb, T, D), F32, kind="ExternalOutput").ap()
    dram.update(scratch_tensors(nc, nb))
    build(nc, dram, nb, *widths)
    result = run_bass_kernel_spmd(nc, [{name + "_in": a for name, a in arrays.items()}], core_ids=[0])
    return result.results[0]["out"]


def scratch_tensors(nc, nb):
    shapes = {"g": (nb, BLK, BLK), "xx": (nb, BLK, 2 * BLK), "z": (P, nb * T), "s": (P, nb)}
    return {name: nc.dram_tensor(name + "_scratch", shape, F32, kind="Internal").ap() for name, shape in shapes.items()}
```

```python
from contextlib import ExitStack

import numpy as np

import concourse.bass as bass
from concourse import mybir

F32 = mybir.dt.float32
I32 = mybir.dt.int32
ALU = mybir.AluOpType
ACT = mybir.ActivationFunctionType
AX = mybir.AxisListType.X

P = 128
T = 128
D = 128
S2 = 77
HEADS = 16
HD = D // HEADS
HQ = 4
QUADS = HEADS // HQ
VW = 32
EXPERTS = 8
HALF = EXPERTS // 2
DFF = 512
HC = DFF // P
CAP = 2 * T // EXPERTS
LAT = 32
KV = 2
I_FF = 352
FP4_BLOCK = 16
E6, LT = 6, 100
LANES = 4
THREADS = 4
BLK = 32
NBLK = T // BLK
EPS = 1e-5
KEY_EPS = 1e-6
MASKED = -1e30


def constants():
    p = np.arange(P)
    f = np.arange(T)
    inv = 1.0 / 10000.0 ** (np.arange(0, HD, 2, dtype=np.float32) / np.float32(HD))
    ang = np.outer(f.astype(np.float32), inv.astype(np.float32)).astype(np.float32)
    half = HD // 2
    cos = np.cos(ang)[:, p % half].T
    sin = np.sin(ang)[:, p % half].T * np.where(p % HD < half, -1.0, 1.0)[:, None]
    return {
        "ident": np.eye(P),
        "quad_mask": (p[:, None] % 32 // HD == np.arange(HQ)[None, :]) * 1.0,
        "group_mask": (p[:, None] // 32 == np.arange(4)[None, :]) * 1.0,
        "upto": (p[:, None] <= f[None, :]) * 1.0,
        "causal": np.where(f[None, :] <= p[:, None], 0.0, MASKED),
        "slots": np.broadcast_to(np.arange(1, CAP + 1), (P, CAP)),
        "falling": np.broadcast_to(np.arange(E6, 0, -1), (P, E6)),
        "ones": np.ones((P, 32)),
        "rope": np.concatenate([cos, sin], axis=1),
    }


def rows_first(a):
    n = a.shape[0] // P
    return a.reshape(n, P, a.shape[1]).transpose(1, 0, 2).reshape(P, -1)


def column(a):
    return a.reshape(-1, 1)


def rope_order(second):
    first = [0, 2, 4, 6, 1, 3, 5, 7]
    order = first[4:] + first[:4] if second else first
    return [h * HD + r for h in range(HEADS) for r in order]


def weight_layouts(w):
    out = {}
    a = "L0_attn_"
    out["rec_qkT"] = np.concatenate([w[a + "Wq"].T, w[a + "Wk"].T], axis=1)
    out["rec_v"] = w[a + "Wv"].T
    out["rec_o"] = w[a + "Wo"].T
    out["rec_bq"] = column(w[a + "bq"])
    a = "L0_xattn_"
    out["x0_q"], out["x0_k"], out["x0_o"] = w[a + "Wq"].T, w[a + "Wk"].T, w[a + "Wc"].T
    out["x0_bq"], out["x0_bk"] = column(w[a + "bq"]), column(w[a + "bk"])
    out["f0_gate"] = w["L0_ffn_gate_w"]
    a = "L1_attn_"
    out["a1_qT"] = rows_first(w[a + "wq"].T)
    out["a1_kdown"], out["a1_vdown"] = w[a + "wk_down"], w[a + "wv_down"]
    out["a1_kupT"], out["a1_vupT"] = w[a + "wk_up"].T, w[a + "wv_up"].T
    out["a1_o"] = rows_first(w[a + "wo"])
    a = "L1_xattn_"
    out["x1_q"], out["x1_k"], out["x1_v"] = w[a + "q_w"].T, w[a + "k_w"].T, w[a + "v_w"].T
    out["x1_bq"], out["x1_bk"] = column(w[a + "q_b"]), column(w[a + "k_b"])
    a = "L1_ffn_"
    out["f1_gate"] = np.concatenate([w[a + "w_gate"][0:128], w[a + "w_gate"][128:256]], axis=1)
    out["f1_up"] = np.concatenate([w[a + "w_up"][0:128], w[a + "w_up"][128:256]], axis=1)
    out["f1_gate_rest"], out["f1_up_rest"] = w[a + "w_gate"][256:352], w[a + "w_up"][256:352]
    out["f1_down"] = w[a + "w_down"]
    a = "L2_attn_"
    out["a2_q"], out["a2_k"] = w[a + "Wq"], w[a + "Wk"]
    out["a2_bq"], out["a2_bk"] = column(w[a + "bq"]), column(w[a + "bk"])
    a = "L2_xattn_"
    out["x2_q"], out["x2_k"] = w[a + "Wq"], w[a + "Wk"]
    out["x2_v"], out["x2_o"] = w[a + "Wv"], w[a + "Wo"]
    out["x2_bq"], out["x2_bk"] = column(w[a + "bq"]), column(w[a + "bk"])
    a = "L2_ffn_"
    out["f2_A"] = w[a + "A"].transpose(2, 0, 1).reshape(16, E6 * LT)
    out["f2_B"] = w[a + "B"].transpose(1, 0, 2).reshape(16, E6 * D)
    out["f2_gate"], out["f2_wtT"], out["f2_wdT"] = w[a + "w_gate"], w[a + "wt_w"].T, w[a + "wd_w"].T
    out["f2_bt"] = column(w[a + "wt_b"])
    a = "L3_attn_"
    q, k, v = w[a + "w_qkv"][0:128], w[a + "w_qkv"][128:256], w[a + "w_qkv"][256:384]
    out["a3_qk"] = np.concatenate([q[rope_order(0)].T, q[rope_order(1)].T,
                                   k[rope_order(0)].T, k[rope_order(1)].T], axis=1)
    out["a3_v"], out["a3_o"] = v.T, w[a + "w_out"].T
    a = "L3_xattn_"
    for n in "qkv":
        out["x3_" + n] = w[a + "kernel_" + n][0, 0]
    out["x3_bq"], out["x3_bk"] = column(w[a + "bias_q"]), column(w[a + "bias_k"])
    out["x3_maskT"] = w["mask_1xSxS2_ff0"][0].T
    a = "L3_ffn_"
    out["f3_conv"] = w[a + "conv_w"].transpose(1, 2, 0).reshape(P, 3 * D)
    qkv = w[a + "wqkv"]
    out["f3_q"], out["f3_k"], out["f3_v"] = qkv[0:128].T, qkv[128:256].T, qkv[256:384].T
    out["f3_bq"], out["f3_bk"] = column(w[a + "bqkv"][0:128]), column(w[a + "bqkv"][128:256])
    out["f3_o"], out["f3_gate"] = w[a + "wo"].T, w[a + "gate_w"]
    out["f3_b1"] = w[a + "b1"].reshape(EXPERTS, HC, P).transpose(2, 0, 1).reshape(P, -1)
    out["f3_b2"] = w[a + "b2"]
    return out


def expert_layouts(w):
    out = {}
    for layer in ("L0", "L3"):
        w1, w2 = w[layer + "_ffn_w1"], w[layer + "_ffn_w2"]
        out[layer + "_w1"] = w1.transpose(1, 0, 2).reshape(P, EXPERTS * DFF)
        out[layer + "_w2"] = w2.reshape(EXPERTS, HC, P, D).transpose(2, 0, 1, 3).reshape(P, EXPERTS * DFF)
    return out


def row_layouts(w):
    out = {
        "rec_bqk": np.concatenate([w["L0_attn_bq"], w["L0_attn_bk"]]),
        "rec_bv": w["L0_attn_bv"], "rec_bo": w["L0_attn_bo"], "x0_bo": w["L0_xattn_bc"],
        "x1_bv": w["L1_xattn_v_b"], "a2_bv": w["L2_attn_bk"],
        "x2_bv": w["L2_xattn_bv"], "x2_bo": w["L2_xattn_bo"],
        "f2_bd": w["L2_ffn_wd_b"], "f2_scale": w["L2_ffn_scale"], "a3_bo": w["L3_attn_b_out"],
        "x3_bv": w["L3_xattn_bias_v"], "f3_bconv": w["L3_ffn_conv_b"],
        "f3_bv": w["L3_ffn_bqkv"][256:384], "f3_bo": w["L3_ffn_bo"],
        "f3_g1": w["L3_ffn_ln1_g"], "f3_n1": w["L3_ffn_ln1_b"], "f3_bgate": w["L3_ffn_gate_b"],
        "f3_g2": w["L3_ffn_ln2_g"], "f3_n2": w["L3_ffn_ln2_b"],
    }
    return out


PREPARED = ("a1_qT", "a1_kdown", "a1_kupT", "a1_vupT", "a1_o", "f1_gate", "f1_up", "f1_gate_rest",
            "f1_up_rest", "f1_down", "f2_A", "f2_B", "f2_wtT", "f2_wdT", "f2_bt")
"""Matrices that only the preparation reads, before the loop."""


class Signal:

    def __init__(self, sem):
        self.sem, self.count = sem, 0


class Steps:

    def __init__(self, thread, engine, done):
        self.thread, self.engine, self.done, self.noted = thread, engine, done, []

    def __call__(self, waits, work):
        self.done.count += 1
        emit, size = work
        fixed, each = RATES[self.engine]
        ns = fixed + each * size
        mark = (self.done, self.done.count)
        self.noted.append((waits, emit, mark, 1, ns))
        return mark


def interleave(threads, queues):
    rest = [steps for t in threads for steps in (t.pe, t.act, t.dve, t.pool, t.dma)]
    open_marks = {mark for steps in rest for _, _, mark, _, _ in steps.noted}
    left = {}
    for steps in rest:
        left[steps.thread] = left.get(steps.thread, 0) + sum(one[4] for one in steps.noted)
    for i, t in enumerate(left):
        left[t] -= LAG_NS * i
    free, ends = {e: 0 for e in ENGINES}, {}
    while open_marks:
        best = None
        for steps in rest:
            if steps.noted and not any(mark in open_marks for mark in steps.noted[0][0]):
                start = max([free[steps.engine]] + [ends[mark] for mark in steps.noted[0][0]])
                key = (start, -left[steps.thread])
                if best is None or key < best[0]:
                    best = key, steps, start
        _, steps, start = best
        waits, emit, mark, by, ns = steps.noted.pop(0)
        free[steps.engine] = start + ns
        left[steps.thread] -= ns
        ends[mark] = start + ns + (HOP_NS if by == 1 else DMA_NS)
        open_marks.remove(mark)
        queues[steps.engine].append((waits, emit, mark[0], by))


def transfer(steps, signal, waits, emit):
    signal.count += 16
    mark = (signal, signal.count)
    steps.noted.append((waits, emit, mark, 16, 50))
    return mark


def play(queue, eng, turn=None):
    for waits, emit, signal, by in queue:
        for s, count in waits:
            eng.wait_ge(s.sem, count)
        (emit(eng, turn) if by == 16 else emit(eng)).then_inc(signal.sem, by)


ENGINES = ("tensor", "scalar", "vector", "gpsimd", "sync")


def new_signal(nc, ctx, name, signals):
    signals.append(Signal(ctx.enter_context(nc.semaphore(name))))
    return signals[-1]


class Thread:
    pass


def new_thread(nc, ctx, name, signals):
    parts = {short: Steps(name, e, new_signal(nc, ctx, f"{name}_{e}_done", signals))
             for short, e in (("pe", "tensor"), ("act", "scalar"), ("dve", "vector"), ("pool", "gpsimd"))}
    thread = Thread()
    thread.dma = Steps(name, "sync", None)
    thread.pe, thread.act, thread.dve, thread.pool = parts["pe"], parts["act"], parts["dve"], parts["pool"]
    return thread


HOP_NS = 235
TRANSPOSE_NS = 117
DMA_NS = 2500
LAG_NS = 4000


RATES = {"tensor": (0, 1.0), "scalar": (110, 0.75), "vector": (65, 1.05), "gpsimd": (100, 2.3)}
"""Nanoseconds of an instruction, and of each of its `size`."""


def row(out):
    return int(np.prod(list(out.shape)[1:]))


def matmul_ns(out):
    columns = int(np.prod(list(out.shape)[1:]))
    return max(64, 1.8 * columns) * (0.3 if out.shape[0] == 32 else 1)


def products(*each):
    def emit(e):
        for out, lhsT, rhs, first, last in each:
            ins = e.matmul(out, lhsT, rhs, start=first, stop=last)
        return ins
    return emit, sum(matmul_ns(one[0]) for one in each)


def product(out, lhsT, rhs):
    return products((out, lhsT, rhs, True, True))


def transposes(ident, *each):
    def emit(e):
        for out, in_ in each:
            ins = e.transpose(out, in_, ident[0:in_.shape[0], 0:in_.shape[0]])
        return ins
    return emit, TRANSPOSE_NS * len(each)


def over(ap, axis, n):
    ap = ap.unsqueeze(axis)
    shape = list(ap.shape)
    shape[axis] = n
    return ap.to_broadcast(shape)


def tt(out, a, b, op):
    return lambda e: e.tensor_tensor(out, a, b, op), row(out)


def copy(out, in_):
    return lambda e: e.tensor_copy(out, in_), row(out)


def recip(out, in_):
    return lambda e: e.reciprocal(out, in_), 6 * row(out)


def reduce_to(out, in_, op, magnitude=False):
    return lambda e: e.tensor_reduce(out, in_, AX, op, apply_absolute_value=magnitude), row(in_)


def ts(out, in_, s1, op0, s2=None, op1=ALU.bypass):
    return lambda e: e.tensor_scalar(out, in_, s1, s2, op0, op1), row(out)


def stt(out, a, s, op0, b, op1):
    return lambda e: e.scalar_tensor_tensor(out=out, in0=a, scalar=s, in1=b, op0=op0, op1=op1), row(out)


def fill(out, value):
    return lambda e: e.memset(out, value), row(out)


def move(out, in_):
    return lambda e, i: e.dma_start(out, in_)


def activate(out, in_, func, **more):
    return lambda e: e.activation(out, in_, func, **more), row(out)


def act_copy(out, in_):
    return activate(out, in_, ACT.Copy)


def act_bias(out, in_, bias):
    return activate(out, in_, ACT.Identity, bias=bias)


def memory_phase(nc, dram, nb, w_off, w_total, rows_off, rows_total, c_off):
    nq = nb // 4
    queues, signals = {e: [] for e in ENGINES}, []
    with ExitStack() as ctx:
        def sb(name, shape):
            return ctx.enter_context(nc.sbuf_tensor("m_" + name, shape, F32))

        w = new_thread(nc, ctx, "m", signals)
        threads = [new_thread(nc, ctx, f"m_quads{i}", signals) for i in range(THREADS)]
        bank = [ctx.enter_context(nc.psum_tensor(f"m_bank{i}", [P, 512], F32)) for i in range(8)]
        loaded = new_signal(nc, ctx, "m_weights_loaded", signals)
        x_loaded = [new_signal(nc, ctx, f"m_x_loaded{i}", signals) for i in range(THREADS)]
        moved = new_signal(nc, ctx, "m_moved", signals)
        results = new_signal(nc, ctx, "m_results_stored", signals)
        ident = sb("ident", [P, P])
        qkw = sb("qkw", [P, 2 * D])
        qkb = sb("qkb", [P, 2 * D])
        xT = [sb(f"xT{i}", [P, 4, T]) for i in range(THREADS)]
        qk = [sb(f"qk{i}", [P, 4, 2 * D]) for i in range(THREADS)]
        tmp = [sb(f"tmp{i}", [P, 4, D]) for i in range(THREADS)]
        u = [sb(f"u{i}", [P, 4, D]) for i in range(THREADS)]
        s_all = sb("s_all", [P, nb])
        norm = sb("norm", [P, nb])
        half = sb("half", [P, 4])
        uT = sb("uT", [P, nb, T])
        A = sb("A", [P, nb, D])
        yT = [sb(f"yT{i}", [P, 4, BLK]) for i in range(THREADS)]
        y = sb("y", [P, nq, D])
        g = sb("g", [P, nq, BLK])
        E = sb("E", [nb, BLK, 2 * BLK])
        outer = sb("outer", [nb, BLK, BLK])
        col = sb("col", [nb, BLK])
        rd = sb("rd", [nb, BLK])
        xx = sb("xx", [nb, BLK, 2 * BLK])
        xs = sb("xs", [P, nq, 2, P])
        W = [sb(f"w{i}", [P, D]) for i in range(THREADS)]
        Z = [sb(f"z{i}", [P, 4, D]) for i in range(THREADS)]
        group_mask = sb("group_mask", [P, 4])

        def wslice(name):
            a, n = w_off[name]
            return dram["weights"][:, a:a + n]

        a, n = c_off["ident"]
        ld = transfer(w.dma, loaded, [], move(ident[:, :], dram["consts"][:, a:a + n]))
        ld = transfer(w.dma, loaded, [], move(qkw[:, :], wslice("rec_qkT")))
        a, n = c_off["group_mask"]
        ld = transfer(w.dma, loaded, [], move(group_mask[:, :], dram["consts"][:, a:a + n]))
        xs_zero = w.pool([], fill(xs[:, :, :, :], 0.0))
        ra, rn = rows_off["rec_bqk"]
        ld = transfer(w.dma, loaded, [], move(
            qkb[:, :], dram["rows"][0:1, ra:ra + rn].to_broadcast([P, rn])))
        half_set = w.pool([], fill(half[:, :], 0.5))
        A_set = {}
        for q in range(nq):
            A_set[q] = w.act([ld], act_copy(A[:, 4 * q:4 * q + 4, :], over(ident[:, :], 1, 4)))

        x_read, u_read, turned_read, tmp_read, s_ready = [[[] for _ in threads] for _ in range(5)]
        uT_ready = {}
        for q in range(nq):
            i = q % THREADS
            t = threads[i]
            xl = transfer(t.dma, x_loaded[i], x_read[i], move(
                xT[i][:, :, :], dram["xT"][:, 4 * q * T:4 * (q + 1) * T].rearrange("p (b t) -> p b t", b=4)))
            b0 = bank[2 * i], bank[2 * i + 1]
            projected = t.pe([ld, xl] + turned_read[i], products(*[
                (b0[b // 2][:, (b % 2) * 256:(b % 2) * 256 + 256], xT[i][:, b, :], qkw[:, :], True, True)
                for b in range(4)]))
            x_read[i] = [projected]
            for h in range(2):
                biased = t.dve([projected], tt(qk[i][:, 2 * h:2 * h + 2, :],
                               b0[h][:, :].rearrange("p (b c) -> p b c", b=2), over(qkb[:, :], 1, 2), ALU.add))
            kk, qq = qk[i][:, :, D:2 * D], qk[i][:, :, 0:D]
            r = slice(4 * q, 4 * q + 4)
            m = t.dve([biased] + tmp_read[i], tt(tmp[i][:, :, :], kk, qq, ALU.mult))
            m = t.dve([m], reduce_to(s_all[:, r], tmp[i][:, :, :], ALU.add))
            s_ready[i] = [m]
            m = t.dve([m], tt(tmp[i][:, :, :], kk, kk, ALU.mult))
            m = t.dve([m], reduce_to(norm[:, r], tmp[i][:, :, :], ALU.add))
            tmp_read[i] = [m]
            m = t.pool([m, half_set], tt(norm[:, r], norm[:, r], half[:, :], ALU.pow))
            m = t.dve([m], ts(norm[:, r], norm[:, r], KEY_EPS, ALU.add))
            m = t.dve([m], recip(norm[:, r], norm[:, r]))
            m = t.dve([m] + u_read[i], tt(u[i][:, :, :], kk, over(norm[:, r], 2, D), ALU.mult))
            turned = t.pe([m], transposes(ident, *[
                (b0[0][:, b * T:(b + 1) * T], u[i][:, b, :]) for b in range(4)]))
            u_read[i] = [turned]
            uT_ready[q] = t.act([turned], act_copy(uT[:, r, :], b0[0][:, :].rearrange("p (b t) -> p b t", b=4)))
            turned_read[i] = [uT_ready[q]]

        z_ready = {q: [] for q in range(nq)}
        E_flat = E[:, :, :].rearrange("b r c -> b (r c)")
        step_of = 2 * BLK + 1
        diag = E_flat[:, 0:BLK * 2 * BLK:step_of]
        inv_diag = E_flat[:, BLK:BLK * 2 * BLK:step_of]
        last_moved = []
        y_read, yT_read, w_read, even_read, odd_read, y_set, g_set, z_set = [
            [[] for _ in threads] for _ in range(8)]
        for blk in range(NBLK):
            cols = slice(blk * BLK, (blk + 1) * BLK)
            for q in range(nq):
                i = q % THREADS
                t = threads[i]
                Yb, Tb = bank[2 * i], bank[2 * i + 1]
                m = t.pe([uT_ready[q], A_set[q]] + turned_read[i] + even_read[i] + odd_read[i], products(*[
                    (Yb[32 * j:32 * j + 32, 0:D], uT[:, 4 * q + j, cols], A[:, 4 * q + j, :], True, True)
                    for j in range(4)] + [
                    (Tb[:, 32 * j:32 * j + 32], A[:, 4 * q + j, :], uT[:, 4 * q + j, cols], True, True)
                    for j in range(4)]))
                y_sb = t.act([m] + y_read[i], act_copy(y[:, q, :], Yb[:, 0:D]))
                y_set[i] = [y_sb]
                yT_sb = t.dve([m] + yT_read[i], copy(yT[i][:, :, :], Tb[:, 0:P].rearrange("p (j r) -> p j r", j=4)))
                m = t.pe([yT_sb, y_sb], products(*[
                    (Yb[32 * j:32 * j + 32, D:D + BLK], yT[i][:, j, :], uT[:, 4 * q + j, cols], True, True)
                    for j in range(4)]))
                yT_read[i] = [m]
                g_sb = t.dve([m] + last_moved, copy(g[:, q, :], Yb[:, D:D + BLK]))
                even_read[i] = odd_read[i] = g_set[i] = [g_sb]
            g_done = [mark for marks in g_set for mark in marks]
            m = transfer(w.dma, moved, g_done, move(
                dram["g"].rearrange("(q j) r c -> (j r) q c", j=4), g[:, :, :]))
            cleared = w.dve(last_moved, fill(E[:, :, BLK:2 * BLK], 0.0))
            cleared = w.dve([cleared], fill(inv_diag, 1.0))
            m = transfer(w.dma, moved, [m, cleared], move(E[:, :, 0:BLK], dram["g"]))
            m = w.dve([m], ts(diag, diag, 1.0, ALU.add))
            for j in range(BLK - 1):
                n = BLK - 1 - j
                win = slice(j + 1, j + 1 + BLK)
                m = w.dve([m], recip(rd[:, 0:1], E[:, j, j:j + 1]))
                m = w.dve([m], ts(col[:, 0:n], E[:, j + 1:, j], rd[:, 0:1], ALU.mult))
                m = w.dve([m], tt(outer[:, 0:n, :], over(col[:, 0:n], 2, BLK), over(E[:, j, win], 1, n), ALU.mult))
                m = w.dve([m], tt(E[:, j + 1:, win], E[:, j + 1:, win], outer[:, 0:n, :], ALU.subtract))
            m = w.dve([m], recip(rd[:, :], diag))
            inv_T = E[:, :, BLK:2 * BLK].rearrange("b r k -> b k r")
            w.dve(last_moved, copy(xx[:, :, 0:BLK], inv_T))
            m = w.dve([m], tt(xx[:, :, BLK:2 * BLK], inv_T, over(rd[:, :], 1, BLK), ALU.mult))
            m = transfer(w.dma, moved, [m], move(dram["xx"], xx[:, :, :]))
            for j in range(4):
                for k in range(2):
                    last = transfer(w.dma, moved, [m, xs_zero] + [mark for marks in y_read for mark in marks], move(
                        xs[32 * j:32 * j + 32, :, k, 32 * j:32 * j + 32],
                        dram["xx"].rearrange("(q j) k (a m) -> j a k q m", j=4, a=2)[j, k]))
            m = last
            last_moved = [m]
            for q in range(nq):
                i = q % THREADS
                t = threads[i]
                Wb, Zb = bank[2 * i], bank[2 * i + 1]
                m2 = t.pe([m] + y_set[i] + even_read[i] + odd_read[i], products(
                    (Wb[:, 0:D], xs[:, q, 0, :], y[:, q, :], True, True),
                    (Zb[:, 0:D], xs[:, q, 1, :], y[:, q, :], True, True),
                    (Wb[:, D:D + P], y[:, q, :], xs[:, q, 1, :], True, True)))
                z_ready[q] = t.act([m2], act_copy(uT[:, 4 * q:4 * q + 4, cols],
                                   Wb[:, D:D + P].rearrange("p (j r) -> p j r", j=4)))
                even_read[i] = z_set[i] = [z_ready[q]]
                y_read[i] = [m2]
                if blk < NBLK - 1:
                    w_sb = t.act([m2] + w_read[i], act_copy(W[i][:, :], Wb[:, 0:D]))
                    z_sb = t.dve([m2] + w_read[i], tt(Z[i][:, :, :], over(Zb[:, 0:D], 1, 4),
                                 over(group_mask[:, :], 2, D), ALU.mult))
                    m3 = t.pe([w_sb, z_sb], product(Zb[:, :], W[i][:, :], Z[i][:, :, :]))
                    w_read[i] = [m3]
                    A_set[q] = t.dve([m3], tt(A[:, 4 * q:4 * q + 4, :], A[:, 4 * q:4 * q + 4, :],
                                       Zb[:, :].rearrange("p (j d) -> p j d", j=4), ALU.subtract))
                    even_read[i], odd_read[i] = [w_sb], [A_set[q]]

        transfer(w.dma, results, [mark for marks in s_ready for mark in marks], move(dram["s"], s_all[:, :]))
        transfer(w.dma, results, [mark for marks in z_set for mark in marks], move(
            dram["z"].rearrange("p (b t) -> p b t", b=nb), uT[:, :, :]))

        interleave([w] + threads, queues)
        with nc.Block() as block:
            block.tensor(lambda e: play(queues["tensor"], e))
            block.scalar(lambda e: play(queues["scalar"], e))
            block.vector(lambda e: play(queues["vector"], e))
            block.gpsimd(lambda e: play(queues["gpsimd"], e))

            @block.sync
            def _(e):
                play(queues["sync"], e)
                e.wait_ge(results.sem, results.count)


class Weights:

    def __init__(self, tensor, offsets):
        self.tensor, self.offsets = tensor, offsets

    def __getitem__(self, name):
        a, n = self.offsets[name]
        return self.tensor[:, a:a + n]

    def part(self, name, k, n=D):
        a, _ = self.offsets[name]
        return self.tensor[:, a + k * n:a + (k + 1) * n]


def new_lane(nc, ctx, n, signals, shared):
    ln = new_thread(nc, ctx, f"lane{n}", signals)
    ln.n = n
    ln.w, ln.r, ln.k, ln.s = shared["w"], shared["r"], shared["k"], shared

    def sb(name, *shape):
        return ctx.enter_context(nc.sbuf_tensor(f"lane{n}_{name}", list(shape), F32))

    ln.a = ctx.enter_context(nc.psum_tensor(f"lane{n}_a", [P, 512], F32))
    ln.b = ctx.enter_context(nc.psum_tensor(f"lane{n}_b", [P, 512], F32))
    ln.x = sb("x", P, D)
    ln.xT = shared["xT_all"][:, n, :]
    ln.base = sb("base", P, D)
    ln.ctxT, ln.ctx_in = sb("ctxT", P, S2), sb("ctx", S2, D)
    ln.zT, ln.kq_dot = sb("zT", P, T), shared["kq"][:, n:n + 1]
    ln.key_mask_int = ctx.enter_context(nc.sbuf_tensor(f"lane{n}_mask_int", [P, S2], I32))
    ln.key_mask = sb("mask", P, S2)
    ln.qT = sb("qT", P, T)
    ln.kq = sb("kq", P, HQ, T)
    ln.v = sb("v", P, HEADS, VW)
    ln.sc = sb("sc", P, HQ, T)
    ln.p = sb("p", P, HQ, T)
    ln.oT = sb("oT", P, QUADS, T)
    ln.o = sb("o", P, D)
    ln.wide = sb("wide", P, 600)
    ln.small = sb("small", P, 64)
    ln.mean_var = sb("mean_var", P, 2)
    ln.stats = sb("stats", P, 6)
    ln.gates = sb("gates", P, EXPERTS)
    ln.hid = shared["gated_hid"][:, n, :, :, :]
    part, slots = shared["own_part"][:, n, :], EXPERTS * CAP
    ln.choice = {
        "pick": part[:, 0:slots].rearrange("p (e s) -> p e s", e=EXPERTS),
        "weighted": part[:, slots:2 * slots].rearrange("p (e s) -> p e s", e=EXPERTS),
        "left": part[0:EXPERTS, 512:640], "best": part[0:EXPERTS, 640:648],
        "taken": part[:, 648:656], "place": part[:, 656:664], "probs": part[:, 664:672],
    }
    ln.out_stored = new_signal(nc, ctx, f"lane{n}_out_stored", signals)
    ln.arrived = {name: new_signal(nc, ctx, f"lane{n}_{name}_arrived", signals) for name in ("x", "xT", "ctx", "mask")}
    return ln


def add_bias_to_x(ln, row, ready):
    return ln.pool(ready, tt(ln.base[:, :], ln.x[:, :], ln.r[row], ALU.add))


def normalize(ln, src, dst, ready, gain=None, shift=None):
    m = ln.dve(ready, (lambda e: e.bn_stats(ln.stats[:, :], src), row(src)))
    m = ln.dve([m], (lambda e: e.bn_aggr(ln.mean_var[:, :], ln.stats[:, :]), 6))
    rstd = ln.small[:, 60:61]
    m = ln.dve([m], ts(rstd, ln.mean_var[:, 1:2], EPS, ALU.add))
    m = ln.pool([m], tt(rstd, rstd, ln.s["minus_half"], ALU.pow))
    m = ln.dve([m], ts(dst, src, ln.mean_var[:, 0:1], ALU.subtract, rstd, ALU.mult))
    if gain is not None:
        m = ln.dve([m], tt(dst, dst, ln.r[gain], ALU.mult))
        m = ln.dve([m], tt(dst, dst, ln.r[shift], ALU.add))
    return m


def finish(ln, y, ready, plain=False):
    base = ln.x if plain else ln.base
    m = ln.dve(ready, tt(ln.x[:, :], base[:, :], y, ALU.add))
    m = normalize(ln, ln.x[:, :], ln.x[:, :], [m])
    m = ln.pe([m], transposes(ln.k["ident"], (ln.a[:, 0:T], ln.x[:, :])))
    m = ln.act([m], act_copy(ln.xT, ln.a[:, 0:T]))
    return m


def query_and_keys(ln, wq, bq, wk, bk, keysT, nk, ready):
    m = ln.pe(ready, products((ln.a[:, 0:T], ln.w[wq], ln.xT, True, True),
                                (ln.b[:, 0:nk], ln.w[wk], keysT, True, True)))
    q = ln.act([m], act_bias(ln.qT[:, :], ln.a[:, 0:T], ln.w[bq]))
    k = ln.dve([m], stt(ln.kq[:, :, 0:nk], over(ln.b[:, 0:nk], 1, HQ), ln.w[bk], ALU.add,
                          over(ln.k["quad_mask"], 2, nk), ALU.mult))
    return q, k


def values(ln, wv, bv, srcT, nk, ready):
    m = ln.pe(ready, product(ln.a[0:nk, 0:D], srcT, ln.w[wv]))
    return ln.dve([m], tt(ln.v[0:nk, :, 0:HD], heads(ln.a[0:nk, 0:D]),
                            heads(ln.r[bv][0:nk, :]), ALU.add))


def attention(ln, nk, scale, ready, bias=None):
    a, b = ln.a, ln.b
    a4 = a[:, :].rearrange("p (h k) -> p h k", h=HQ)
    b4 = b[:, :].rearrange("p (h q) -> p h q", h=HQ)
    top = ln.small[:, 0:HQ]
    src, sc = a4[:, :, 0:nk], ln.sc[:, :, 0:nk]

    def scores(quad, ready):
        rows = slice(32 * quad, 32 * quad + 32)
        m = ln.pe(ready, product(src, ln.qT[rows, :], ln.kq[rows, :, 0:nk]))
        if bias is not None:
            m = ln.dve([m], tt(sc, src, over(bias, 1, HQ), ALU.add))
        biased = src if bias is None else sc
        m = ln.dve([m], reduce_to(top, biased, ALU.max))
        return ln.dve([m], tt(sc, biased, over(top, 2, nk), ALU.subtract))

    shifted = scores(0, ready)
    m = shifted
    for quad in range(QUADS):
        turned = ln.pe([shifted, m], transposes(ln.k["ident"], *[
            (b4[0:nk, h, :], ln.sc[:, h, 0:nk]) for h in range(HQ)]))
        m = ln.act([turned], activate(ln.p[0:nk, :, :], b4[0:nk, :, :], ACT.Exp, scale=scale))
        if quad < QUADS - 1:
            shifted = scores(quad + 1, [shifted])
        m = ln.pe([m], products(*[
            (b[32 * h:32 * h + 32, 0:T], ln.v[0:nk, HQ * quad + h, :], ln.p[0:nk, h, :], True, True)
            for h in range(HQ)]))
        m = ln.act([m], act_copy(ln.oT[:, quad, :], b[:, 0:T]))
    m = ln.pe([m], transposes(ln.k["ident"], *[
        (a4[:, quad, :], ln.oT[:, quad, :]) for quad in range(QUADS)]))
    out = a[:, :].rearrange("p (h c) -> p h c", h=HEADS)
    total = ln.small[:, 0:HEADS]
    m = ln.dve([m], recip(total, out[:, :, HD]))
    m = ln.dve([m], tt(heads(ln.o[:, :]), out[:, :, 0:HD], over(total, 2, HD), ALU.mult))
    return m


def project_out(ln, wo, ready):
    m = ln.pe([ready], transposes(ln.k["ident"], (ln.b[:, 0:T], ln.o[:, :])))
    m = ln.act([m], act_copy(ln.oT[:, 0, :], ln.b[:, 0:T]))
    return ln.pe([m], product(ln.a[:, 0:D], ln.oT[:, 0, :], ln.w[wo]))

def recurrent_attention(ln, turned_loaded, x_loaded, s_loaded):
    a, b = ln.a, ln.b
    base = add_bias_to_x(ln, "rec_bo", x_loaded)
    m = ln.pe(turned_loaded, products((a[:, 0:D], ln.xT, ln.w["rec_v"], True, True),
                                   (b[:, 0:T], ln.w.part("rec_qkT", 0), ln.xT, True, True)))
    v = ln.dve([m], tt(ln.o[:, :], a[:, 0:D], ln.r["rec_bv"], ALU.add))
    q = ln.act([m], act_bias(ln.qT[:, :], b[:, 0:T], ln.w["rec_bq"]))
    m = ln.pe([q, v], product(a[:, 0:T], ln.zT[:, :], ln.qT[:, :]))
    m = ln.dve([m, s_loaded], stt(ln.sc[:, 0, :], a[:, 0:T], ln.kq_dot, ALU.mult, ln.k["upto"], ALU.mult))
    m = ln.pe([v, m], product(b[:, 0:T], ln.o[:, :], ln.sc[:, 0, :]))
    m = ln.act([m], act_copy(ln.oT[:, 0, :], b[:, 0:T]))
    m = ln.pe([m], product(a[:, 0:D], ln.oT[:, 0, :], ln.w["rec_o"]))
    return finish(ln, a[:, 0:D], [m, base])


def context_attention(ln, ready, name, scale, bias=None, out=True, raw_values=False):
    if out:
        base = add_bias_to_x(ln, name + "_bo", ready)
    if raw_values:
        v = ln.pool(ready, copy(ln.v[0:S2, :, 0:HD], heads(ln.ctx_in[:, :])))
    else:
        v = values(ln, name + "_v", name + "_bv", ln.ctxT[:, :], S2, ready)
    q, k = query_and_keys(ln, name + "_q", name + "_bq", name + "_k", name + "_bk", ln.ctxT[:, :], S2, ready + [v])
    o = attention(ln, S2, scale, [q, k, v], bias)
    if out:
        y = project_out(ln, name + "_o", o)
        return finish(ln, ln.a[:, 0:D], [y, base])
    return finish(ln, ln.o[:, :], [o], plain=True)


def route(ln, ready):
    a, b, c, ident = ln.a, ln.b, ln.choice, ln.k["ident"]
    m = ln.pe(ready, product(a[:, 0:EXPERTS], ln.xT, ln.w["f0_gate"]))
    m = gate_softmax(ln, m, c["probs"])
    m = ln.pe([m], transposes(ident, (a[0:EXPERTS, 0:T], c["probs"])))
    left, best, taken, place = c["left"], c["best"], c["taken"], c["place"]
    m = ln.act([m], act_copy(left, a[0:EXPERTS, 0:T]))
    for _ in range(CAP // 8):
        m = ln.dve([m], (lambda e: e.max(best, left), row(left)))
        m = ln.dve([m], (lambda e: e.match_replace(left, best, left, -1.0), row(left)))
    m = ln.dve([m], ts(left, left, 0.0, ALU.is_lt))
    m = ln.pe([m], transposes(ident, (a[:, 0:EXPERTS], left)))
    m = ln.act([m], act_copy(taken, a[:, 0:EXPERTS]))
    m = ln.pe([m], product(a[:, 0:EXPERTS], ln.k["upto"], taken))
    m = ln.dve([m], tt(place, a[:, 0:EXPERTS], taken, ALU.mult))
    pick, weighted = c["pick"], c["weighted"]
    m = ln.dve([m], tt(pick, over(place, 2, CAP), over(ln.k["slots"], 1, EXPERTS), ALU.is_equal))
    weighed = ln.pool([m], tt(weighted, pick, over(c["probs"], 2, CAP), ALU.mult))
    taken_x = a[:, 0:EXPERTS * CAP].rearrange("p (e s) -> p e s", e=EXPERTS)
    m = ln.pe([m], product(taken_x, ln.x[:, :], pick))
    ln.act([m], act_copy(ln.s["xin"][:, :, ln.n, :], taken_x))
    m = ln.pe([weighed], transposes(ident, *[
        (b[:, half * T:(half + 1) * T],
         weighted[:, half * HALF:(half + 1) * HALF, :].rearrange("p e s -> p (e s)")) for half in range(2)]))
    ln.act([m], act_copy(ln.s["back"][:, ln.n, :, :], b[:, 0:2 * T].rearrange("p (h t) -> p h t", h=2)))


def gate_softmax(ln, m, out):
    logits = ln.small[:, 0:EXPERTS]
    top, total = ln.small[:, 16:17], ln.small[:, 17:18]
    m = ln.dve([m], reduce_to(top, ln.a[:, 0:EXPERTS], ALU.max))
    m = ln.dve([m], ts(logits, ln.a[:, 0:EXPERTS], top, ALU.subtract))
    m = ln.act([m], activate(logits, logits, ACT.Exp))
    m = ln.dve([m], reduce_to(total, logits, ALU.add))
    m = ln.dve([m], recip(total, total))
    return ln.dve([m], ts(out, logits, total, ALU.mult))


def latent_attention(ln, ready):
    a, b = ln.a, ln.b
    a4 = a[:, :].rearrange("p (h k) -> p h k", h=HQ)
    b4 = b[:, :].rearrange("p (h q) -> p h q", h=HQ)
    top = ln.small[:, 0:HQ]
    for kv in range(KV):
        start = ready if kv == 0 else [o]
        m = ln.pe(start, products((a[:, 0:T], ln.s["a1_q"][:, kv, :], ln.xT, True, True),
                                    (b[:, 0:T], ln.s["a1_k"][:, kv, :], ln.xT, True, True)))
        q = ln.act([m], act_copy(ln.qT[:, :], a[:, 0:T]))
        k = ln.dve([m], tt(ln.kq[:, :, :], over(b[:, 0:T], 1, HQ), over(ln.k["group_mask"], 2, T), ALU.mult))
        if kv == 0:
            m = ln.pe([k], product(b[:, 0:KV * LAT], ln.xT, ln.w["a1_vdown"]))
            v = ln.act([m], act_copy(ln.wide[:, 0:KV * LAT], b[:, 0:KV * LAT]))
        m = ln.pe([q, k], product(a[:, :], ln.qT[:, :], ln.kq[:, :, :]))
        m = ln.dve([m], tt(ln.sc[:, :, :], a4, over(ln.k["causal"], 1, HQ), ALU.add))
        m = ln.dve([m], reduce_to(top, ln.sc[:, :, :], ALU.max))
        m = ln.dve([m], tt(ln.sc[:, :, :], ln.sc[:, :, :], over(top, 2, T), ALU.subtract))
        m = ln.pe([m, v], transposes(ln.k["ident"], *[
            (b4[:, h, :], ln.sc[:, h, :]) for h in range(HQ)]))
        m = ln.act([m], activate(ln.p[:, :, :], b4, ACT.Exp, scale=float(P) ** -0.5))
        m = ln.pe([m, v], products(*[
            (b[32 * h:32 * h + 32, 0:T], ln.wide[:, kv * LAT:(kv + 1) * LAT], ln.p[:, h, :], True, True)
            for h in range(HQ)] + [
            (b[32 * h:32 * h + 32, T:2 * T], ln.k["ones"], ln.p[:, h, :], True, True)
            for h in range(HQ)]))
        m = ln.dve([m], recip(ln.sc[:, 0, :], b[:, T:2 * T]))
        o = ln.dve([m], tt(ln.oT[:, kv, :], b[:, 0:T], ln.sc[:, 0, :], ALU.mult))
    m = ln.pe([o], products(*[(a[:, 0:D], ln.oT[:, kv, :], ln.s["a1_vo"][:, kv, :], kv == 0, kv == KV - 1)
                                for kv in range(KV)]))
    return finish(ln, a[:, 0:D], [m], plain=True)


def fp4_feed_forward(ln, ready):
    a, b = ln.a, ln.b
    x_rounded = ln.o
    m = fp4_round(ln, ln.x[:, :], x_rounded[:, :], D // FP4_BLOCK, ready, fp4_buffers(ln))
    m = ln.pe([m], transposes(ln.k["ident"], (a[:, 0:T], x_rounded[:, :])))
    m = ln.act([m], act_copy(ln.qT[:, :], a[:, 0:T]))
    m = ln.pe([m], products((a[:, 0:I_FF], ln.qT[:, :], ln.s["f1_gateT"][:, :], True, True),
                              (b[:, 0:I_FF], ln.qT[:, :], ln.s["f1_upT"][:, :], True, True)))
    h = ln.wide[:, 0:I_FF]
    m = ln.act([m], activate(h, a[:, 0:I_FF], ACT.Silu))
    m = ln.dve([m], tt(h, h, b[:, 0:I_FF], ALU.mult))
    m = fp4_round(ln, h, h, I_FF // FP4_BLOCK, [m], fp4_buffers(ln))
    chunks = [(c, min(P, I_FF - c * P)) for c in range(3)]
    m = ln.pe([m], transposes(ln.k["ident"], *[
        (a[0:n, c * T:(c + 1) * T], ln.wide[:, c * P:c * P + n]) for c, n in chunks]))
    m = ln.act([m], act_copy(ln.p[:, 0:2, :], a[:, 0:2 * T].rearrange("p (c t) -> p c t", c=2)))
    n = chunks[2][1]
    m = ln.act([m], act_copy(ln.p[0:n, 2, :], a[0:n, 2 * T:3 * T]))
    m = ln.pe([m], products(*[(b[:, 0:D], ln.p[0:n, c, :], ln.s["f1_downT"][0:n, c, :], c == 0, c == 2)
                                for c, n in chunks]))
    return finish(ln, b[:, 0:D], [m], plain=True)


def self_attention_shared_values(ln, ready):
    v = values(ln, "a2_k", "a2_bv", ln.xT, T, ready)
    q, k = query_and_keys(ln, "a2_q", "a2_bq", "a2_k", "a2_bk", ln.xT, T, ready + [v])
    o = attention(ln, T, float(D) ** -0.5, [q, k, v])
    return finish(ln, ln.o[:, :], [o], plain=True)


def low_rank_feed_forward(ln, ready):
    a, b = ln.a, ln.b
    half = E6 // 2 * LT
    tokT = ln.s["f2_tokT"]
    m = ln.pe(ready, products(
        (a[:, 0:half], ln.xT, tokT[:, 0:half], True, True),
        (a[:, half:half + E6], ln.xT, ln.w["f2_gate"], True, True),
        (b[:, 0:half], ln.xT, tokT[:, half:2 * half], True, True)))
    g, top, tie = ln.small[:, 0:E6], ln.small[:, 16:17], ln.small[:, 8:8 + E6]
    g_m = ln.dve([m], reduce_to(top, a[:, half:half + E6], ALU.max))
    g_m = ln.dve([g_m], ts(tie, a[:, half:half + E6], top, ALU.is_equal))
    g_m = ln.dve([g_m], tt(tie, tie, ln.k["falling"], ALU.mult))
    g_m = ln.dve([g_m], reduce_to(top, tie, ALU.max))
    g_m = ln.dve([g_m], tt(g, tie, top.to_broadcast([P, E6]), ALU.is_equal))
    wide = ln.wide[:, :].rearrange("p (e l) -> p e l", e=E6)
    m = ln.dve([g_m], tt(wide[:, 0:3, :], a[:, 0:half].rearrange("p (e l) -> p e l", e=3),
                           over(ln.small[:, 0:3], 2, LT), ALU.mult))
    m = ln.dve([g_m], tt(wide[:, 3:6, :], b[:, 0:half].rearrange("p (e l) -> p e l", e=3),
                           over(ln.small[:, 3:6], 2, LT), ALU.mult))
    own = ln.sc[:, 0, 0:LT]
    m = ln.dve([m], reduce_to(own, ln.wide[:, :].rearrange("p (e l) -> p l e", e=E6), ALU.add))
    m = ln.dve([m], reduce_to(top, own, ALU.max))
    m = ln.dve([m], ts(top, top, -float(D) ** -0.5, ALU.mult))
    total = ln.small[:, 17:18]
    m = ln.act([m], activate(own, own, ACT.Exp, bias=top, scale=float(D) ** -0.5, accum_out=total))
    m = ln.dve([m], recip(total, total))
    m = ln.dve([m], ts(own, own, total, ALU.mult))
    m = ln.pe([m], transposes(ln.k["ident"], (a[0:LT, 0:T], own)))
    m = ln.act([m], act_copy(ln.p[0:LT, 0, :], a[0:LT, 0:T]))
    val = ln.s["f2_val"]
    m = ln.pe([m], products(
        (a[:, 0:3 * D], ln.p[0:LT, 0, :], val[0:LT, 0:3 * D], True, True),
        (a[:, 3 * D:4 * D], ln.xT, ln.s["f2_wd"][:, :], True, True),
        (b[:, 0:3 * D], ln.p[0:LT, 0, :], val[0:LT, 3 * D:6 * D], True, True)))
    acc = ln.o[:, :]
    m = ln.dve([m], tt(acc, a[:, 3 * D:4 * D], ln.s["f2_bd"], ALU.add))
    for e in range(E6):
        bank = a if e < 3 else b
        m = ln.dve([m], stt(acc, bank[:, e % 3 * D:(e % 3 + 1) * D], ln.small[:, e:e + 1], ALU.mult,
                              acc, ALU.add))
    m = ln.act([m], activate(acc, acc, ACT.Exp))
    zero = ln.sc[:, 0, :]
    m = ln.dve([m], ts(zero, acc, 0.0, ALU.is_equal, float(np.finfo(np.float32).eps), ALU.mult))
    m = ln.dve([m], tt(acc, acc, zero, ALU.add))
    m = ln.act([m], activate(acc, acc, ACT.Ln))
    m = ln.dve([m], tt(acc, acc, ln.x[:, :], ALU.add))
    return finish(ln, acc, [m], plain=True)


def rotary_attention(ln, ready):
    a, b = ln.a, ln.b
    base = add_bias_to_x(ln, "a3_bo", ready)
    m = ln.pe(ready, product(b[:, 0:D], ln.xT, ln.w["a3_v"]))
    v = ln.act([m], act_copy(ln.v[:, :, 0:HD], heads(b[:, 0:D])))
    m = ln.pe(ready, products(*[(a[:, i * T:(i + 1) * T], ln.w.part("a3_qk", i), ln.xT, True, True)
                                  for i in range(4)]))
    rot = ln.sc[:, :, :].rearrange("p (n f) t -> p n f t", n=2)
    m = ln.dve([m], tt(rot, a[:, :].rearrange("p (n f t) -> p n f t", n=2, f=2),
                         over(ln.k["rope"].rearrange("p (f t) -> p f t", f=2), 1, 2), ALU.mult))
    q = ln.dve([m], tt(ln.qT[:, :], ln.sc[:, 0, :], ln.sc[:, 1, :], ALU.add))
    k = ln.dve([m], tt(ln.o[:, :], ln.sc[:, 2, :], ln.sc[:, 3, :], ALU.add))
    k = ln.dve([k], tt(ln.kq[:, :, :], over(ln.o[:, :], 1, HQ), over(ln.k["quad_mask"], 2, T), ALU.mult))
    o = attention(ln, T, float(HD) ** -0.5, [q, k, v])
    y = project_out(ln, "a3_o", o)
    return finish(ln, a[:, 0:D], [y, base])


def relu_attention(ln, ready):
    a, b = ln.a, ln.b
    m = ln.pe(ready, products((a[:, 0:T], ln.w["x3_q"], ln.xT, True, True),
                                (b[:, 0:S2], ln.w["x3_k"], ln.ctxT[:, :], True, True)))
    q = ln.act([m], activate(ln.qT[:, :], a[:, 0:T], ACT.Relu, bias=ln.w["x3_bq"]))
    kT = ln.kq[:, 0, 0:S2]
    k = ln.dve([m], ts(kT, b[:, 0:S2], ln.w["x3_bk"], ALU.add, 0.0, ALU.max))
    m = ln.pe([q], product(a[0:S2, 0:D], ln.ctxT[:, :], ln.w["x3_v"]))
    vals = ln.wide[0:S2, 0:D]
    v = ln.dve([m], tt(vals, a[0:S2, 0:D], ln.r["x3_bv"][0:S2, :], ALU.add))
    v = ln.dve([v], ts(vals, vals, 0.0, ALU.max))
    m = ctx_read = ln.pe([q, k], product(b[0:S2, 0:T], kT, ln.qT[:, :]))
    lg = ln.p[0:S2, 0, :]
    m = ln.dve([m], ts(lg, b[0:S2, 0:T], 0.0, ALU.max, float(D) ** -0.5, ALU.mult))
    m = ln.dve([m], tt(lg, lg, ln.w["x3_maskT"][0:S2, :], ALU.add))
    m = ln.pe([m, v], product(b[:, 0:D], lg, vals))
    m = ln.act([m], activate(ln.o[:, :], b[:, 0:D], ACT.Relu))
    return finish(ln, ln.o[:, :], [m], plain=True), ctx_read


def conv_and_attention(ln, ready):
    a, b = ln.a, ln.b
    ends = ln.pool(ready, fill(ln.wide[:, 0:T + 2:T + 1], 0.0))
    m = ln.pool(ready, copy(ln.wide[:, 1:T + 1], ln.xT))
    conv = ln.pe([m, ends], products(*[
        (a[:, 0:D], ln.wide[:, i:i + T], ln.w.part("f3_conv", i), i == 0, i == 2) for i in range(3)]))
    conv_out = ln.oT[:, 3, :]
    m = ln.dve([conv], tt(conv_out, a[:, 0:D], ln.r["f3_bconv"], ALU.add))
    base = ln.pool([m], tt(ln.base[:, :], conv_out, ln.r["f3_bo"], ALU.add))
    m = ln.pe([m], transposes(ln.k["ident"], (b[:, 0:T], conv_out)))
    y_ready = ln.act([m], act_copy(ln.xT, b[:, 0:T]))
    v = values(ln, "f3_v", "f3_bv", ln.xT, T, [y_ready])
    q, k = query_and_keys(ln, "f3_q", "f3_bq", "f3_k", "f3_bk", ln.xT, T, [y_ready, v])
    o = attention(ln, T, float(HD) ** -0.5, [q, k, v, base])
    y = project_out(ln, "f3_o", o)
    m = ln.dve([y, base], tt(ln.o[:, :], ln.base[:, :], a[:, 0:D], ALU.add))
    mid = ln.base
    m = normalize(ln, ln.o[:, :], mid[:, :], [m], "f3_g1", "f3_n1")
    m = ln.pe([m], transposes(ln.k["ident"], (a[:, 0:T], mid[:, :])))
    midT = ln.act([m], act_copy(ln.xT, a[:, 0:T]))
    m = ln.pe([midT], product(a[:, 0:EXPERTS], ln.xT, ln.w["f3_gate"]))
    logits = ln.small[:, 0:EXPERTS]
    top, total = ln.small[:, 16:17], ln.small[:, 17:18]
    m = ln.dve([m], tt(logits, a[:, 0:EXPERTS], ln.r["f3_bgate"], ALU.add))
    m = ln.dve([m], reduce_to(top, logits, ALU.max))
    m = ln.dve([m], ts(logits, logits, top, ALU.subtract))
    m = ln.act([m], activate(logits, logits, ACT.Exp))
    m = ln.dve([m], reduce_to(total, logits, ALU.add))
    m = ln.dve([m], recip(total, total))
    m = ln.dve([m], ts(ln.gates[:, :], logits, total, ALU.mult))
    m = ln.pe([m], transposes(ln.k["ident"], (a[0:EXPERTS, 0:T], ln.gates[:, :])))
    m = a_read = ln.act([m], act_copy(ln.o[0:EXPERTS, :], a[0:EXPERTS, 0:T]))
    m = ln.pe([m], product(b[:, 0:D], ln.o[0:EXPERTS, :], ln.w["f3_b2"][0:EXPERTS, :]))
    m = ln.dve([m], tt(mid[:, :], mid[:, :], b[:, 0:D], ALU.add))
    return [midT, a_read], m


def end_of_layer(ln, mixed):
    m = normalize(ln, ln.base[:, :], ln.o[:, :], [mixed], "f3_g2", "f3_n2")
    m = ln.dve([m], tt(ln.x[:, :], ln.x[:, :], ln.o[:, :], ALU.add))
    return normalize(ln, ln.x[:, :], ln.base[:, :], [m])


def heads(ap):
    return ap.rearrange("p (h c) -> p h c", h=HEADS)


def blocks(ap, n):
    return ap.rearrange("p (b c) -> p b c", b=n)


def fp4_buffers(lane):
    flat = [t[:, :, :].rearrange("p h t -> p (h t)") for t in (lane.sc, lane.p, lane.oT)]
    return flat + [lane.kq[:, :, :].rearrange("p h t -> p (h t)"), lane.small]


def fp4_round(w, src, dst, n, ready, buffers, rows=P):
    mag, sign, level, high, small = buffers
    size = n * FP4_BLOCK
    mag, sign, level, high = [t[0:rows, 0:size] for t in (mag, sign, level, high)]
    scale, inv = small[0:rows, 0:n], small[0:rows, 32:32 + n]
    m = w.dve(ready, reduce_to(scale, blocks(src, n), ALU.max, magnitude=True))
    m = w.dve([m], ts(scale, scale, 1.0 / 6.0, ALU.mult, 1e-12, ALU.max))
    m2 = w.dve([m], recip(inv, scale))
    m2 = w.dve([m2], tt(blocks(mag, n), blocks(src, n), over(inv, 2, FP4_BLOCK), ALU.mult))
    s = w.act([m2], activate(sign, mag, ACT.Sign))
    s = w.pool([s, m], tt(blocks(sign, n), blocks(sign, n), over(scale, 2, FP4_BLOCK), ALU.mult))
    m2 = w.act([m2], activate(mag, mag, ACT.Abs))
    high_m = w.pool([m2], ts(high, mag, 5.0, ALU.is_gt, 4.0, ALU.mult))
    m = w.dve([m2], ts(level, mag, 3.5, ALU.is_gt))
    m = w.dve([m], stt(level, mag, 2.5, ALU.is_gt, level, ALU.add))
    m = w.dve([m, high_m], stt(level, level, 2.0, ALU.mult, high, ALU.add))
    for mid in (1.75, 1.25, 0.75, 0.25):
        m = w.dve([m], stt(level, mag, mid, ALU.is_gt, level, ALU.add))
    return w.dve([m, s], stt(dst, level, 0.5, ALU.mult, sign, ALU.mult))


def routed_mixture(w, lanes, s, banks):
    xin, back, hid, y = s["xin"], s["back"], s["hid"], s["moe_y"]
    w1, w2 = s["L0_w1"], s["L0_w2"]
    bank_read, gelu = [[], [], [], []], []
    for e in range(EXPERTS):
        bank = banks[e % 4]
        m = w.pe(bank_read[e % 4], products(*[
            (bank[:, c * P:(c + 1) * P], w1[:, e, c * P:(c + 1) * P], xin[:, e, :, :], True, True)
            for c in range(HC)]))
        gelu.append(w.act([m], activate(hid[:, e, :], bank[:, :], ACT.Gelu)))
        bank_read[e % 4] = [gelu[e]]
    y_set = []
    for half in range(2):
        out = banks[4 + half]
        m = w.pe(gelu[half * HALF:(half + 1) * HALF], products(*[
            (out[CAP * i:CAP * (i + 1), n * D:(n + 1) * D],
             hid[:, half * HALF + i, c * P + CAP * n:c * P + CAP * (n + 1)],
             w2[:, half * HALF + i, c, :], c == 0, c == HC - 1)
            for n in range(LANES) for c in range(HC) for i in range(HALF)]))
        y_set.append(w.dve([m], copy(y[:, half, :, :], out[:, :].rearrange("p (n d) -> p n d", n=LANES))))
    return [ln.pe(y_set + bank_read[ln.n], products(*[
        (ln.a[:, 0:D], back[:, ln.n, half, :], y[:, half, ln.n, :], half == 0, half == 1)
        for half in range(2)])) for ln in lanes]


def gated_mixture(ln, ready, acc, scratch_free):
    a, b, w1, w2 = ln.a, ln.b, ln.s["L3_w1"], ln.s["L3_w2"]
    a4 = a[:, :].rearrange("p (c t) -> p c t", c=HC)

    def hidden(e, ready):
        return ln.pe(ready, products(*[
            (a4[:, c, :], w1[:, e, c * P:(c + 1) * P], ln.xT, True, True) for c in range(HC)]))

    m = hidden(0, ready)
    read = [scratch_free, scratch_free]
    for e in range(EXPERTS):
        hid = ln.hid[:, e % 2, :, :]
        m = ln.dve([m] + read[e % 2], tt(hid, a4, over(ln.w.part("f3_b1", e, HC), 2, T), ALU.add))
        relu = ln.act([m], activate(hid, hid, ACT.Relu))
        if e < EXPERTS - 1:
            m = xT_read = hidden(e + 1, [m])
        out = ln.pe([relu, acc], products(*[
            (b[:, 0:D], hid[:, c, :], w2[:, e, c, :], c == 0, c == HC - 1) for c in range(HC)]))
        read[e % 2] = [out]
        acc = ln.dve([out, acc], stt(ln.base[:, :], b[:, 0:D], ln.gates[:, e:e + 1], ALU.mult,
                                     ln.base[:, :], ALU.add))
    return acc, xT_read


def prepare(w, s, wt, ready, banks, temp):
    k = s["k"]
    w.dve(ready, fill(temp["small"][:, :], 0.0))
    w.act(ready, act_copy(temp["first"][:, :], k["ident"]))
    w.pe(ready, transposes(k["ident"], (banks[7][:, 0:P], k["ident"])))
    m = w.pe([], products(*[
        (banks[0][:, h * LAT:(h + 1) * LAT], wt.part("a1_qT", h), wt["a1_kupT"], True, True) for h in range(8)]))
    w.dve([m], copy(s["a1_q"][:, :, :], banks[0][:, 0:8 * LAT].rearrange("p (n c) -> p n c", n=KV)))
    vo = []
    for kv in range(KV):
        w.dve([], copy(s["a1_k"][:, kv, :].rearrange("p (h c) -> p h c", h=HQ),
                       over(wt["a1_kdown"][:, kv * LAT:(kv + 1) * LAT], 1, HQ)))
        m = w.pe(vo, products(*[
            (banks[1][32 * h:32 * h + 32, 0:D], wt["a1_vupT"], wt.part("a1_o", kv * HQ + h), True, True)
            for h in range(HQ)]))
        vo = [w.dve([m], copy(s["a1_vo"][:, kv, :], banks[1][:, 0:D]))]
    scale = s["r"]["f2_scale"]
    wd = w.dve([], ts(s["f2_wd"][:, :], wt["f2_wdT"], scale, ALU.mult))
    w.dve([], ts(s["f2_bd"], s["r"]["f2_bd"], scale, ALU.mult))
    valT = temp["valT"]
    for e in range(E6):
        m = w.pe([], product(banks[2][:, 0:LT], wt["f2_B"][0:16, e * D:(e + 1) * D],
                             wt["f2_A"][0:16, e * LT:(e + 1) * LT]))
        tokT = s["f2_tokT"][:, e * LT:(e + 1) * LT]
        m = w.dve([m], copy(tokT, banks[2][:, 0:LT]))
        m = w.pe([m], product(banks[3][:, 0:LT], wt["f2_wtT"], tokT))
        m = w.act([m], act_bias(valT[:, 0:LT], banks[3][:, 0:LT], wt["f2_bt"]))
        m = w.pe([m, wd], product(banks[4][0:LT, 0:D], valT[:, 0:LT], s["f2_wd"][:, :]))
        val = w.dve([m], copy(s["f2_val"][0:LT, e * D:(e + 1) * D], banks[4][0:LT, 0:D]))
    w.dve([val], fill(s["f2_val"][0:1, :], 0.0))
    w.dve([], ts(s["x2_mask"][:, :], s["x2_mask_int"][:, :], 0.0, ALU.is_equal, MASKED, ALU.mult))
    buffers = (temp["mag"], temp["sign"], temp["level"], temp["high"], temp["small"])
    m = None
    for name in ("gate", "up"):
        tiles = [(wt.part("f1_" + name, 0), P, 0), (wt.part("f1_" + name, 1), P, P),
                 (wt[f"f1_{name}_rest"][0:96, :], 96, 2 * P)]
        for tile, rows, at in tiles:
            m = fp4_round(w, tile, tile, D // FP4_BLOCK, [m] if m else [], buffers, rows)
            t = w.pe([m], transposes(k["ident"], (banks[5][:, 0:rows], tile)))
            w.act([t], act_copy(s[f"f1_{name}T"][:, at:at + rows], banks[5][:, 0:rows]))
    m = fp4_round(w, wt["f1_down"], wt["f1_down"], I_FF // FP4_BLOCK, [m], buffers)
    bank_read = []
    for c in range(3):
        n = min(P, I_FF - c * P)
        t = w.pe([m] + bank_read, transposes(k["ident"], (banks[6][0:n, 0:D], wt["f1_down"][:, c * P:c * P + n])))
        bank_read = [w.act([t], act_copy(s["f1_downT"][0:n, c, :], banks[6][0:n, 0:D]))]


def decoder_phase(nc, dram, nb, w_off, w_total, p_off, p_total, rows_off, rows_total, c_off, c_total):
    with ExitStack() as ctx:
        def sb(name, *shape, dt=F32):
            return ctx.enter_context(nc.sbuf_tensor(name, list(shape), dt))

        signals = []
        experts_loaded = Signal(ctx.enter_context(nc.semaphore("experts_loaded")))
        weights, rows, consts = sb("weights_sb", P, w_total), sb("rows_sb", P, rows_total), sb("consts_sb", P, c_total)
        s = {
            "w": Weights(weights, w_off), "r": Weights(rows, rows_off), "k": Weights(consts, c_off),
            "xT_all": sb("xT_all", P, LANES, T),
            "a1_q": sb("a1_q", P, KV, P), "a1_k": sb("a1_k", P, KV, P), "a1_vo": sb("a1_vo", P, KV, D),
            "f1_gateT": sb("f1_gateT", P, I_FF), "f1_upT": sb("f1_upT", P, I_FF), "f1_downT": sb("f1_downT", P, 3, D),
            "f2_tokT": sb("f2_tokT", P, E6 * LT), "f2_val": sb("f2_val", P, E6 * D), "f2_wd": sb("f2_wd", P, D),
            "x2_mask": sb("x2_mask", P, S2), "x2_mask_int": sb("x2_mask_int", P, S2, dt=I32),
            "kq": sb("kq_dots", P, LANES),
        }
        s["f2_bd"] = sb("f2_bd_scaled", P, D)[:, :]
        s["minus_half"] = sb("minus_half", P, 1)[:, :]
        for layer in ("L0", "L3"):
            s[layer + "_w1"] = sb(layer + "_w1", P, EXPERTS, DFF)
            s[layer + "_w2"] = sb(layer + "_w2", P, EXPERTS, HC, D)
        scratch = sb("mixture_scratch", P, 6144)
        own_part = scratch[:, 0:4096].rearrange("p (n f) -> p n f", n=LANES)
        s["own_part"] = own_part
        s["gated_hid"] = own_part.rearrange("p n (i c t) -> p n i c t", i=2, c=HC)
        s["moe_y"] = scratch[:, 4096:5120].rearrange("p (h n d) -> p h n d", h=2, n=LANES)
        s["hid"] = scratch[:, 0:4096].rearrange("p (e f) -> p e f", e=EXPERTS)
        s["xin"] = scratch[:, 4096:5120].rearrange("p (e n s) -> p e n s", e=EXPERTS, n=LANES)
        s["back"] = scratch[:, 5120:6144].rearrange("p (n h t) -> p n h t", n=LANES, h=2)
        with ExitStack() as own:
            def setup_sb(name, *shape):
                return own.enter_context(nc.sbuf_tensor("setup_" + name, list(shape), F32))

            setup, once = {e: [] for e in ENGINES}, []
            w = new_thread(nc, own, "setup", once)
            banks = [own.enter_context(nc.psum_tensor(f"setup_bank{i}", [P, 512], F32)) for i in range(8)]
            raw = setup_sb("weights", P, p_total)
            temp = {"small": setup_sb("small", P, 64), "first": setup_sb("first", P, P), "valT": setup_sb("valT", P, LT)}
            temp.update({n: setup_sb(n, P, I_FF) for n in ("mag", "sign", "level", "high")})
            loaded = new_signal(nc, own, "weights_loaded", once)
            for out, in_ in [(weights[:, :], dram["weights"]), (consts[:, :], dram["consts"]),
                             (raw[:, :], dram["prepared"]),
                             (rows[:, :], dram["rows"].to_broadcast([P, rows_total])),
                             (s["x2_mask_int"][:, :], dram["x2_mask"])]:
                m = transfer(w.dma, loaded, [], move(out, in_))
            for layer in ("L0", "L3"):
                for out, name in ((s[layer + "_w1"][:, :, :].rearrange("p e f -> p (e f)"), "_w1"),
                                  (s[layer + "_w2"][:, :, :, :].rearrange("p e c d -> p (e c d)"), "_w2")):
                    experts = transfer(w.dma, experts_loaded, [], move(out, dram[layer + name]))
            w.pool([], fill(s["minus_half"], -0.5))
            prepare(w, s, Weights(raw, p_off), [m], banks, temp)
            interleave([w], setup)
            with nc.Block() as block:
                block.sync(lambda e: play(setup["sync"], e))
                block.tensor(lambda e: play(setup["tensor"], e))
                block.scalar(lambda e: play(setup["scalar"], e))
                block.vector(lambda e: play(setup["vector"], e))
                block.gpsimd(lambda e: play(setup["gpsimd"], e))

        lanes = [new_lane(nc, ctx, n, signals, s) for n in range(LANES)]
        banks = [ln.a for ln in lanes] + [ln.b for ln in lanes]
        both = new_thread(nc, ctx, "lanes", signals)
        s_signal = new_signal(nc, ctx, "s_arrived", signals)

        def load_s(ahead):
            return transfer(both.dma, s_signal, [], lambda e, turn: e.dma_start(
                s["kq"][:, :], dram["s"][:, bass.ds(turn * LANES + ahead * LANES, LANES)]))

        def load(ln, signal, ahead, waits, out, src):
            return transfer(ln.dma, ln.arrived[signal], waits, lambda e, turn: e.dma_start(
                out, src(turn * LANES + (ahead * LANES + ln.n))))

        def load_first(ln, ahead):
            load(ln, "xT", ahead, [], ln.zT[:, :], lambda b: dram["z"][:, bass.ds(b * T, T)])
            return load(ln, "x", ahead, [], ln.ctx_in[:, :],
                        lambda b: dram["ctx"][bass.ds(b, 1)].rearrange("a t d -> (a t) d"))

        def load_context(ln, ahead, waits):
            return load(ln, "ctx", ahead, waits, ln.ctxT[:, :], lambda b: dram["ctxT"][:, bass.ds(b * S2, S2)])

        def load_mask(ln, ahead, waits):
            return load(ln, "mask", ahead, waits, ln.key_mask_int[:, :],
                        lambda b: dram["key_mask"][bass.ds(b, 1), :].to_broadcast([P, S2]))

        def load_x(ln, ahead, x_read, xT_read):
            x = load(ln, "x", ahead, x_read, ln.x[:, :], lambda b: dram["x"][bass.ds(b, 1)].rearrange("a t d -> (a t) d"))
            return load(ln, "xT", ahead, xT_read, ln.xT, lambda b: dram["xT"][:, bass.ds(b * T, T)]), x

        def first_part(ln, turned_arrived, x_arrived, s_arrived):
            m = recurrent_attention(ln, turned_arrived, x_arrived, s_arrived)
            m = context_attention(ln, [m], "x0", float(HD) ** -0.5, raw_values=True)
            route(ln, [m])

        def second_part(ln, mixed):
            mask = ln.pool([], ts(ln.key_mask[:, :], ln.key_mask_int[:, :], 0.0, ALU.is_gt, MASKED, ALU.mult))
            m = finish(ln, ln.a[:, 0:D], [mixed[ln.n]], plain=True)
            m = latent_attention(ln, [m])
            m = context_attention(ln, [m, mask], "x1", float(HD) ** -0.5, bias=ln.key_mask[:, :], out=False)
            m = fp4_feed_forward(ln, [m])
            m = self_attention_shared_values(ln, [m])
            m = context_attention(ln, [m], "x2", float(HD) ** -0.5, bias=s["x2_mask"][:, :])
            m = low_rank_feed_forward(ln, [m])
            m = rotary_attention(ln, [m])
            m, ctx_read = relu_attention(ln, [m])
            ready, acc = conv_and_attention(ln, [m])
            m, xT_read = gated_mixture(ln, ready, acc, mixed)
            ended = end_of_layer(ln, m)
            stored = transfer(ln.dma, ln.out_stored, [ended], lambda e, turn: e.dma_start(
                dram["out"][bass.ds(turn * LANES + ln.n, 1)].rearrange("a t d -> (a t) d"), ln.base[:, :]))
            return mask, ctx_read, ended, xT_read, stored

        def close():
            queues = {e: [] for e in ENGINES}
            interleave(lanes + [both], queues)
            counts = [(sig, sig.count) for sig in signals if sig.count]
            ends = {e: [] for e in ENGINES}
            for thread in lanes + [both]:
                for steps in (thread.pe, thread.act, thread.dve, thread.pool):
                    if steps.done.count:
                        ends[steps.engine].append((steps.done, steps.done.count))
            engines_own = [sig for e in ENGINES for sig, _ in ends[e]]
            ends["sync"] = [one for one in counts if one[0] not in engines_own]
            for sig in signals:
                sig.count = 0
            return queues, ends, [sig for sig, _ in counts]

        s_arrived = load_s(0)
        for ln in lanes:
            load_first(ln, 0)
            load_mask(ln, 0, [])
            xT, x = load_x(ln, 0, [], [])
            first_part(ln, [xT, load_context(ln, 0, [])], [x], s_arrived)
        opening = close()

        s_arrived = load_s(1)
        for ln in lanes:
            load_first(ln, 1)
        mixed = routed_mixture(both, lanes, s, banks)
        for ln in lanes:
            mask, ctx_read, x_read, xT_read, stored = second_part(ln, mixed)
            load_mask(ln, 1, [mask])
            context = load_context(ln, 1, [ctx_read])
            xT, x = load_x(ln, 1, [x_read], [xT_read])
            first_part(ln, [xT, context], [x, stored], s_arrived)
        body = close()

        mixed = routed_mixture(both, lanes, s, banks)
        for ln in lanes:
            second_part(ln, mixed)
        closing = close()

        met = ctx.enter_context(nc.semaphore("engines_met"))
        go = {e: ctx.enter_context(nc.semaphore(f"{e}_goes_on")) for e in ENGINES[:4]}
        ones_set = ctx.enter_context(nc.semaphore("value_columns_set"))
        turns = nb // LANES

        def step(name, eng, phase, turn):
            queues, ends, counted = phase
            play(queues[name], eng, turn)
            for sig, count in ends[name]:
                eng.wait_ge(sig.sem, count)
            if name == "sync":
                eng.wait_ge(met, 4)
                eng.sem_clear(met)
                for sig in counted:
                    eng.sem_clear(sig.sem)
                for other in ENGINES[:4]:
                    eng.sem_inc(go[other], 1)
            else:
                eng.sem_inc(met, 1)
                eng.wait_ge(go[name], 1)
                eng.sem_clear(go[name])

        def run(name, eng):
            if name == "gpsimd":
                for n, ln in enumerate(lanes):
                    eng.memset(ln.v[:, :, :], 0.0).then_inc(ones_set, 1)
                    eng.wait_ge(ones_set, 2 * n + 1)
                    eng.memset(ln.v[:, :, HD:HD + 1], 1.0).then_inc(ones_set, 1)
            elif name != "sync":
                eng.wait_ge(ones_set, 2 * LANES)
            if name == "tensor":
                eng.wait_ge(experts_loaded.sem, experts_loaded.count)
            step(name, eng, opening, 0)
            if turns > 1:
                with eng.Fori(0, turns - 1) as turn:
                    step(name, eng, body, turn)
            step(name, eng, closing, turns - 1)

        with nc.Block() as block:
            block.sync(lambda e: run("sync", e))
            block.tensor(lambda e: run("tensor", e))
            block.scalar(lambda e: run("scalar", e))
            block.vector(lambda e: run("vector", e))
            block.gpsimd(lambda e: run("gpsimd", e))


def offsets(widths):
    found, at = {}, 0
    for name, n in widths:
        found[name] = (at, n)
        at += n
    return found, at


def build(nc, dram, nb, w_widths, p_widths, r_widths, c_widths):
    w_off, w_total = offsets(w_widths)
    p_off, p_total = offsets(p_widths)
    r_off, r_total = offsets(r_widths)
    c_off, c_total = offsets(c_widths)
    memory_phase(nc, dram, nb, w_off, w_total, r_off, r_total, c_off)
    decoder_phase(nc, dram, nb, w_off, w_total, p_off, p_total, r_off, r_total, c_off, c_total)


def lay_out(inputs):
    w = {name: np.asarray(a) for name, a in inputs.items()}
    nb = w["x"].shape[0]
    mats, rows, consts = weight_layouts(w), row_layouts(w), constants()
    prepared = {name: mats.pop(name) for name in PREPARED}

    def padded(a):
        a = np.asarray(a)
        return np.pad(a, ((0, P - a.shape[0]), (0, 0)))

    arrays = {
        "weights": np.concatenate([padded(a) for a in mats.values()], axis=1),
        "prepared": np.concatenate([padded(a) for a in prepared.values()], axis=1),
        "rows": np.concatenate(list(rows.values())).reshape(1, -1),
        "consts": np.concatenate(list(consts.values()), axis=1).astype(np.float32),
        "x": w["x"],
        "xT": w["x"].transpose(2, 0, 1).reshape(P, nb * T),
        "ctx": w["ctx_1024"],
        "ctxT": w["ctx_1024"].transpose(2, 0, 1).reshape(P, nb * S2),
        "key_mask": w["mask_BxS2_ik0"],
        "x2_mask": w["mask_1x1xSxS2_ik0"][0, 0],
    }
    arrays.update(expert_layouts(w))
    arrays = {name: np.ascontiguousarray(a) for name, a in arrays.items()}
    widths = [[(name, a.shape[-1]) for name, a in group.items()] for group in (mats, prepared, rows, consts)]
    return arrays, widths, nb


def kernel(**inputs):
    import concourse.bacc as bacc
    from concourse.bass_utils import run_bass_kernel_spmd

    arrays, widths, nb = lay_out(inputs)
    nc = bacc.Bacc("TRN2", target_bir_lowering=False, num_devices=1)
    dram = {name: nc.dram_tensor(name + "_in", a.shape, mybir.dt.from_np(a.dtype), kind="ExternalInput").ap()
            for name, a in arrays.items()}
    dram["out"] = nc.dram_tensor("out", (nb, T, D), F32, kind="ExternalOutput").ap()
    dram.update(scratch_tensors(nc, nb))
    build(nc, dram, nb, *widths)
    result = run_bass_kernel_spmd(nc, [{name + "_in": a for name, a in arrays.items()}], core_ids=[0])
    return result.results[0]["out"]


def scratch_tensors(nc, nb):
    shapes = {"g": (nb, BLK, BLK), "xx": (nb, BLK, 2 * BLK), "z": (P, nb * T), "s": (P, nb)}
    return {name: nc.dram_tensor(name + "_scratch", shape, F32, kind="Internal").ap() for name, shape in shapes.items()}
```
